# Optimizing a Trainium2 kernel written in Bass

```python
import numpy as np
import jax
import jax.numpy as jnp

def _softmax(x, axis=-1):
    return jax.nn.softmax(x, axis=axis)

def _gelu(x):
    return jax.nn.gelu(x, approximate=True)

def _silu(x):
    return jax.nn.silu(x)

def _sigmoid(x):
    return jax.nn.sigmoid(x)

def _layernorm(x, axis=-1, eps=1e-05):
    m = jnp.mean(x, axis=axis, keepdims=True)
    v = jnp.var(x, axis=axis, keepdims=True)
    return (x - m) / jnp.sqrt(v + eps)

def _scatter_add(tgt, idx, src, axis=0):
    return tgt.at[idx].add(src)

def _segment_sum(src, seg, n):
    return jax.ops.segment_sum(src, seg, n)
kernel_name = 'mk_decoder_preln_d1_seqx_r8_1be48a'

def setup_inputs(seed: int=0):
    np.random.seed(seed)
    _w = jnp.asarray

    def _rec_inputs():
        import jax
        import jax.numpy as jnp
        _rk = jax.random.key(seed)
        x = -0.0003929 + 0.9999 * jax.random.normal(jax.random.fold_in(_rk, 1), (64, 128, 128), jnp.float32)
        _lenS = 128 - jax.random.randint(jax.random.fold_in(_rk, 7), (64,), 0, max(1, 128 // 4) + 1, jnp.int32)
        _lenS2 = 77 - jax.random.randint(jax.random.fold_in(_rk, 8), (64,), 0, max(1, 77 // 4) + 1, jnp.int32)
        _ctx_1024P = jax.random.normal(jax.random.fold_in(_rk, 11), (64, 16, 128), jnp.float32)
        _ctx_1024c = jax.random.dirichlet(jax.random.fold_in(_rk, 511), 0.3 * jnp.ones((16,), jnp.float32), (64, 77))
        _ctx_1024t = jnp.einsum('bsk,bkd->bsd', _ctx_1024c, _ctx_1024P)
        _ctx_1024t = _ctx_1024t * jax.lax.rsqrt(jnp.mean(jnp.square(_ctx_1024t)) + 1e-12) * 0.953939
        ctx_1024 = 2.81802e-05 + 1.00001 * (_ctx_1024t + 0.3 * jax.random.normal(jax.random.fold_in(_rk, 611), (64, 77, 128), jnp.float32))
        return (x, ctx_1024)
    x, ctx_1024 = _rec_inputs()

    def _L0_attn_setup():
        import jax, jax.numpy as jnp
        import numpy as np
        GAMMA = 0.99

        def _get_D(gamma, T, dtype=jnp.float32):
            n = jnp.arange(T)
            diff = n[:, None] - n[None, :]
            return jnp.where(diff >= 0, jnp.power(jnp.asarray(gamma, dtype), jnp.maximum(diff, 0).astype(dtype)), jnp.zeros((), dtype))

        def _reference_tuple_inner(X, att_mask, S_n, W_Q, W_K, W_V):
            B, T, _ = X.shape
            C = W_Q.shape[1]
            Q = X @ W_Q
            K = X @ W_K
            V = X @ W_V
            A = jnp.einsum('btc,bsc->bts', Q, K)
            A = A * _get_D(GAMMA, T, X.dtype)[None, :, :]
            out = A @ V
            out = jnp.swapaxes(out, -2, -1).reshape(B, T, C)
            return (out, S_n)
        key = jax.random.key(seed)
        kX, kQ, kK, kV = jax.random.split(key, 4)
        B, T, I, C = (2, 512, 128, 128)
        X = jax.random.normal(kX, (B, T, I), dtype=jnp.float32)
        att_mask = jnp.ones((B, T), dtype=jnp.float32)
        S_n = jnp.zeros((B, C, C), dtype=jnp.float32)
        W_Q = jax.random.normal(kQ, (I, C), dtype=jnp.float32) / I
        W_K = jax.random.normal(kK, (I, C), dtype=jnp.float32) / I
        W_V = jax.random.normal(kV, (I, I), dtype=jnp.float32) / I
        return {'X': X, 'att_mask': att_mask, 'S_n': S_n, 'W_Q': W_Q, 'W_K': W_K, 'W_V': W_V}
    _L0_attn_all = _L0_attn_setup()
    _L0_attn_in = {k: v for k, v in _L0_attn_all.items() if k in ('att_mask', 'S_n', 'W_Q', 'W_K', 'W_V')}
    del _L0_attn_all

    def _L0_xattn_setup():
        import jax, jax.numpy as jnp
        import numpy as np
        B, S, E = (8, 256, 128)
        EPS = 0.001

        def _layer_norm(x, gamma, beta):
            mu = jnp.mean(x, axis=-1, keepdims=True)
            var = jnp.mean(jnp.square(x - mu), axis=-1, keepdims=True)
            return gamma * (x - mu) * jax.lax.rsqrt(var + EPS) + beta

        def _attention(q_in, k_in, v_in, WQ, WK, WV, causal):
            Q = jnp.einsum('bse,ed->bsd', q_in, WQ)
            K = jnp.einsum('bse,ed->bsd', k_in, WK)
            V = jnp.einsum('bse,ed->bsd', v_in, WV)
            d = K.shape[-1]
            scores = jnp.einsum('bqd,bkd->bqk', Q, K) / jnp.sqrt(jnp.float32(d))
            if causal:
                qlen, klen = (scores.shape[-2], scores.shape[-1])
                mask = jnp.triu(jnp.ones((qlen, klen), bool), k=1)
                scores = jnp.where(mask[None], -jnp.inf, scores)
            p = jax.nn.softmax(scores, axis=-1)
            return jnp.einsum('bqk,bkd->bqd', p, V)
        key = jax.random.key(seed)
        ks = jax.random.split(key, 10)
        sc = 1.0 / np.sqrt(E)
        return {'inputs': jax.random.normal(ks[0], (B, S, E), jnp.float32), 'context': jax.random.normal(ks[1], (B, S, E), jnp.float32), 'Wq': jax.random.normal(ks[2], (E, E), jnp.float32) * sc, 'Wk': jax.random.normal(ks[3], (E, E), jnp.float32) * sc, 'Wv': jax.random.normal(ks[4], (E, E), jnp.float32) * sc, 'Wcq': jax.random.normal(ks[5], (E, E), jnp.float32) * sc, 'Wck': jax.random.normal(ks[6], (E, E), jnp.float32) * sc, 'Wcv': jax.random.normal(ks[7], (E, E), jnp.float32) * sc, 'gamma': jnp.ones((E,), jnp.float32), 'beta': jnp.zeros((E,), jnp.float32), 'W1': jax.random.normal(ks[8], (E, E), jnp.float32) * sc, 'b1': jnp.zeros((E,), jnp.float32)}
    _L0_xattn_all = _L0_xattn_setup()
    _L0_xattn_in = {k: v for k, v in _L0_xattn_all.items() if k in ('Wq', 'Wk', 'Wv', 'Wcq', 'Wck', 'Wcv', 'gamma', 'beta', 'W1', 'b1')}
    del _L0_xattn_all

    def _L0_ffn_setup():
        import jax, jax.numpy as jnp
        import numpy as np
        B, S = (4, 256)
        D_MODEL, D_FF, N_EXPERTS, TOP_K = (128, 512, 8, 2)
        T = B * S
        CAPACITY_FACTOR, MIN_CAP = (1.25, 4)
        CAP = max(int(CAPACITY_FACTOR * (T * TOP_K / N_EXPERTS)), MIN_CAP)
        key = jax.random.key(seed)
        ks = jax.random.split(key, 6)

        def w(k, shape, fan):
            return jax.random.normal(k, shape, jnp.float32) * fan ** (-0.5)
        return {'x': jax.random.normal(ks[0], (B, S, D_MODEL), jnp.float32), 'Wr': w(ks[1], (D_MODEL, N_EXPERTS), D_MODEL), 'W1': w(ks[2], (N_EXPERTS, D_MODEL, D_FF), D_MODEL), 'b1': jnp.zeros((N_EXPERTS, D_FF), jnp.float32), 'W2': w(ks[3], (N_EXPERTS, D_FF, D_MODEL), D_FF), 'b2': jnp.zeros((N_EXPERTS, D_MODEL), jnp.float32), 'fw1': w(ks[4], (D_MODEL, D_FF), D_MODEL), 'fb1': jnp.zeros((D_FF,), jnp.float32), 'fw2': w(ks[5], (D_FF, D_MODEL), D_FF), 'fb2': jnp.zeros((D_MODEL,), jnp.float32)}
    _L0_ffn_all = _L0_ffn_setup()
    _L0_ffn_in = {k: v for k, v in _L0_ffn_all.items() if k in ('Wr', 'W1', 'b1', 'W2', 'b2', 'fw1', 'fb1', 'fw2', 'fb2')}
    del _L0_ffn_all
    return {'x': x, 'ctx_1024': ctx_1024, 'L0_attn_att_mask': _L0_attn_in['att_mask'], 'L0_attn_S_n': _L0_attn_in['S_n'], 'L0_attn_W_Q': _L0_attn_in['W_Q'], 'L0_attn_W_K': _L0_attn_in['W_K'], 'L0_attn_W_V': _L0_attn_in['W_V'], 'L0_xattn_Wq': _L0_xattn_in['Wq'], 'L0_xattn_Wk': _L0_xattn_in['Wk'], 'L0_xattn_Wv': _L0_xattn_in['Wv'], 'L0_xattn_Wcq': _L0_xattn_in['Wcq'], 'L0_xattn_Wck': _L0_xattn_in['Wck'], 'L0_xattn_Wcv': _L0_xattn_in['Wcv'], 'L0_xattn_gamma': _L0_xattn_in['gamma'], 'L0_xattn_beta': _L0_xattn_in['beta'], 'L0_xattn_W1': _L0_xattn_in['W1'], 'L0_xattn_b1': _L0_xattn_in['b1'], 'L0_ffn_Wr': _L0_ffn_in['Wr'], 'L0_ffn_W1': _L0_ffn_in['W1'], 'L0_ffn_b1': _L0_ffn_in['b1'], 'L0_ffn_W2': _L0_ffn_in['W2'], 'L0_ffn_b2': _L0_ffn_in['b2'], 'L0_ffn_fw1': _L0_ffn_in['fw1'], 'L0_ffn_fb1': _L0_ffn_in['fb1'], 'L0_ffn_fw2': _L0_ffn_in['fw2'], 'L0_ffn_fb2': _L0_ffn_in['fb2']}

def reference(x, ctx_1024, L0_attn_att_mask, L0_attn_S_n, L0_attn_W_Q, L0_attn_W_K, L0_attn_W_V, L0_xattn_Wq, L0_xattn_Wk, L0_xattn_Wv, L0_xattn_Wcq, L0_xattn_Wck, L0_xattn_Wcv, L0_xattn_gamma, L0_xattn_beta, L0_xattn_W1, L0_xattn_b1, L0_ffn_Wr, L0_ffn_W1, L0_ffn_b1, L0_ffn_W2, L0_ffn_b2, L0_ffn_fw1, L0_ffn_fb1, L0_ffn_fw2, L0_ffn_fb2):
    import jax
    import jax.numpy as jnp

    def _L0_attn_ref(X, att_mask, S_n, W_Q, W_K, W_V):
        import jax, jax.numpy as jnp
        import numpy as np
        GAMMA = 0.99

        def _get_D(gamma, T, dtype=jnp.float32):
            n = jnp.arange(T)
            diff = n[:, None] - n[None, :]
            return jnp.where(diff >= 0, jnp.power(jnp.asarray(gamma, dtype), jnp.maximum(diff, 0).astype(dtype)), jnp.zeros((), dtype))

        def _reference_tuple_inner(X, att_mask, S_n, W_Q, W_K, W_V):
            B, T, _ = X.shape
            C = W_Q.shape[1]
            Q = X @ W_Q
            K = X @ W_K
            V = X @ W_V
            A = jnp.einsum('btc,bsc->bts', Q, K)
            A = A * _get_D(GAMMA, T, X.dtype)[None, :, :]
            out = A @ V
            out = jnp.swapaxes(out, -2, -1).reshape(B, T, C)
            return (out, S_n)
        return _reference_tuple_inner(X, att_mask, S_n, W_Q, W_K, W_V)[0]

    def _L0_xattn_ref(inputs, context, Wq, Wk, Wv, Wcq, Wck, Wcv, gamma, beta, W1, b1):
        import jax, jax.numpy as jnp
        import numpy as np
        B, S, E = (8, 256, 128)
        EPS = 0.001

        def _layer_norm(x, gamma, beta):
            mu = jnp.mean(x, axis=-1, keepdims=True)
            var = jnp.mean(jnp.square(x - mu), axis=-1, keepdims=True)
            return gamma * (x - mu) * jax.lax.rsqrt(var + EPS) + beta

        def _attention(q_in, k_in, v_in, WQ, WK, WV, causal):
            Q = jnp.einsum('bse,ed->bsd', q_in, WQ)
            K = jnp.einsum('bse,ed->bsd', k_in, WK)
            V = jnp.einsum('bse,ed->bsd', v_in, WV)
            d = K.shape[-1]
            scores = jnp.einsum('bqd,bkd->bqk', Q, K) / jnp.sqrt(jnp.float32(d))
            if causal:
                qlen, klen = (scores.shape[-2], scores.shape[-1])
                mask = jnp.triu(jnp.ones((qlen, klen), bool), k=1)
                scores = jnp.where(mask[None], -jnp.inf, scores)
            p = jax.nn.softmax(scores, axis=-1)
            return jnp.einsum('bqk,bkd->bqd', p, V)
        a = _attention(inputs, inputs, inputs, Wq, Wk, Wv, causal=True) + inputs
        h = _layer_norm(a, gamma, beta)
        c = _attention(h, context, context, Wcq, Wck, Wcv, causal=False) + h
        h = _layer_norm(c, gamma, beta)
        f = jax.nn.relu(jnp.einsum('bse,ed->bsd', h, W1) + b1)
        out = _layer_norm(f + h, gamma, beta)
        return jax.nn.relu(out)

    def _L0_ffn_ref(x, Wr, W1, b1, W2, b2, fw1, fb1, fw2, fb2):
        import jax, jax.numpy as jnp
        import numpy as np
        B, S = (4, 256)
        D_MODEL, D_FF, N_EXPERTS, TOP_K = (128, 512, 8, 2)
        T = B * S
        CAPACITY_FACTOR, MIN_CAP = (1.25, 4)
        CAP = max(int(CAPACITY_FACTOR * (T * TOP_K / N_EXPERTS)), MIN_CAP)
        Bx, Sx, D = x.shape
        Tn = Bx * Sx
        xf = x.reshape(Tn, D)
        logits = xf @ Wr
        probs = jax.nn.softmax(logits, axis=-1)
        scores, experts = jax.lax.top_k(probs, TOP_K)
        scores = scores / jnp.maximum(scores.sum(-1, keepdims=True), 1e-09)
        y_fb = jax.nn.gelu(xf @ fw1 + fb1, approximate=False) @ fw2 + fb2
        y = jnp.zeros_like(xf)
        fb_mask = jnp.zeros((Tn,), bool)
        for e in range(N_EXPERTS):
            assign = experts == e
            w_e = jnp.where(assign, scores, 0.0).sum(-1)
            eligible = assign.any(-1) & ~fb_mask
            rank = jnp.cumsum(eligible.astype(jnp.int32)) - 1
            keep = eligible & (rank < CAP)
            overflow = eligible & ~keep
            fb_mask = fb_mask | overflow
            y = jnp.where(overflow[:, None], y_fb, y)
            idx = jnp.nonzero(keep, size=CAP, fill_value=0)[0]
            valid = jnp.arange(CAP) < keep.sum()
            h = jax.nn.gelu(xf[idx] @ W1[e] + b1[e], approximate=False)
            y_e = h @ W2[e] + b2[e]
            y = y.at[idx].add(y_e * (w_e[idx] * valid)[:, None])
        return y.reshape(Bx, Sx, D)
    x = x + _L0_attn_ref(_layernorm(x, axis=-1), L0_attn_att_mask, L0_attn_S_n, L0_attn_W_Q, L0_attn_W_K, L0_attn_W_V)
    x = x + _L0_xattn_ref(_layernorm(x, axis=-1), ctx_1024, L0_xattn_Wq, L0_xattn_Wk, L0_xattn_Wv, L0_xattn_Wcq, L0_xattn_Wck, L0_xattn_Wcv, L0_xattn_gamma, L0_xattn_beta, L0_xattn_W1, L0_xattn_b1)
    x = x + _L0_ffn_ref(_layernorm(x, axis=-1), L0_ffn_Wr, L0_ffn_W1, L0_ffn_b1, L0_ffn_W2, L0_ffn_b2, L0_ffn_fw1, L0_ffn_fb1, L0_ffn_fw2, L0_ffn_fb2)
    return x

_drawn_inputs = setup_inputs


def setup_inputs(seed=0):
    import zlib

    import numpy as np

    out = dict(_drawn_inputs(seed))
    spreads = {'L0_attn_S_n': (0.0, 0.1),
     'L0_xattn_gamma': (1.0, 0.2),
     'L0_xattn_beta': (0.0, 0.1),
     'L0_xattn_b1': (0.0, 0.1),
     'L0_ffn_b1': (0.0, 0.695),
     'L0_ffn_b2': (0.0, 0.476),
     'L0_ffn_fb1': (0.0, 0.1),
     'L0_ffn_fb2': (0.0, 0.1)}
    factors = {}
    for name, (base, spread) in spreads.items():
        noise = np.random.default_rng([zlib.crc32(name.encode()), seed]).standard_normal(out[name].shape)
        drawn = base * np.exp(spread * noise) if base else spread * noise
        out[name] = jnp.asarray(drawn.astype(out[name].dtype))
    for name, factor in factors.items():
        out[name] = (out[name] * factor).astype(out[name].dtype)
    return out
```

```python
import concourse.bass as bass
from concourse import mybir
from contextlib import ExitStack

DVE_ORDER = (
    (0, "a_stats"), (1, "a_p"), (0, "a_aggr"), (2, "b_max"), (5, "d_x2"), (4, "d_norm"), (1, "a_x1"),
    (0, "a_norm"), (1, "b_stats"), (2, "b_rinv"), (5, "e_stats"), (1, "b_aggr"), (3, "c_max"), (5, "e_aggr"),
    (2, "b_a"), (4, "d_u"), (1, "b_norm"), (4, "d_stats2"), (2, "c_stats"), (4, "d_aggr2"), (3, "c_rinv"),
    (5, "e_norm"), (2, "c_aggr"), (3, "c_c"), (4, "d_norm2"), (3, "d_stats"), (2, "c_norm"), (3, "d_aggr"),
    (5, "e_l_sb"),
)
POOL_ORDER = (
    (5, "d_t"), (4, "d_rstd"), (0, "a_rstd"), (4, "d_h"), (1, "b_rstd"), (5, "e_rstd"), (3, "c_h"),
    (4, "d_rstd2"), (2, "c_rstd"),
)
PE_ORDER = (
    (1, "a_o"), (3, "c_g"), (3, "c_v"), (4, "d_xt"), (2, "b_pt"), (0, "a_xt"), (3, "c_s"), (2, "b_o"),
    (4, "d_f"), (0, "a_g"), (0, "a_v"), (3, "c_pt"), (1, "b_xt"), (0, "a_s"), (3, "c_o"), (1, "b_g"),
    (5, "e_xt"), (1, "b_v"), (5, "e_l"), (1, "b_s"), (2, "c_xt"), (2, "c_ct"),
)
ACT_ORDER = (
    (2, "b_exp"), (3, "c_g_sb"), (2, "b_pt_sb"), (4, "d_ht_sb"), (0, "a_xt_sb"), (3, "c_v_sb"), (3, "c_exp"),
    (0, "a_g_sb"), (3, "c_pt_sb"), (1, "b_xt_sb"), (0, "a_v_sb"), (1, "b_g_sb"), (5, "e_xt_sb"), (1, "b_v_sb"),
    (2, "c_ht_sb"), (2, "c_ct_sb"),
)
SP_ORDER = ((2, "load_ctx"), (5, "store_z"), (5, "store_zT"))



def decoder_program(nc, A, out):
    fp32, bf16 = mybir.dt.float32, mybir.dt.bfloat16
    i32, u32 = mybir.dt.int32, mybir.dt.uint32
    ALU, ACT, AX = mybir.AluOpType, mybir.ActivationFunctionType, mybir.AxisListType

    NB, P, D = A["x"].shape
    SC = A["ctx_1024"].shape[1]
    J = 4
    G = NB // J
    W = J * D
    NT = NB
    NE, _, FF = A["L0_ffn_W1"].shape
    FB = FF // P
    CAP = 320
    SQ = (P, P, CAP - 2 * P)
    NQ = len(SQ)
    TOKENS = NB * P
    EPS1, EPS2 = 1e-5, 1e-3
    SCALE = float(D) ** -0.5
    NEG = -1e30
    LAGS = 1 + max(lag for o in (DVE_ORDER, POOL_ORDER, PE_ORDER, ACT_ORDER) for lag, _ in o)
    GF = 11

    x_v = A["x"].rearrange("(g j) t d -> t g j d", j=J)
    ctx_v = A["ctx_1024"].rearrange("(g j) s d -> s g j d", j=J)
    out_v = out.rearrange("(g j) t d -> t g j d", j=J)
    z_rows = nc.dram_tensor("z_rows", (TOKENS, D), fp32, kind="Internal").ap()
    z_rows_v = z_rows.rearrange("(g j t) d -> t g j d", j=J, t=P)
    SPARE = NE * NQ * P
    acc_rows = nc.dram_tensor("acc_rows", (TOKENS + SPARE, D), fp32, kind="Internal").ap()
    acc_v = acc_rows[0:TOKENS, :].rearrange("(g j t) d -> t g j d", j=J, t=P)
    acc_fill = acc_rows.rearrange("(p a b) d -> p a (b d)", p=P, b=J)
    NFILL = (TOKENS + SPARE) // P // J

    with ExitStack() as ctx:
        def sb(name, shape, dt=fp32):
            return ctx.enter_context(nc.sbuf_tensor(name, shape, dt))

        def sem(name):
            return ctx.enter_context(nc.semaphore(name))

        xs = sb("xs", [P, G, W])
        mid = sb("mid", [P, G, W])
        zT = sb("zT", [P, G, W])
        cx = sb("cx", [SC, W])
        ident = sb("ident", [P, P])
        identb = sb("identb", [P, P], bf16)
        decay = sb("decay", [P, P])
        maskf = sb("maskf", [P, P])
        maskb = sb("maskb", [P, J, P], bf16)
        trif = sb("trif", [P, P])
        trib = sb("trib", [P, P], bf16)
        onesb = sb("onesb", [P, P], bf16)
        NW = 12
        wts = sb("wts", [P, NW, D])
        Wn = {n: wts[:, i, :] for i, n in enumerate(
            ["L0_attn_W_Q", "L0_attn_W_K", "L0_attn_W_V", "L0_xattn_Wq", "L0_xattn_Wk", "L0_xattn_Wv",
             "L0_xattn_Wcq", "L0_xattn_Wck", "L0_xattn_Wcv", "L0_xattn_W1"])}
        wtT = sb("wtT", [P, 6, D])
        mqk = sb("mqk", [P, 3, D])
        MA, MB, MC = (mqk[:, i, :] for i in range(3))
        gam = sb("gam", [P, D])
        bet = sb("bet", [P, D])
        gamT = sb("gamT", [P, 1])
        betT = sb("betT", [P, 1])
        negh = sb("negh", [P, J])
        wr = sb("wr", [P, NE])
        BR = 65
        ball = sb("ball", [BR, (2 + NE) * D], bf16)
        fw1 = sb("fw1", [P, FF])
        fw2 = sb("fw2", [P, FB, D])
        fb1 = sb("fb1", [P, FB])
        eb1 = sb("eb1", [P, NE, FB])
        zeros = sb("zeros", [P, W])

        st = {k: sb(f"st_{k}", [P, J, 6]) for k in ("a", "b", "c", "d", "u", "e")}
        mv = {k: sb(f"mv_{k}", [P, J, 2]) for k in ("a", "b", "c", "d", "u", "e")}
        ve = {k: sb(f"ve_{k}", [P, J]) for k in ("a", "b", "c", "d", "u", "e")}
        rs = {k: sb(f"rs_{k}", [P, J]) for k in ("a", "b", "c", "d", "u", "e")}
        work = sb("work", [P, 29, W])
        places = iter(range(29))

        def buffers(*keys):
            return {k: work[:, next(places), :] for k in keys}

        gq, va, pa = {}, {}, {}
        gq.update(buffers("c"))
        va.update(buffers("c"))
        pa.update(buffers("c"))
        pT = buffers("c")
        hres = buffers("c", "d")
        hmul = buffers("c", "d", "u")
        ud, td = buffers("u").values(), buffers("t").values()
        (ud,), (td,) = ud, td
        nrm = buffers("u", "c", "d", "e")
        tr = buffers("c", "d", "e")
        nrm.update(buffers("a", "b"))
        tr.update(buffers("a", "b"))
        gq.update(buffers("a", "b"))
        va.update(buffers("a", "b"))
        pa.update(buffers("a", "b"))
        pT.update(buffers("b"))
        cT = sb("cT", [P, J * SC])
        nmax = {k: sb(f"nmax_{k}", [P, J]) for k in ("b", "c")}
        rsum = {k: sb(f"rsum_{k}", [P, J]) for k in ("b", "c")}
        rinv = {k: sb(f"rinv_{k}", [P, J]) for k in ("b", "c")}
        BW = (2 + NE) * D
        brow, bres = (work[0:BR, i:i + 3, :].rearrange("p a b -> p (a b)")[:, 0:BW] for i in (0, 3))
        bhi, bmid, blo = (work[0:BR, i:i + 2, :].rearrange("p a b -> p (a b)").bitcast(bf16)[:, 0:BW] for i in (6, 8, 10))
        logits = sb("logits", [P, NT, NE])

        rt = {k: sb(f"rt_{k}", [P, NT]) for k in ("max", "sum", "inv", "m1", "m2", "i1", "i2", "free", "cum", "drop")}
        def te(t):
            return t[:, :].rearrange("p (t e) -> p t e", e=NE)

        def et(t):
            return t[:, :].rearrange("p (e t) -> p e t", e=NE)

        ex, prob, cand = te(nrm["a"]), te(tr["a"]), te(gq["a"])
        oh = [te(va["a"]), te(pa["a"])]
        wch = sb("wch", [P, 2, NT])
        wres = sb("wres", [P, 2, NT])
        revio = sb("revio", [P, NE])
        col0 = sb("col0", [P, NE])
        asg = et(nrm["b"])
        elig = sb("elig", [P, NT])
        eligb = sb("eligb", [P, NT + 2], bf16)
        ones = sb("ones", [P, NT])
        rank = et(tr["b"])
        keep = et(gq["b"])
        piece, slot, colm = et(va["b"]), et(pa["b"]), et(pT["b"])
        NC = NE * NQ
        NV = 5
        CT = 8
        NCH = 2 * NT // CT
        slotc = sb("slotc", [P, 2 * NT])
        colc = sb("colc", [P, 2 * NT])
        vals = sb("vals", [P, 2 * NT, NV], bf16)
        iop = sb("iop", [P, P])
        ioc = sb("ioc", [P, NC])
        iot = sb("iot", [P, NT])
        plus1 = sb("plus1", [P, 1])
        spare = sb("spare", [P, NC])
        ohp = [work[:, 8 + i, :].bitcast(bf16).rearrange("p (t q) -> p t q", q=P) for i in range(2)]
        ohc = [sb(f"ohc{i}", [P, CT, NC], bf16) for i in range(2)]
        ohv = [work[:, 10 + i, :].bitcast(bf16)[:, 0:CT * NV * NC].rearrange("p (t v c) -> p t v c", v=NV, c=NC)
               for i in range(2)]
        zb = sb("zb", [P, P], bf16)
        tab = sb("tab", [P, NV, NC])
        tidx = sb("tidx", [P, NC])
        temp = sb("temp", [P, NC])
        tw = sb("tw", [P, NC])
        gidx = sb("gidx", [P, NC], u32)
        sidx = sb("sidx", [P, NC], u32)
        hf = [work[:, FB * i:FB * (i + 1), :] for i in range(2)]
        ew1 = [sb(f"ew1_{i}", [P, FF]) for i in range(2)]
        ew2 = [sb(f"ew2_{i}", [P, FB, D]) for i in range(2)]
        gi = [sb(f"gi{i}", [P, NQ], u32) for i in range(2)]
        si = [sb(f"si{i}", [P, NQ], u32) for i in range(2)]
        xg = [t[:, 0:NQ * D].rearrange("p (n d) -> p n d", d=D) for t in (nrm["a"], tr["a"])]
        xgT = [t[:, 0:CAP] for t in (gq["a"], va["a"])]
        ye = [t[:, 0:NQ * D].rearrange("p (n d) -> p n d", d=D) for t in (pa["a"], nrm["b"])]
        NF = 4
        fin = [nrm["c"], nrm["d"], tr["c"], tr["d"]]

        bank = [ctx.enter_context(nc.psum_tensor(f"bank{i}", [P, W], fp32)) for i in range(8)]
        a0, a1, b0, b1, c0, c1, d0, e0 = bank

        names = set(n for o in (DVE_ORDER, POOL_ORDER, PE_ORDER, ACT_ORDER) for _, n in o)
        S = {n: sem(n) for n in sorted(names)}
        for n in ("a_veps", "b_veps", "c_veps", "d_veps", "d_veps2", "e_veps", "c_hmul", "d_hmul", "d_tmul"):
            S[n] = sem(n)
        s_wload, s_const, s_x0, s_x1, s_x2, s_ctx = (
            sem(n) for n in ("weights_loaded", "constants_loaded", "x_first", "x_next", "x_rest", "ctx_loaded"))
        s_brow = sem("bias_rows_loaded")
        s_prep_dve, s_prep_pe, s_prep_act = sem("prep_dve"), sem("prep_pe"), sem("prep_act")
        s_prep_pool = sem("prep_pool")
        s_zrow, s_zT = sem("z_rows_stored"), sem("zT_stored")
        s_fill = sem("acc_filled")
        s_late = sem("late_constants")
        s_fw = sem("fallback_weights")
        r_chain, r_sub, r_exp, r_elig, r_cnt, r_step = (
            sem(n) for n in ("route_chain", "route_shifted", "route_exp", "route_eligible", "route_counts", "route_rank"))
        t_chunk, t_used, t_table = (sem(n) for n in ("table_chunk", "table_chunk_used", "table_sum"))
        t_link, t_index = sem("table_chain"), sem("table_ready")
        f_h, f_gelu, f_y, f_ysb = (sem(n) for n in ("f_hidden", "f_gelu", "f_out", "f_out_sb"))
        x_w = [sem(f"x_weights{i}") for i in range(2)]
        x_g = [sem(f"x_gathered{i}") for i in range(2)]
        x_t, x_tsb, x_h, x_gelu, x_y, x_ysb, x_add, x_idx = (
            sem(n) for n in ("x_transposed", "x_transposed_sb", "x_hidden", "x_gelu", "x_out", "x_out_sb", "x_added",
                             "x_indices"))
        o_base, o_fin = sem("base_ready"), sem("result_ready")
        o_ld = [sem(f"acc_loaded{i}") for i in range(NF)]
        o_st = [sem(f"result_stored{i}") for i in range(NF)]

        def r(t):
            return t[:, :].rearrange("p (j d) -> p j d", j=J)

        def later(g):
            return not (isinstance(g, int) and g == 0)

        def wait_apart(eng, semaphore, value):
            value = value if isinstance(value, int) else eng.to_reg(value)
            eng.wait_ge(s_const, NCONST)
            eng.wait_ge(semaphore, value)

        NWAIT = 10 * 16
        NCONST = 9 * 16
        NTAIL = 7 * 16

        with nc.Block() as block:
            def runs(eng, order, steps):
                def turn(t, filled):
                    for lag, name in order:
                        if filled or 0 <= t - lag < G:
                            steps[name](t - lag)
                for t in range(LAGS):
                    turn(t, False)
                with eng.Fori(LAGS, G) as t:
                    turn(t, True)
                for t in range(G, G + LAGS - 1):
                    turn(t, False)

            @block.sync
            def _(sp):
                for n, t in Wn.items():
                    sp.dma_start(t, A[n]).then_inc(s_wload, 16)
                sp.dma_start(ident[:, :], A["c_ident"]).then_inc(s_const, 16)
                sp.dma_start(xs[:, 0, :].rearrange("p (j d) -> p j d", j=J), x_v[:, 0, :, :]).then_inc(s_x0, 16)
                sp.dma_start(decay[:, :], A["c_decay"]).then_inc(s_const, 16)
                sp.dma_start(maskf[:, :], A["c_mask"]).then_inc(s_const, 16)
                sp.dma_start(trif[:, :], A["c_tri"]).then_inc(s_const, 16)
                sp.dma_start(gam[:, :], A["L0_xattn_gamma"].partition_broadcast(P)).then_inc(s_const, 16)
                sp.dma_start(bet[:, :], A["L0_xattn_beta"].partition_broadcast(P)).then_inc(s_const, 16)
                sp.dma_start(gamT[:, :], A["L0_xattn_gamma"].unsqueeze(1)).then_inc(s_const, 16)
                sp.dma_start(betT[:, :], A["L0_xattn_beta"].unsqueeze(1)).then_inc(s_const, 16)
                sp.dma_start(wr[:, :], A["L0_ffn_Wr"]).then_inc(s_const, 16)
                sp.wait_ge(s_prep_pool, 1)
                for k in (0, 32, 64):
                    sp.dma_start(brow[k:k + 1, 0:D], A["L0_xattn_b1"].unsqueeze(0)).then_inc(s_brow, 16)
                    sp.dma_start(brow[k:k + 1, D:2 * D], A["L0_ffn_fb2"].unsqueeze(0)).then_inc(s_brow, 16)
                    sp.dma_start(brow[k:k + 1, 2 * D:(2 + NE) * D],
                                 A["L0_ffn_b2"].rearrange("e d -> (e d)").unsqueeze(0)).then_inc(s_brow, 16)
                sp.dma_start(revio[:, :], A["c_revio"]).then_inc(s_late, 16)
                sp.dma_start(col0[:, :], A["c_col0"]).then_inc(s_late, 16)
                sp.dma_start(iop[:, :], A["c_iop"]).then_inc(s_late, 16)
                sp.dma_start(ioc[:, :], A["c_ioc"]).then_inc(s_late, 16)
                sp.dma_start(iot[:, :], A["c_iot"]).then_inc(s_late, 16)
                sp.dma_start(plus1[:, :], A["c_plus1"]).then_inc(s_late, 16)
                sp.dma_start(spare[:, :], A["c_spare"]).then_inc(s_late, 16)
                sp.dma_start(fw1[:, :], A["L0_ffn_fw1"]).then_inc(s_fw, 16)
                sp.dma_start(fw2[:, :, :], A["L0_ffn_fw2"].rearrange("(k p) d -> p k d", p=P)).then_inc(s_fw, 16)
                with nc.allow_non_contiguous_dma("bias columns, once"):
                    sp.dma_start(fb1[:, :], A["L0_ffn_fb1"].rearrange("(k p) -> p k", p=P)).then_inc(s_fw, 16)
                    for e in range(NE):
                        sp.dma_start(eb1[:, e, :], A["L0_ffn_b1"][e, :].rearrange("(k p) -> p k", p=P)).then_inc(s_fw, 16)
                for g in range(1, 4):
                    sp.dma_start(xs[:, g, :].rearrange("p (j d) -> p j d", j=J), x_v[:, g, :, :]).then_inc(s_x1, 16)
                sp.dma_start(xs[:, 4:G, :].rearrange("p g (j d) -> p (g j) d", j=J),
                             x_v[:, 4:G].rearrange("t g j d -> t (g j) d")).then_inc(s_x2, 16)

                def load_ctx(g):
                    if later(g):
                        sp.wait_ge(S["c_ct"], g)
                    sp.dma_start(cx[:, :].rearrange("s (j d) -> s j d", j=J), ctx_v[:, g, :, :]).then_inc(s_ctx, 16)

                def store_z(g):
                    sp.wait_ge(S["e_norm"], g + 1)
                    sp.dma_start(z_rows_v[:, g, :, :], r(nrm["e"])).then_inc(s_zrow, 16)

                def store_zT(g):
                    sp.wait_ge(S["e_xt_sb"], g + 1)
                    sp.dma_start(zT[:, g, :], tr["e"][:, :]).then_inc(s_zT, 16)

                sp.wait_ge(s_prep_pool, 2)
                sp.dma_start(acc_fill, zeros[:, :].unsqueeze(1).broadcast_to([P, NFILL, W])).then_inc(s_fill, 16)

                def load_expert(e, i):
                    if not isinstance(e, int):
                        sp.wait_ge(x_y, e - 1)
                    sp.dma_start(ew1[i][:, :], A["L0_ffn_W1"][e, :, :]).then_inc(x_w[i], 16)
                    sp.dma_start(ew2[i][:, :, :], A["L0_ffn_W2"][e, :, :].rearrange("(k p) d -> p k d", p=P))\
                      .then_inc(x_w[i], 16)

                load_expert(0, 0)
                load_expert(1, 1)
                runs(sp, SP_ORDER, dict(load_ctx=load_ctx, store_z=store_z, store_zT=store_zT))
                with sp.Fori(1, NE // 2) as q:
                    for i in range(2):
                        load_expert(2 * q + i, i)
                sp.wait_ge(x_add, 16 * NQ * NE)
                for i in range(NF):
                    sp.dma_start(fin[i][:, :].rearrange("p (j d) -> p j d", j=J), acc_v[:, i, :, :]).then_inc(o_ld[i], 16)
                with sp.Fori(1, G // NF) as q:
                    for i in range(NF):
                        sp.wait_ge(o_st[i], 16 * q)
                        sp.dma_start(fin[i][:, :].rearrange("p (j d) -> p j d", j=J), acc_v[:, NF * q + i, :, :])\
                          .then_inc(o_ld[i], 16)

            @block.tensor
            def _(pe):
                pe.wait_ge(s_wload, NWAIT)
                pe.wait_ge(s_const, NCONST)
                keys = ["L0_attn_W_Q", "L0_attn_W_K", "L0_xattn_Wq", "L0_xattn_Wk", "L0_xattn_Wcq", "L0_xattn_Wck"]
                for i, n in enumerate(keys):
                    last = pe.transpose(bank[i // 4][:, (i % 4) * D:(i % 4 + 1) * D], Wn[n], ident[:, :])
                last.then_inc(s_prep_pe, 1)
                pe.wait_ge(s_prep_act, 2)
                for k in range(3):
                    last = pe.matmul(bank[2][:, k * D:(k + 1) * D], wtT[:, 2 * k, :], wtT[:, 2 * k + 1, :],
                                     start=True, stop=True)
                last.then_inc(s_prep_pe, 1)
                pe.wait_ge(s_prep_act, 3)
                pe.wait_ge(s_prep_dve, 6)

                def transposed(k, dst):
                    def step(g):
                        done = {"a": "a_norm", "b": "b_norm", "c": "c_norm", "d": "d_norm", "e": "e_norm"}[k]
                        free = {"a": "a_x1", "b": "b_pt_sb", "c": "c_c", "d": "d_u", "e": "e_l_sb"}[k]
                        pe.wait_ge(S[done], g + 1)
                        if later(g):
                            pe.wait_ge(S[free], g)
                        for j in range(J):
                            last = pe.transpose(dst[:, j * D:(j + 1) * D], nrm[k][:, j * D:(j + 1) * D], ident[:, :])
                        last.then_inc(S[f"{k}_xt"], 1)
                    return step

                def a_g(g):
                    pe.wait_ge(S["a_xt_sb"], g + 1)
                    if later(g):
                        pe.wait_ge(S["a_p"], g)
                    pe.matmul(a1[:, :], MA, tr["a"][:, :], start=True, stop=True).then_inc(S["a_g"], 1)

                def a_v(g):
                    pe.wait_ge(S["a_xt_sb"], g + 1)
                    for j in range(J):
                        c = slice(j * D, (j + 1) * D)
                        last = pe.matmul(a0[:, c], tr["a"][:, c], Wn["L0_attn_W_V"], start=True, stop=True)
                    last.then_inc(S["a_v"], 1)

                def a_s(g):
                    pe.wait_ge(S["a_g_sb"], g + 1)
                    for j in range(J):
                        c = slice(j * D, (j + 1) * D)
                        last = pe.matmul(a1[:, c], tr["a"][:, c], gq["a"][:, c], start=True, stop=True)
                    last.then_inc(S["a_s"], 1)

                def a_o(g):
                    pe.wait_ge(S["a_p"], g + 1)
                    pe.wait_ge(S["a_v_sb"], g + 1)
                    for j in range(J):
                        c = slice(j * D, (j + 1) * D)
                        last = pe.matmul(a0[:, c], va["a"][:, c], pa["a"][:, c], start=True, stop=True)
                    last.then_inc(S["a_o"], 1)

                def b_g(g):
                    pe.wait_ge(S["b_xt_sb"], g + 1)
                    if later(g):
                        pe.wait_ge(S["b_a"], g)
                    pe.matmul(b1[:, :], MB, tr["b"][:, :], start=True, stop=True).then_inc(S["b_g"], 1)

                def b_v(g):
                    pe.wait_ge(S["b_xt_sb"], g + 1)
                    for j in range(J):
                        c = slice(j * D, (j + 1) * D)
                        last = pe.matmul(b0[:, c], tr["b"][:, c], Wn["L0_xattn_Wv"], start=True, stop=True)
                    last.then_inc(S["b_v"], 1)

                def b_s(g):
                    pe.wait_ge(S["b_g_sb"], g + 1)
                    pe.matmul(b1[:, :], identb[:, :], maskb[:, :, :].rearrange("p j d -> p (j d)"),
                              start=True, stop=False, skip_group_check=True)
                    for j in range(J):
                        c = slice(j * D, (j + 1) * D)
                        last = pe.matmul(b1[:, c], gq["b"][:, c], tr["b"][:, c], start=False, stop=(j == J - 1),
                                         skip_group_check=True)
                    last.then_inc(S["b_s"], 1)

                def b_pt(g):
                    pe.wait_ge(S["b_exp"], g + 1)
                    pe.wait_ge(S["b_v_sb"], g + 1)
                    for j in range(J):
                        c = slice(j * D, (j + 1) * D)
                        last = pe.transpose(b0[:, c], pa["b"][:, c], ident[:, :])
                    last.then_inc(S["b_pt"], 1)

                def b_o(g):
                    pe.wait_ge(S["b_pt_sb"], g + 1)
                    for j in range(J):
                        c = slice(j * D, (j + 1) * D)
                        last = pe.matmul(b1[:, c], pT["b"][:, c], va["b"][:, c], start=True, stop=True)
                    last.then_inc(S["b_o"], 1)

                def c_ct(g):
                    if later(g):
                        pe.wait_ge(S["c_pt_sb"], g)
                    pe.wait_ge(s_ctx, 16 * (g + 1))
                    for j in range(J):
                        last = pe.transpose(c1[:, j * SC:(j + 1) * SC], cx[:, j * D:(j + 1) * D], ident[0:SC, 0:SC])
                    last.then_inc(S["c_ct"], 1)

                def c_v(g):
                    pe.wait_ge(S["c_ct_sb"], g + 1)
                    for j in range(J):
                        last = pe.matmul(c1[0:SC, j * D:(j + 1) * D], cT[:, j * SC:(j + 1) * SC],
                                         Wn["L0_xattn_Wcv"], start=True, stop=True)
                    last.then_inc(S["c_v"], 1)

                def c_g(g):
                    pe.wait_ge(S["c_ht_sb"], g + 1)
                    pe.matmul(c0[:, :], MC, tr["c"][:, :], start=True, stop=True).then_inc(S["c_g"], 1)

                def c_s(g):
                    pe.wait_ge(S["c_g_sb"], g + 1)
                    pe.wait_ge(S["c_ct_sb"], g + 1)
                    for j in range(J):
                        last = pe.matmul(c0[:, j * SC:(j + 1) * SC], gq["c"][:, j * D:(j + 1) * D],
                                         cT[:, j * SC:(j + 1) * SC], start=True, stop=True)
                    last.then_inc(S["c_s"], 1)

                def c_pt(g):
                    pe.wait_ge(S["c_exp"], g + 1)
                    pe.wait_ge(S["c_v_sb"], g + 1)
                    for j in range(J):
                        last = pe.transpose(c1[0:SC, j * D:(j + 1) * D], pa["c"][:, j * SC:(j + 1) * SC], ident[:, :])
                    last.then_inc(S["c_pt"], 1)

                def c_o(g):
                    pe.wait_ge(S["c_pt_sb"], g + 1)
                    for j in range(J):
                        c = slice(j * D, (j + 1) * D)
                        last = pe.matmul(c0[:, c], pT["c"][0:SC, c], va["c"][0:SC, c], start=True, stop=True)
                    last.then_inc(S["c_o"], 1)

                def d_f(g):
                    pe.wait_ge(S["d_ht_sb"], g + 1)
                    pe.matmul(d0[:, :], onesb[0:BR, :], ball[:, 0:D].unsqueeze(1).broadcast_to([BR, J, D]),
                              start=True, stop=False, skip_group_check=True)
                    for j in range(J):
                        c = slice(j * D, (j + 1) * D)
                        last = pe.matmul(d0[:, c], tr["d"][:, c], Wn["L0_xattn_W1"], start=False, stop=(j == J - 1),
                                         skip_group_check=True)
                    last.then_inc(S["d_f"], 1)

                def e_l(g):
                    pe.wait_ge(S["e_xt_sb"], g + 1)
                    for j in range(J):
                        last = pe.matmul(e0[:, j * NE:(j + 1) * NE], tr["e"][:, j * D:(j + 1) * D], wr[:, :],
                                         start=True, stop=True)
                    last.then_inc(S["e_l"], 1)

                runs(pe, PE_ORDER, dict(
                    a_xt=transposed("a", a0), b_xt=transposed("b", b0), c_xt=transposed("c", c0),
                    d_xt=transposed("d", d0), e_xt=transposed("e", e0),
                    a_g=a_g, a_v=a_v, a_s=a_s, a_o=a_o, b_g=b_g, b_v=b_v, b_s=b_s, b_pt=b_pt, b_o=b_o,
                    c_ct=c_ct, c_v=c_v, c_g=c_g, c_s=c_s, c_pt=c_pt, c_o=c_o, d_f=d_f, e_l=e_l))

                pe.wait_ge(S["e_l_sb"], G)
                pe.wait_ge(s_fw, (3 + NE) * 16)
                pe.wait_ge(s_zT, 16 * G)

                def f_hidden(g):
                    for k in range(FB):
                        if not (isinstance(g, int) and g == 0):
                            pe.wait_ge(f_gelu, FB * (g - 1) + k + 1)
                        pe.matmul(bank[k][:, :], fw1[:, k * P:(k + 1) * P], zT[:, g, :], start=True, stop=True)\
                          .then_inc(f_h, 1)

                def f_out(g, i):
                    y = bank[4 + i]
                    pe.wait_ge(f_gelu, FB * (g + 1))
                    if not (isinstance(g, int) and g < 2):
                        pe.wait_ge(f_ysb, g - 1)
                    pe.matmul(y[:, :], onesb[0:BR, :], ball[:, D:2 * D].unsqueeze(1).broadcast_to([BR, J, D]),
                              start=True, stop=False, skip_group_check=True)
                    for j in range(J):
                        for k in range(FB):
                            last = pe.matmul(y[:, j * D:(j + 1) * D], hf[i][:, k, j * P:(j + 1) * P], fw2[:, k, :],
                                             start=False, stop=(j == J - 1 and k == FB - 1), skip_group_check=True)
                    last.then_inc(f_y, 1)

                def f_unit(g, i):
                    f_hidden(g + 1)
                    f_out(g, i)

                def route(e):
                    pe.wait_ge(r_elig, e + 1)
                    pe.matmul(bank[6][:, 0:NT], trib[:, :], eligb[:, 1:NT + 1], start=True, stop=True)
                    pe.matmul(bank[6][:, NT:2 * NT], onesb[:, :], eligb[:, 0:NT], start=True, stop=True)\
                      .then_inc(r_cnt, 1)

                def table(n, i):
                    pe.wait_ge(t_chunk, n + 1)
                    for t in range(CT):
                        last = pe.matmul(bank[7][:, 0:NV * NC], ohp[i][:, t, :],
                                         ohv[i][:, t, :, :].rearrange("p v c -> p (v c)"), start=False, stop=False,
                                         skip_group_check=True)
                    last.then_inc(t_used, 1)

                def table_edge(start):
                    return pe.matmul(bank[7][:, 0:NV * NC], zb[:, :], ohv_zero, start=start, stop=not start,
                                     skip_group_check=True)

                ohv_zero = zb[:, 0:NV * NC]
                f_hidden(0)
                f_unit(0, 0)
                f_unit(1, 1)
                with pe.Fori(0, 2) as q:
                    for i in range(2):
                        f_unit(2 + 2 * q + i, i)
                        route(4 * q + 2 * i)
                        route(4 * q + 2 * i + 1)
                table_edge(True)
                with pe.Fori(0, 2) as q:
                    for i in range(2):
                        f_unit(6 + 2 * q + i, i)
                        for n in range(4):
                            table(8 * q + 4 * i + n, n % 2)
                table_edge(False).then_inc(t_table, 1)
                f_out(10, 0)

                def x_hidden(e, i, arrived):
                    pe.wait_ge(x_tsb, e + 1)
                    pe.wait_ge(x_w[i], arrived)
                    for k in range(FB):
                        if not (isinstance(e, int) and e == 0):
                            pe.wait_ge(x_gelu, FB * (e - 1) + k + 1)
                        pe.matmul(bank[k][:, 0:CAP], ew1[i][:, k * P:(k + 1) * P], xgT[i][:, :], start=True, stop=True)\
                          .then_inc(x_h, 1)

                def x_out(e, i):
                    y = bank[4 + i]
                    pe.wait_ge(x_gelu, FB * (e + 1))
                    if not (isinstance(e, int) and e < 2):
                        pe.wait_ge(x_ysb, e - 1)
                    pe.matmul(y[:, 0:NQ * D], onesb[0:BR, :],
                              ball[:, bass.ds((2 + e) * D, D)].unsqueeze(1).broadcast_to([BR, NQ, D]),
                              start=True, stop=False, skip_group_check=True)
                    for n, w in enumerate(SQ):
                        for k in range(FB):
                            last = pe.matmul(y[0:w, n * D:(n + 1) * D], hf[i][:, k, n * P:n * P + w], ew2[i][:, k, :],
                                             start=False, stop=(n == NQ - 1 and k == FB - 1), skip_group_check=True)
                    last.then_inc(x_y, 1)

                def transpose_gathered(e, i, pair):
                    pe.wait_ge(x_g[i], 16 * NQ * (pair + 1))
                    if not (isinstance(e, int) and e == 0):
                        pe.wait_ge(x_tsb, e)
                    for n, w in enumerate(SQ):
                        last = pe.transpose(bank[6][:, n * P:n * P + w], xg[i][0:w, n, :], ident[0:w, 0:w])
                    last.then_inc(x_t, 1)

                pe.wait_ge(f_ysb, GF)
                transpose_gathered(0, 0, 0)
                x_hidden(0, 0, 32)
                transpose_gathered(1, 1, 0)
                x_hidden(1, 1, 32)
                x_out(0, 0)
                transpose_gathered(2, 0, 1)
                x_hidden(2, 0, 64)
                x_out(1, 1)
                with pe.Fori(1, NE // 2 - 1) as q:
                    transpose_gathered(2 * q + 1, 1, q)
                    x_hidden(2 * q + 1, 1, 32 * (q + 1))
                    x_out(2 * q, 0)
                    transpose_gathered(2 * q + 2, 0, q + 1)
                    x_hidden(2 * q + 2, 0, 32 * (q + 2))
                    x_out(2 * q + 1, 1)
                transpose_gathered(NE - 1, 1, NE // 2 - 1)
                x_hidden(NE - 1, 1, 32 * NE // 2)
                x_out(NE - 2, 0)
                x_out(NE - 1, 1)

                pe.wait_ge(x_ysb, NE)
                f_hidden(GF)
                with pe.Fori(0, 2) as q:
                    f_unit(GF + 2 * q, 1)
                    f_unit(GF + 2 * q + 1, 0)
                f_out(G - 1, 1)

            @block.scalar
            def _(act):
                act.wait_ge(s_prep_pe, 1)
                for i in range(6):
                    last = act.activation(wtT[:, i, :], bank[i // 4][:, (i % 4) * D:(i % 4 + 1) * D], ACT.Copy)
                last.then_inc(s_prep_act, 2)
                act.wait_ge(s_prep_pe, 2)
                act.activation(mqk[:, :, :].rearrange("p k d -> p (k d)"), bank[2][:, 0:3 * D], ACT.Copy)\
                   .then_inc(s_prep_act, 1)

                def copied(dst, src, done, name, scale=1.0, free=None):
                    def step(g):
                        act.wait_ge(S[done], g + 1)
                        if free is not None and later(g):
                            act.wait_ge(S[free], g)
                        act.activation(dst, src, ACT.Copy, scale=scale).then_inc(S[name], 1)
                    return step

                def affine(k, src):
                    def step(g):
                        act.wait_ge(S[f"{k}_xt"], g + 1)
                        act.wait_ge(s_const, NCONST)
                        act.activation(tr[k][:, :], src[:, :], ACT.Identity, scale=gamT[:, :], bias=betT[:, :])\
                           .then_inc(S[f"{k}_ht_sb"], 1)
                    return step

                def exponent(k, src, width):
                    def step(g):
                        act.wait_ge(S[f"{k}_max"], g + 1)
                        if later(g):
                            act.wait_ge(S[f"{k}_pt"], g)
                            act.wait_ge(S[f"{k}_rinv"], g)
                        for j in range(J):
                            c = slice(j * width, (j + 1) * width)
                            last = act.activation(pa[k][:, c], src[:, c], ACT.Exp, bias=nmax[k][:, j:j + 1],
                                                  accum_out=rsum[k][:, j:j + 1])
                        last.then_inc(S[f"{k}_exp"], 1)
                    return step

                def e_xt_sb(g):
                    act.wait_ge(S["e_xt"], g + 1)
                    if later(g):
                        act.wait_ge(S["e_l"], g)
                        act.wait_ge(s_zT, 16 * g)
                    act.activation(tr["e"][:, :], e0[:, :], ACT.Copy).then_inc(S["e_xt_sb"], 1)

                runs(act, ACT_ORDER, dict(
                    a_xt_sb=copied(tr["a"][:, :], a0[:, :], "a_xt", "a_xt_sb"),
                    a_g_sb=copied(gq["a"][:, :], a1[:, :], "a_g", "a_g_sb"),
                    a_v_sb=copied(va["a"][:, :], a0[:, :], "a_v", "a_v_sb"),
                    b_xt_sb=copied(tr["b"][:, :], b0[:, :], "b_xt", "b_xt_sb"),
                    b_g_sb=copied(gq["b"][:, :], b1[:, :], "b_g", "b_g_sb", scale=SCALE),
                    b_v_sb=copied(va["b"][:, :], b0[:, :], "b_v", "b_v_sb", free="b_o"),
                    b_exp=exponent("b", b1, D),
                    b_pt_sb=copied(pT["b"][:, :], b0[:, :], "b_pt", "b_pt_sb"),
                    c_ht_sb=affine("c", c0),
                    c_g_sb=copied(gq["c"][:, :], c0[:, :], "c_g", "c_g_sb", scale=SCALE),
                    c_ct_sb=copied(cT[:, :], c1[:, 0:J * SC], "c_ct", "c_ct_sb", free="c_s"),
                    c_v_sb=copied(va["c"][0:SC, :], c1[0:SC, :], "c_v", "c_v_sb", free="c_o"),
                    c_exp=exponent("c", c0, SC),
                    c_pt_sb=copied(pT["c"][0:SC, :], c1[0:SC, :], "c_pt", "c_pt_sb"),
                    d_ht_sb=affine("d", d0),
                    e_xt_sb=e_xt_sb))

                act.wait_ge(r_sub, 1)
                act.activation(prob[:, :, :], ex[:, :, :], ACT.Exp).then_inc(r_exp, 1)
                act.wait_ge(s_fw, (3 + NE) * 16)

                def f_act(g, i):
                    for k in range(FB):
                        act.wait_ge(f_h, FB * g + k + 1)
                        if k == 0 and not (isinstance(g, int) and g < 2):
                            act.wait_ge(f_y, g - 1)
                        act.activation(hf[i][:, k, :], bank[k][:, :], ACT.Gelu, bias=fb1[:, k:k + 1]).then_inc(f_gelu, 1)

                def f_out_sb(g, i):
                    act.wait_ge(f_y, g + 1)
                    act.activation(mid[:, g, :], bank[4 + i][:, :], ACT.Copy).then_inc(f_ysb, 1)

                def x_act(e, i):
                    for k in range(FB):
                        act.wait_ge(x_h, FB * e + k + 1)
                        if k == 0 and not (isinstance(e, int) and e < 2):
                            act.wait_ge(x_y, e - 1)
                        act.activation(hf[i][:, k, 0:CAP], bank[k][:, 0:CAP], ACT.Gelu,
                                       bias=eb1[:, e, k:k + 1]).then_inc(x_gelu, 1)

                f_act(0, 0)
                f_act(1, 1)
                f_out_sb(0, 0)
                with act.Fori(0, (GF - 3) // 2) as q:
                    f_act(2 * q + 2, 0)
                    f_out_sb(2 * q + 1, 1)
                    f_act(2 * q + 3, 1)
                    f_out_sb(2 * q + 2, 0)
                f_act(GF - 1, 0)
                f_out_sb(GF - 2, 1)
                f_out_sb(GF - 1, 0)
                x_act(0, 0)
                x_act(1, 1)
                with act.Fori(1, NE // 2) as q:
                    x_act(2 * q, 0)
                    x_act(2 * q + 1, 1)
                act.wait_ge(x_y, NE)
                f_act(GF, 1)
                with act.Fori(0, 2) as q:
                    f_act(GF + 2 * q + 1, 0)
                    f_out_sb(GF + 2 * q, 1)
                    f_act(GF + 2 * q + 2, 1)
                    f_out_sb(GF + 2 * q + 1, 0)
                f_out_sb(G - 1, 1)

            @block.gpsimd
            def _(pool):
                pool.memset(brow[:, :], 0.0).then_inc(s_prep_pool, 1)
                pool.memset(negh[:, :], -0.5)
                pool.memset(zeros[:, :], 0.0).then_inc(s_prep_pool, 1)
                pool.wait_ge(s_prep_pool, 2)
                pool.wait_ge(s_const, NCONST)

                def root(k, n, eps):
                    u = "u" if n else k
                    def step(g):
                        wait_apart(pool, S[f"{k}_aggr{n}"], g + 1)
                        pool.tensor_scalar(ve[u][:, :], mv[u][:, :, 1], eps, None, ALU.add).then_inc(S[f"{k}_veps{n}"], 1)
                        pool.wait_ge(S[f"{k}_veps{n}"], g + 1)
                        if later(g):
                            pool.wait_ge(S[f"{k}_norm{n}"], g)
                        pool.tensor_tensor(rs[u][:, :], ve[u][:, :], negh[:, :], ALU.pow).then_inc(S[f"{k}_rstd{n}"], 1)
                    return step

                def gamma_beta(src, mul, dst, done, mid_name, name, free):
                    def step(g):
                        pool.wait_ge(S[done], g + 1)
                        pool.tensor_tensor(r(mul), r(src), gam[:, :].unsqueeze(1).broadcast_to([P, J, D]), ALU.mult)\
                            .then_inc(S[mid_name], 1)
                        pool.wait_ge(S[mid_name], g + 1)
                        if later(g):
                            pool.wait_ge(S[free], g)
                        pool.tensor_tensor(r(dst), r(mul), bet[:, :].unsqueeze(1).broadcast_to([P, J, D]), ALU.add)\
                            .then_inc(S[name], 1)
                    return step

                runs(pool, POOL_ORDER, dict(
                    a_rstd=root("a", "", EPS1), b_rstd=root("b", "", EPS1), c_rstd=root("c", "", EPS2),
                    d_rstd=root("d", "", EPS2), d_rstd2=root("d", "2", EPS2), e_rstd=root("e", "", EPS1),
                    c_h=gamma_beta(nrm["c"], hmul["c"], hres["c"], "c_norm", "c_hmul", "c_h", "c_c"),
                    d_h=gamma_beta(nrm["d"], hmul["d"], hres["d"], "d_norm", "d_hmul", "d_h", "d_u"),
                    d_t=gamma_beta(nrm["u"], hmul["u"], td, "d_norm2", "d_tmul", "d_t", "d_x2")))

                pool.wait_ge(t_index, 1)
                pool.wait_ge(s_zrow, 16 * G)
                pool.wait_ge(s_fill, 16)

                def indices(e, i):
                    pool.tensor_copy(gi[i][:, :], gidx[:, bass.ds(NQ * e, NQ)])
                    pool.tensor_copy(si[i][:, :], sidx[:, bass.ds(NQ * e, NQ)]).then_inc(x_idx, 1)
                    wait_apart(pool, x_idx, e + 1)

                def gather(e, i):
                    if not (isinstance(e, int) and e < 2):
                        pool.wait_ge(x_t, e - 1)
                    indices(e, i)
                    for n, w in enumerate(SQ):
                        pool.indirect_dma_start(xg[i][0:w, n, :], None, z_rows,
                                                bass.IndirectOffsetOnAxis(ap=gi[i][0:w, n:n + 1], axis=0))\
                            .then_inc(x_g[i], 16)

                def add(e, i):
                    wait_apart(pool, x_ysb, e + 1)
                    if not (isinstance(e, int) and e == 0):
                        wait_apart(pool, x_add, 16 * NQ * e)
                    for n, w in enumerate(SQ):
                        pool.indirect_dma_start(acc_rows, bass.IndirectOffsetOnAxis(ap=si[i][0:w, n:n + 1], axis=0),
                                                ye[i][0:w, n, :], None, compute_op=ALU.add).then_inc(x_add, 16)

                gather(0, 0)
                gather(1, 1)
                with pool.Fori(0, NE // 2 - 1) as q:
                    for i in range(2):
                        add(2 * q + i, i)
                        pool.wait_ge(x_add, 16 * NQ * (2 * q + i + 1))
                        gather(2 * q + i + 2, i)
                add(NE - 2, 0)
                add(NE - 1, 1)

                def store(q, i):
                    pool.wait_ge(o_fin, NF * q + i + 1)
                    pool.dma_start(out_v[:, NF * q + i, :, :], fin[i][:, :].rearrange("p (j d) -> p j d", j=J))\
                        .then_inc(o_st[i], 16)

                with pool.Fori(0, G // NF) as q:
                    for i in range(NF):
                        store(q, i)
                for i in range(NF):
                    pool.wait_ge(o_st[i], 16 * G // NF)

            @block.vector
            def _(dve):
                dve.wait_ge(s_const, NCONST)
                dve.tensor_copy(maskb[:, :, :], maskf[:, :].unsqueeze(1).broadcast_to([P, J, P]))
                dve.tensor_copy(trib[:, :], trif[:, :])
                dve.tensor_copy(identb[:, :], ident[:, :])
                dve.memset(onesb[:, :], 1.0).then_inc(s_prep_dve, 1)
                dve.memset(ball[:, :], 0.0)
                dve.wait_ge(s_brow, 9 * 16)
                dve.tensor_copy(bhi[:, :], brow[:, :]).then_inc(s_prep_dve, 1)
                dve.wait_ge(s_prep_dve, 2)
                dve.tensor_tensor(bres[:, :], brow[:, :], bhi[:, :], ALU.subtract).then_inc(s_prep_dve, 1)
                dve.wait_ge(s_prep_dve, 3)
                dve.tensor_copy(bmid[:, :], bres[:, :]).then_inc(s_prep_dve, 1)
                dve.wait_ge(s_prep_dve, 4)
                dve.tensor_tensor(blo[:, :], bres[:, :], bmid[:, :], ALU.subtract)
                dve.tensor_copy(ball[0:1, :], bhi[0:1, :])
                dve.tensor_copy(ball[32:33, :], bmid[32:33, :]).then_inc(s_prep_dve, 1)
                dve.wait_ge(s_prep_dve, 5)
                dve.tensor_copy(ball[64:65, :], blo[64:65, :]).then_inc(s_prep_dve, 1)

                def source(k, g):
                    return {"a": xs, "b": xs, "c": mid, "d": mid, "e": xs}[k][:, g, :]

                def stats(k, n, wait):
                    u = "u" if n else k
                    def step(g):
                        if k == "a" and isinstance(g, int):
                            if g == 0:
                                dve.wait_ge(s_x0, 16)
                            if g == 1:
                                dve.wait_ge(s_x1, 3 * 16)
                            if g == 4:
                                dve.wait_ge(s_x2, 16)
                        if wait:
                            wait_apart(dve, S[wait], g + 1)
                        src = ud[:, :] if n else source(k, g)
                        for j in range(J):
                            last = dve.bn_stats(st[u][:, j, :], src[:, j * D:(j + 1) * D])
                        last.then_inc(S[f"{k}_stats{n}"], 1)
                    return step

                def aggr(k, n):
                    u = "u" if n else k
                    def step(g):
                        wait_apart(dve, S[f"{k}_stats{n}"], g + 1)
                        if later(g):
                            dve.wait_ge(S[f"{k}_norm{n}"], g)
                        for j in range(J):
                            last = dve.bn_aggr(mv[u][:, j, :], st[u][:, j, :])
                        last.then_inc(S[f"{k}_aggr{n}"], 1)
                    return step

                def norm(k, n, free):
                    u = "u" if n else k
                    def step(g):
                        dve.wait_ge(S[f"{k}_rstd{n}"], g + 1)
                        if later(g):
                            for f in free:
                                dve.wait_ge(S[f], g)
                            if k == "e":
                                dve.wait_ge(s_zrow, 16 * g)
                        src = ud[:, :] if n else source(k, g)
                        for j in range(J):
                            c = slice(j * D, (j + 1) * D)
                            last = dve.tensor_scalar(nrm[u][:, c], src[:, c], mv[u][:, j, 0:1], rs[u][:, j:j + 1],
                                                     ALU.subtract, ALU.mult)
                        last.then_inc(S[f"{k}_norm{n}"], 1)
                    return step

                def a_p(g):
                    dve.wait_ge(S["a_s"], g + 1)
                    if later(g):
                        dve.wait_ge(S["a_o"], g)
                    dve.tensor_tensor(r(pa["a"]), r(a1), decay[:, :].unsqueeze(1).broadcast_to([P, J, D]), ALU.mult)\
                       .then_inc(S["a_p"], 1)

                def a_x1(g):
                    dve.wait_ge(S["a_o"], g + 1)
                    dve.tensor_tensor(xs[:, g, :], a0[:, :], xs[:, g, :], ALU.add).then_inc(S["a_x1"], 1)

                def row_max(k, src, width):
                    def step(g):
                        dve.wait_ge(S[f"{k}_s"], g + 1)
                        if later(g):
                            dve.wait_ge(S[f"{k}_exp"], g)
                        dve.tensor_reduce(nmax[k][:, :], src[:, 0:J * width].rearrange("p (j s) -> p j s", j=J),
                                          AX.X, ALU.max, negate=True).then_inc(S[f"{k}_max"], 1)
                    return step

                def row_inv(k):
                    def step(g):
                        dve.wait_ge(S[f"{k}_exp"], g + 1)
                        if later(g):
                            dve.wait_ge(S[{"b": "b_a", "c": "c_c"}[k]], g)
                        dve.reciprocal(rinv[k][:, :], rsum[k][:, :]).then_inc(S[f"{k}_rinv"], 1)
                    return step

                def attended(k, src, res, name):
                    def step(g):
                        dve.wait_ge(S[f"{k}_o"], g + 1)
                        dve.wait_ge(S[f"{k}_rinv"], g + 1)
                        if k == "c":
                            dve.wait_ge(S["c_h"], g + 1)
                        for j in range(J):
                            c = slice(j * D, (j + 1) * D)
                            last = dve.scalar_tensor_tensor(mid[:, g, :][:, c], src[:, c], rinv[k][:, j:j + 1], res[:, c],
                                                            ALU.mult, ALU.add)
                        last.then_inc(S[name], 1)
                    return step

                def d_u(g):
                    dve.wait_ge(S["d_f"], g + 1)
                    dve.wait_ge(S["d_h"], g + 1)
                    if later(g):
                        dve.wait_ge(S["d_norm2"], g)
                    dve.scalar_tensor_tensor(ud[:, :], d0[:, :], 0.0, hres["d"][:, :], ALU.max, ALU.add)\
                       .then_inc(S["d_u"], 1)

                def d_x2(g):
                    dve.wait_ge(S["d_t"], g + 1)
                    dve.scalar_tensor_tensor(xs[:, g, :], td[:, :], 0.0, xs[:, g, :], ALU.max, ALU.add)\
                       .then_inc(S["d_x2"], 1)

                def e_l_sb(g):
                    dve.wait_ge(S["e_l"], g + 1)
                    dve.tensor_copy(logits[:, :, :].rearrange("p (g j) e -> p g (j e)", j=J)[:, g, :], e0[:, 0:J * NE])\
                       .then_inc(S["e_l_sb"], 1)

                runs(dve, DVE_ORDER, dict(
                    a_stats=stats("a", "", None), a_aggr=aggr("a", ""), a_norm=norm("a", "", ("a_xt",)),
                    b_stats=stats("b", "", "a_x1"), b_aggr=aggr("b", ""), b_norm=norm("b", "", ("b_xt", "b_a")),
                    c_stats=stats("c", "", "b_a"), c_aggr=aggr("c", ""), c_norm=norm("c", "", ("c_xt", "c_hmul")),
                    d_stats=stats("d", "", "c_c"), d_aggr=aggr("d", ""), d_norm=norm("d", "", ("d_xt", "d_hmul")),
                    d_stats2=stats("d", "2", "d_u"), d_aggr2=aggr("d", "2"), d_norm2=norm("d", "2", ("d_tmul",)),
                    e_stats=stats("e", "", "d_x2"), e_aggr=aggr("e", ""), e_norm=norm("e", "", ("e_xt",)),
                    a_p=a_p, a_x1=a_x1, b_max=row_max("b", b1, D), b_rinv=row_inv("b"),
                    b_a=attended("b", b1, nrm["b"], "b_a"), c_max=row_max("c", c0, SC), c_rinv=row_inv("c"),
                    c_c=attended("c", c0, hres["c"], "c_c"), d_u=d_u, d_x2=d_x2, e_l_sb=e_l_sb))

                linked = [0]

                def link(ins):
                    linked[0] += 1
                    ins.then_inc(r_chain, 1)
                    dve.wait_ge(r_chain, linked[0])

                def over_e(t):
                    return t[:, :].unsqueeze(2).broadcast_to([P, NT, NE])

                rev = revio[:, :].unsqueeze(1).broadcast_to([P, NT, NE])
                dve.wait_ge(S["e_l_sb"], G)
                dve.wait_ge(s_late, 7 * 16)
                link(dve.tensor_reduce(rt["max"][:, :], logits[:, :, :], AX.X, ALU.max))
                dve.tensor_tensor(ex[:, :, :], logits[:, :, :], over_e(rt["max"]), ALU.subtract).then_inc(r_sub, 1)
                dve.memset(eligb[:, :], 0.0)
                dve.memset(rt["free"][:, :], 1.0)
                dve.memset(ones[:, :], 1.0)
                dve.memset(zb[:, :], 0.0)
                dve.wait_ge(r_exp, 1)
                link(dve.tensor_reduce(rt["sum"][:, :], prob[:, :, :], AX.X, ALU.add))
                link(dve.reciprocal(rt["inv"][:, :], rt["sum"][:, :]))
                link(dve.tensor_tensor(prob[:, :, :], prob[:, :, :], over_e(rt["inv"]), ALU.mult))
                for c, (m, at) in enumerate((("m1", "i1"), ("m2", "i2"))):
                    link(dve.tensor_reduce(rt[m][:, :], prob[:, :, :], AX.X, ALU.max))
                    link(dve.tensor_tensor(cand[:, :, :], prob[:, :, :], over_e(rt[m]), ALU.is_equal))
                    link(dve.tensor_tensor(cand[:, :, :], cand[:, :, :], rev, ALU.mult))
                    link(dve.tensor_reduce(rt[at][:, :], cand[:, :, :], AX.X, ALU.max))
                    link(dve.tensor_tensor(oh[c][:, :, :], rev, over_e(rt[at]), ALU.is_equal))
                    if c == 0:
                        link(dve.scalar_tensor_tensor(prob[:, :, :], oh[0][:, :, :], -2.0, prob[:, :, :], ALU.mult, ALU.add))
                link(dve.tensor_tensor(asg[:, :, :].rearrange("p e t -> p t e"), oh[0][:, :, :], oh[1][:, :, :], ALU.add))

                def route(e):
                    def step_link(ins, n):
                        ins.then_inc(r_step, 1)
                        dve.wait_ge(r_step, 5 * e + n)
                    step_link(dve.tensor_tensor(elig[:, :], asg[:, e, :], rt["free"][:, :], ALU.mult), 1)
                    dve.tensor_copy(eligb[:, 1:NT + 1], elig[:, :]).then_inc(r_elig, 1)
                    dve.wait_ge(r_cnt, e + 1)
                    step_link(dve.tensor_tensor_scan(rt["cum"][:, :], ones[:, :], bank[6][:, NT:2 * NT], 0.0,
                                                     ALU.mult, ALU.add), 2)
                    step_link(dve.tensor_tensor(rank[:, e, :], bank[6][:, 0:NT], rt["cum"][:, :], ALU.add), 3)
                    dve.scalar_tensor_tensor(keep[:, e, :], rank[:, e, :], float(CAP), elig[:, :], ALU.is_le, ALU.mult)
                    step_link(dve.scalar_tensor_tensor(rt["drop"][:, :], rank[:, e, :], float(CAP), elig[:, :],
                                                       ALU.is_gt, ALU.mult), 4)
                    step_link(dve.tensor_tensor(rt["free"][:, :], rt["free"][:, :], rt["drop"][:, :], ALU.subtract), 5)

                with dve.Fori(0, NE) as e:
                    route(e)

                link(dve.tensor_scalar(piece[:, :, :], rank[:, :, :], float(P), None, ALU.is_gt))
                link(dve.scalar_tensor_tensor(piece[:, :, :], rank[:, :, :], 2.0 * P, piece[:, :, :], ALU.is_gt, ALU.add))
                dve.scalar_tensor_tensor(slot[:, :, :], piece[:, :, :], -float(P), rank[:, :, :], ALU.mult, ALU.add)
                link(dve.tensor_tensor(colm[:, :, :], piece[:, :, :], col0[:, :].unsqueeze(2).broadcast_to([P, NE, NT]), ALU.add))
                link(dve.tensor_tensor(slot[:, :, :], slot[:, :, :], keep[:, :, :], ALU.mult))
                for c in range(2):
                    for src, dst in ((slot, slotc), (colm, colc)):
                        link(dve.tensor_tensor(cand[:, :, :], oh[c][:, :, :], src[:, :, :].rearrange("p e t -> p t e"), ALU.mult))
                        link(dve.tensor_reduce(dst[:, c * NT:(c + 1) * NT], cand[:, :, :], AX.X, ALU.add))
                link(dve.tensor_tensor(rt["sum"][:, :], rt["m1"][:, :], rt["m2"][:, :], ALU.add))
                link(dve.tensor_scalar(rt["sum"][:, :], rt["sum"][:, :], 1e-9, None, ALU.max))
                link(dve.reciprocal(rt["inv"][:, :], rt["sum"][:, :]))
                dve.tensor_tensor(wch[:, 0, :], rt["m1"][:, :], rt["inv"][:, :], ALU.mult)
                link(dve.tensor_tensor(wch[:, 1, :], rt["m2"][:, :], rt["inv"][:, :], ALU.mult))
                wv = wch[:, :, :].rearrange("p c t -> p (c t)")
                wr_ = wres[:, :, :].rearrange("p c t -> p (c t)")
                for c in range(2):
                    dve.tensor_copy(vals[:, c * NT:(c + 1) * NT, 0], iot[:, :])
                dve.tensor_copy(vals[:, :, 1], plus1[:, 0:1].broadcast_to([P, 2 * NT]))
                link(dve.tensor_copy(vals[:, :, 2], wv))
                link(dve.tensor_tensor(wr_, wv, vals[:, :, 2], ALU.subtract))
                link(dve.tensor_copy(vals[:, :, 3], wr_))
                link(dve.tensor_tensor(wv, wr_, vals[:, :, 3], ALU.subtract))
                link(dve.tensor_copy(vals[:, :, 4], wv))

                def chunk(n, i, q):
                    cs = bass.ds(n * CT, CT)
                    if q is not None:
                        dve.wait_ge(t_used, n - 1)
                    dve.tensor_tensor(ohp[i][:, :, :], slotc[:, cs].unsqueeze(2).broadcast_to([P, CT, P]),
                                      iop[:, :].unsqueeze(1).broadcast_to([P, CT, P]), ALU.is_equal)
                    dve.tensor_tensor(ohc[i][:, :, :], colc[:, cs].unsqueeze(2).broadcast_to([P, CT, NC]),
                                      ioc[:, :].unsqueeze(1).broadcast_to([P, CT, NC]), ALU.is_equal).then_inc(t_link, 1)
                    dve.wait_ge(t_link, n + 1)
                    dve.tensor_tensor(ohv[i][:, :, :, :], ohc[i][:, :, :].unsqueeze(2).broadcast_to([P, CT, NV, NC]),
                                      vals[:, cs, :].unsqueeze(3).broadcast_to([P, CT, NV, NC]), ALU.mult)\
                       .then_inc(t_chunk, 1)

                chunk(0, 0, None)
                chunk(1, 1, None)
                with dve.Fori(1, NCH // 2) as q:
                    chunk(2 * q, 0, q)
                    chunk(2 * q + 1, 1, q)

                dve.wait_ge(t_table, 1)
                link(dve.tensor_copy(tab[:, :, :].rearrange("p v c -> p (v c)"), bank[7][:, 0:NV * NC]))
                link(dve.scalar_tensor_tensor(tidx[:, :], tab[:, 0, :], float(P), tab[:, 1, :], ALU.mult, ALU.add))
                link(dve.tensor_scalar(tidx[:, :], tidx[:, :], -1.0, None, ALU.add))
                dve.tensor_scalar(gidx[:, :], tidx[:, :], 0.0, None, ALU.max)
                link(dve.tensor_scalar(temp[:, :], tab[:, 1, :], 0.0, None, ALU.is_equal))
                link(dve.tensor_tensor(temp[:, :], temp[:, :], spare[:, :], ALU.mult))
                link(dve.tensor_tensor(tw[:, :], tab[:, 3, :], tab[:, 4, :], ALU.add))
                link(dve.tensor_tensor(tw[:, :], tw[:, :], tab[:, 2, :], ALU.add))
                dve.tensor_tensor(sidx[:, :], tidx[:, :], temp[:, :], ALU.add).then_inc(t_index, 1)
                link(dve.tensor_scalar(rt["drop"][:, :], rt["free"][:, :], -1.0, 1.0, ALU.mult, ALU.add))

                def base(g):
                    dve.wait_ge(f_ysb, g + 1)
                    for j in range(J):
                        c = slice(j * D, (j + 1) * D)
                        last = dve.scalar_tensor_tensor(xs[:, g, :][:, c], mid[:, g, :][:, c], dropv[:, g, :][:, j:j + 1],
                                                        xs[:, g, :][:, c], ALU.mult, ALU.add)
                    last.then_inc(o_base, 1)

                dropv = rt["drop"][:, :].rearrange("p (g j) -> p g j", j=J)
                freev = rt["free"][:, :].rearrange("p (g j) -> p g j", j=J)

                def gathered_sb(e, i):
                    dve.wait_ge(x_t, e + 1)
                    if not (isinstance(e, int) and e < 2):
                        dve.wait_ge(x_h, FB * (e - 1))
                    dve.tensor_copy(xgT[i][:, :], bank[6][:, 0:CAP]).then_inc(x_tsb, 1)

                def weighted(e, i):
                    dve.wait_ge(x_y, e + 1)
                    if not (isinstance(e, int) and e < 2):
                        dve.wait_ge(x_add, 16 * NQ * (e - 1))
                    dve.tensor_tensor(ye[i][:, :, :], bank[4 + i][:, 0:NQ * D].rearrange("p (n d) -> p n d", n=NQ),
                                      tw[:, bass.ds(NQ * e, NQ)].unsqueeze(2).broadcast_to([P, NQ, D]), ALU.mult)\
                       .then_inc(x_ysb, 1)

                gathered_sb(0, 0)
                gathered_sb(1, 1)
                weighted(0, 0)
                base(0)
                gathered_sb(2, 0)
                weighted(1, 1)
                base(1)
                with dve.Fori(1, NE // 2 - 1) as q:
                    gathered_sb(2 * q + 1, 1)
                    weighted(2 * q, 0)
                    base(2 * q)
                    gathered_sb(2 * q + 2, 0)
                    weighted(2 * q + 1, 1)
                    base(2 * q + 1)
                gathered_sb(NE - 1, 1)
                weighted(NE - 2, 0)
                base(NE - 2)
                weighted(NE - 1, 1)
                base(NE - 1)

                def result(q, i):
                    dve.wait_ge(o_base, NF * q + i + 1)
                    dve.wait_ge(o_ld[i], 16 * (q + 1))
                    for j in range(J):
                        c = slice(j * D, (j + 1) * D)
                        last = dve.scalar_tensor_tensor(fin[i][:, c], fin[i][:, c], freev[:, NF * q + i, :][:, j:j + 1],
                                                        xs[:, NF * q + i, :][:, c], ALU.mult, ALU.add)
                    last.then_inc(o_fin, 1)

                with dve.Fori(0, NE // NF) as q:
                    for i in range(NF):
                        result(q, i)
                with dve.Fori(NE // NF, G // NF) as q:
                    for i in range(NF):
                        base(NF * q + i)
                        result(q, i)
    return nc


_INS = ["x", "ctx_1024", "L0_attn_W_Q", "L0_attn_W_K", "L0_attn_W_V", "L0_xattn_Wq", "L0_xattn_Wk", "L0_xattn_Wv",
        "L0_xattn_Wcq", "L0_xattn_Wck", "L0_xattn_Wcv", "L0_xattn_gamma", "L0_xattn_beta", "L0_xattn_W1",
        "L0_xattn_b1", "L0_ffn_Wr", "L0_ffn_W1", "L0_ffn_b1", "L0_ffn_W2", "L0_ffn_b2", "L0_ffn_fw1", "L0_ffn_fb1",
        "L0_ffn_fw2", "L0_ffn_fb2"]


def constants():
    import numpy as np
    n = np.arange(128)
    d = n[None, :] - n[:, None]
    return {
        "c_ident": np.eye(128, dtype=np.float32),
        "c_decay": np.where(d >= 0, np.power(np.float32(0.99), np.maximum(d, 0).astype(np.float32)), 0).astype(np.float32),
        "c_mask": np.where(d > 0, np.float32(-1e30), np.float32(0)).astype(np.float32),
        "c_tri": (d >= 0).astype(np.float32),
        "c_revio": np.tile(8 - np.arange(8, dtype=np.float32), (128, 1)),
        "c_col0": np.tile(3 * np.arange(8, dtype=np.float32), (128, 1)),
        "c_iop": np.tile(np.arange(1, 129, dtype=np.float32), (128, 1)),
        "c_ioc": np.tile(np.arange(24, dtype=np.float32), (128, 1)),
        "c_iot": np.tile(np.arange(64, dtype=np.float32), (128, 1)),
        "c_plus1": np.arange(1, 129, dtype=np.float32)[:, None],
        "c_spare": (8192 + 1 + np.arange(128 * 24, dtype=np.float32)).reshape(128, 24),
    }


def kernel(**inputs):
    import numpy as _np
    import concourse.bacc as _bacc
    from concourse import mybir as _mybir
    from concourse.bass_utils import run_bass_kernel_spmd as _run

    nc = _bacc.Bacc("TRN2", target_bir_lowering=False, num_devices=1)
    arrays, args = {}, {}
    for name, a in [(n, _np.ascontiguousarray(inputs[n])) for n in _INS] + list(constants().items()):
        arrays[f"in_{name}_dram"] = a
        args[name] = nc.dram_tensor(f"in_{name}_dram", a.shape, _mybir.dt.from_np(a.dtype), kind="ExternalInput").ap()
    out = nc.dram_tensor("out_0_dram", (64, 128, 128), _mybir.dt.float32, kind="ExternalOutput").ap()
    decoder_program(nc, args, out)
    r = _run(nc, [arrays], core_ids=[0])
    return r.results[0]["out_0_dram"]
```

```python
import concourse.bass as bass
from concourse import mybir
from contextlib import ExitStack

DVE_ORDER = (
    (0, "a_stats"), (4, "d_norm"), (0, "a_aggr"), (1, "a_x1"), (2, "b_rinv"), (1, "b_stats"), (5, "d_x2"),
    (0, "a_shift"), (1, "b_aggr"), (5, "e_stats"), (3, "c_max"), (5, "e_aggr"), (2, "b_a"), (4, "d_u"),
    (1, "b_norm"), (5, "e_shift"), (2, "c_stats"), (4, "d_stats2"), (2, "c_aggr"), (3, "c_rinv"),
    (4, "d_aggr2"), (3, "c_c"), (2, "c_shift"), (3, "d_stats"), (4, "d_shift2"), (3, "d_aggr"), (5, "e_l_sb"),
    (0, "a_p"), (1, "b_max"),
)
POOL_ORDER = (
    (0, "a_rstd"), (4, "d_h"), (1, "b_rstd"), (5, "e_rstd"), (3, "c_h"), (2, "c_rstd"), (4, "d_rstd2"),
    (3, "d_rstd"), (4, "d_t"),
)
PE_ORDER = (
    (2, "b_v"), (3, "c_ct"), (3, "c_g"), (4, "d_xt"), (2, "b_pt"), (3, "c_v"), (3, "c_s"), (2, "b_o"),
    (4, "d_f"), (0, "a_xt"), (3, "c_pt"), (0, "a_g"), (3, "c_o"), (1, "b_xt"), (0, "a_v"), (5, "e_xt"),
    (1, "b_g"), (0, "a_s"), (5, "e_l"), (1, "b_s"), (2, "c_xt"), (0, "a_o"),
)
ACT_ORDER = (
    (2, "b_exp"), (2, "b_v_sb"), (3, "c_ct_sb"), (3, "c_g_sb"), (4, "d_ht_sb"), (2, "b_pt_sb"), (3, "c_v_sb"),
    (0, "a_norm"), (3, "c_exp"), (0, "a_xt_sb"), (3, "c_pt_sb"), (5, "e_norm"), (1, "b_xt_sb"), (0, "a_g_sb"),
    (0, "a_v_sb"), (5, "e_xt_sb"), (1, "b_g_sb"), (2, "c_norm"), (4, "d_norm2"), (2, "c_ht_sb"),
)
SP_ORDER = ((5, "store_z"), (5, "store_zT"), (2, "load_ctx"))



def decoder_program(nc, A, out):
    fp32, bf16 = mybir.dt.float32, mybir.dt.bfloat16
    i32, u32 = mybir.dt.int32, mybir.dt.uint32
    ALU, ACT, AX = mybir.AluOpType, mybir.ActivationFunctionType, mybir.AxisListType

    NB, P, D = A["x"].shape
    SC = A["ctx_1024"].shape[1]
    J = 4
    G = NB // J
    W = J * D
    NT = NB
    NE, _, FF = A["L0_ffn_W1"].shape
    FB = FF // P
    CAP = 320
    SQ = (P, P, CAP - 2 * P)
    NQ = len(SQ)
    TOKENS = NB * P
    EPS1, EPS2 = 1e-5, 1e-3
    SCALE = float(D) ** -0.5
    NEG = -1e30
    LAGS = 1 + max(lag for o in (DVE_ORDER, POOL_ORDER, PE_ORDER, ACT_ORDER) for lag, _ in o)
    ACT_NORMS = ("a", "c", "u", "e",)

    x_v = A["x"].rearrange("(g j) t d -> t g j d", j=J)
    ctx_v = A["ctx_1024"].rearrange("(g j) s d -> s g j d", j=J)
    SPARE = NQ * P
    out_v = out[0:TOKENS, :].rearrange("(g j t) d -> t g j d", j=J, t=P)
    out_spare = out[TOKENS:TOKENS + SPARE, :].rearrange("(n p) d -> p n d", p=P)
    z_rows = nc.dram_tensor("z_rows", (TOKENS, D), fp32, kind="Internal").ap()
    z_rows_v = z_rows.rearrange("(g j t) d -> t g j d", j=J, t=P)

    with ExitStack() as ctx:
        def sb(name, shape, dt=fp32):
            return ctx.enter_context(nc.sbuf_tensor(name, shape, dt))

        def sem(name):
            return ctx.enter_context(nc.semaphore(name))

        xs = sb("xs", [P, G, W])
        mid = sb("mid", [P, G, W])
        zT = sb("zT", [P, G, W])
        cx = sb("cx", [SC, W])
        ident = sb("ident", [P, P])
        identb = sb("identb", [P, P], bf16)
        decay = sb("decay", [P, P])
        maskf = sb("maskf", [P, P])
        maskb = sb("maskb", [P, J, P], bf16)
        trif = sb("trif", [P, P])
        trib = sb("trib", [P, P], bf16)
        onesb = sb("onesb", [P, P], bf16)
        NW = 12
        wts = sb("wts", [P, NW, D])
        Wn = {n: wts[:, i, :] for i, n in enumerate(
            ["L0_attn_W_Q", "L0_attn_W_K", "L0_attn_W_V", "L0_xattn_Wq", "L0_xattn_Wk", "L0_xattn_Wv",
             "L0_xattn_Wcq", "L0_xattn_Wck", "L0_xattn_Wcv", "L0_xattn_W1"])}
        wtT = sb("wtT", [P, 6, D])
        mqk = sb("mqk", [P, 3, D])
        MA, MB, MC = (mqk[:, i, :] for i in range(3))
        gam = sb("gam", [P, D])
        bet = sb("bet", [P, D])
        gamT = sb("gamT", [P, 1])
        betT = sb("betT", [P, 1])
        negh = sb("negh", [P, J])
        wr = sb("wr", [P, NE])
        BR = 65
        ball = sb("ball", [BR, (2 + NE) * D], bf16)
        fw1 = sb("fw1", [P, FF])
        fw2 = sb("fw2", [P, FB, D])
        fb1 = sb("fb1", [P, FB])
        eb1 = sb("eb1", [P, NE, FB])
        zeros = sb("zeros", [P, W])

        st = {k: sb(f"st_{k}", [P, J, 6]) for k in ("a", "b", "c", "d", "u", "e")}
        mv = {k: sb(f"mv_{k}", [P, J, 2]) for k in ("a", "b", "c", "d", "u", "e")}
        ve = {k: sb(f"ve_{k}", [P, J]) for k in ("a", "b", "c", "d", "u", "e")}
        rs = {k: sb(f"rs_{k}", [P, J]) for k in ("a", "b", "c", "d", "u", "e")}
        shift = {k: sb(f"shift_{k}", [P, J]) for k in ACT_NORMS}
        work = sb("work", [P, 29, W])
        places = iter(range(29))

        def buffers(*keys):
            return {k: work[:, next(places), :] for k in keys}

        gq, va, pa = {}, {}, {}
        gq.update(buffers("c"))
        va.update(buffers("c"))
        pa.update(buffers("c"))
        pT = buffers("c")
        hres = buffers("c", "d")
        hmul = buffers("c", "d", "u")
        ud = work[:, next(places), :]
        td = work[:, next(places), :]
        nrm = buffers("u", "c", "d", "e")
        tr = buffers("c", "d", "e")
        nrm.update(buffers("a", "b"))
        tr.update(buffers("a", "b"))
        gq.update(buffers("a", "b"))
        va.update(buffers("a", "b"))
        pa.update(buffers("a", "b"))
        pT.update(buffers("b"))
        cT = sb("cT", [P, J * SC])
        nmax = {k: sb(f"nmax_{k}", [P, J]) for k in ("b", "c")}
        rsum = {k: sb(f"rsum_{k}", [P, J]) for k in ("b", "c")}
        rinv = {k: sb(f"rinv_{k}", [P, J]) for k in ("b", "c")}
        BW = (2 + NE) * D
        brow, bres = (work[0:BR, i:i + 3, :].rearrange("p a b -> p (a b)")[:, 0:BW] for i in (0, 3))
        bhi, bmid, blo = (work[0:BR, i:i + 2, :].rearrange("p a b -> p (a b)").bitcast(bf16)[:, 0:BW] for i in (6, 8, 10))
        logits = sb("logits", [P, NT, NE])

        rt = {k: sb(f"rt_{k}", [P, NT]) for k in ("max", "sum", "inv", "m1", "m2", "i1", "i2", "free", "cum", "drop")}
        def te(t):
            return t[:, :].rearrange("p (t e) -> p t e", e=NE)

        def et(t):
            return t[:, :].rearrange("p (e t) -> p e t", e=NE)

        ex, prob, cand = te(nrm["a"]), te(tr["a"]), te(gq["a"])
        oh = [te(va["a"]), te(pa["a"])]
        wch = sb("wch", [P, 2, NT])
        wres = sb("wres", [P, 2, NT])
        revio = sb("revio", [P, NE])
        col0 = sb("col0", [P, NE])
        asg = et(nrm["b"])
        elig = sb("elig", [P, NT])
        eligb = sb("eligb", [P, NT + 2], bf16)
        ones = sb("ones", [P, NT])
        rank = et(tr["b"])
        keep = et(gq["b"])
        piece, slot, colm = et(va["b"]), et(pa["b"]), et(pT["b"])
        NC = NE * NQ
        NV = 5
        CT = 8
        NCH = 2 * NT // CT
        slotc = sb("slotc", [P, 2 * NT])
        colc = sb("colc", [P, 2 * NT])
        vals = sb("vals", [P, 2 * NT, NV], bf16)
        iop = sb("iop", [P, P])
        ioc = sb("ioc", [P, NC])
        iot = sb("iot", [P, NT])
        plus1 = sb("plus1", [P, 1])
        spare = sb("spare", [P, NC])
        ohp = [work[:, 8 + i, :].bitcast(bf16).rearrange("p (t q) -> p t q", q=P) for i in range(2)]
        ohc = [sb(f"ohc{i}", [P, CT, NC], bf16) for i in range(2)]
        ohv = [work[:, 10 + i, :].bitcast(bf16)[:, 0:CT * NV * NC].rearrange("p (t v c) -> p t v c", v=NV, c=NC)
               for i in range(2)]
        zb = sb("zb", [P, P], bf16)
        tab = sb("tab", [P, NV, NC])
        tidx = sb("tidx", [P, NC])
        temp = sb("temp", [P, NC])
        tw = sb("tw", [P, NC])
        gidx = sb("gidx", [P, NC], u32)
        sidx = sb("sidx", [P, NC], u32)
        hf = [work[:, FB * i:FB * (i + 1), :] for i in range(2)]
        ew1 = [sb(f"ew1_{i}", [P, FF]) for i in range(2)]
        ew2 = [sb(f"ew2_{i}", [P, FB, D]) for i in range(2)]
        gi = [sb(f"gi{i}", [P, NQ], u32) for i in range(2)]
        si = [sb(f"si{i}", [P, NQ], u32) for i in range(2)]
        xg = [work[:, 12 + i, 0:NQ * D].rearrange("p (n d) -> p n d", d=D) for i in range(2)]
        ye = [work[:, 14 + i, 0:NQ * D].rearrange("p (n d) -> p n d", d=D) for i in range(2)]
        XR = 4
        xgT = work[:, 18:18 + NE, 0:CAP]

        bank = [ctx.enter_context(nc.psum_tensor(f"bank{i}", [P, W], fp32)) for i in range(8)]
        a0, a1, b0, b1, c0, c1, d0, e0 = bank

        names = set(n for o in (DVE_ORDER, POOL_ORDER, PE_ORDER, ACT_ORDER) for _, n in o)
        S = {n: sem(n) for n in sorted(names)}
        for n in ("a_veps", "b_veps", "c_veps", "d_veps", "d_veps2", "e_veps", "c_hmul", "d_hmul", "d_tmul"):
            S[n] = sem(n)
        s_wload, s_const, s_x0, s_x1, s_x2, s_ctx = (
            sem(n) for n in ("weights_loaded", "constants_loaded", "x_first", "x_next", "x_rest", "ctx_loaded"))
        s_brow = sem("bias_rows_loaded")
        s_prep_dve, s_prep_pe, s_prep_act = sem("prep_dve"), sem("prep_pe"), sem("prep_act")
        s_prep_pool = sem("prep_pool")
        s_zrow, s_zT = sem("z_rows_stored"), sem("zT_stored")
        s_fill = sem("acc_filled")
        s_late = sem("late_constants")
        s_fw = sem("fallback_weights")
        r_chain, r_sub, r_exp, r_elig, r_cnt, r_step = (
            sem(n) for n in ("route_chain", "route_shifted", "route_exp", "route_eligible", "route_counts", "route_rank"))
        t_chunk, t_used, t_table = (sem(n) for n in ("table_chunk", "table_chunk_used", "table_sum"))
        t_link, t_index = sem("table_chain"), sem("table_ready")
        n_hid, n_gelu, n_out, n_taken = (
            sem(n) for n in ("net_hidden", "net_gelu", "net_out", "net_out_taken"))
        x_w = [sem(f"x_weights{i}") for i in range(2)]
        x_g = [sem(f"x_gathered{i}") for i in range(2)]
        x_t, x_tsb, x_add, x_gi, x_si = (
            sem(n) for n in ("x_transposed", "x_transposed_sb", "x_added", "x_gather_rows", "x_add_rows"))
        o_base, o_st = sem("base_ready"), sem("base_stored")

        def r(t):
            return t[:, :].rearrange("p (j d) -> p j d", j=J)

        def later(g):
            return not (isinstance(g, int) and g == 0)

        def wait_apart(eng, semaphore, value):
            value = value if isinstance(value, int) else eng.to_reg(value)
            eng.wait_ge(s_const, NCONST)
            eng.wait_ge(semaphore, value)

        def ln_source(k, n, g):
            return ud[:, :] if n else {"a": xs, "b": xs, "c": mid, "d": mid, "e": xs}[k][:, g, :]

        def norm_free(eng, k, n, g):
            if later(g):
                for f in {"a": ("a_xt",), "b": ("b_xt", "b_a"), "c": ("c_xt", "c_hmul"), "d": ("d_xt", "d_hmul"),
                          "d2": ("d_tmul",), "e": ("e_xt",)}[k + n]:
                    eng.wait_ge(S[f], g)
                if k == "e":
                    eng.wait_ge(s_zrow, 16 * g)

        NWAIT = 10 * 16
        NCONST = 9 * 16

        with nc.Block() as block:
            def runs(eng, order, steps):
                def turn(t, filled):
                    for lag, name in order:
                        if filled or 0 <= t - lag < G:
                            steps[name](t - lag)
                for t in range(LAGS):
                    turn(t, False)
                with eng.Fori(LAGS, G) as t:
                    turn(t, True)
                for t in range(G, G + LAGS - 1):
                    turn(t, False)

            @block.sync
            def _(sp):
                for n, t in Wn.items():
                    sp.dma_start(t, A[n]).then_inc(s_wload, 16)
                sp.dma_start(ident[:, :], A["c_ident"]).then_inc(s_const, 16)
                sp.dma_start(xs[:, 0, :].rearrange("p (j d) -> p j d", j=J), x_v[:, 0, :, :]).then_inc(s_x0, 16)
                sp.dma_start(decay[:, :], A["c_decay"]).then_inc(s_const, 16)
                sp.dma_start(maskf[:, :], A["c_mask"]).then_inc(s_const, 16)
                sp.dma_start(trif[:, :], A["c_tri"]).then_inc(s_const, 16)
                sp.dma_start(gam[:, :], A["L0_xattn_gamma"].partition_broadcast(P)).then_inc(s_const, 16)
                sp.dma_start(bet[:, :], A["L0_xattn_beta"].partition_broadcast(P)).then_inc(s_const, 16)
                sp.dma_start(gamT[:, :], A["L0_xattn_gamma"].unsqueeze(1)).then_inc(s_const, 16)
                sp.dma_start(betT[:, :], A["L0_xattn_beta"].unsqueeze(1)).then_inc(s_const, 16)
                sp.dma_start(wr[:, :], A["L0_ffn_Wr"]).then_inc(s_const, 16)
                sp.wait_ge(s_prep_pool, 1)
                for k in (0, 32, 64):
                    sp.dma_start(brow[k:k + 1, 0:D], A["L0_xattn_b1"].unsqueeze(0)).then_inc(s_brow, 16)
                    sp.dma_start(brow[k:k + 1, D:2 * D], A["L0_ffn_fb2"].unsqueeze(0)).then_inc(s_brow, 16)
                    sp.dma_start(brow[k:k + 1, 2 * D:(2 + NE) * D],
                                 A["L0_ffn_b2"].rearrange("e d -> (e d)").unsqueeze(0)).then_inc(s_brow, 16)
                sp.dma_start(revio[:, :], A["c_revio"]).then_inc(s_late, 16)
                sp.dma_start(col0[:, :], A["c_col0"]).then_inc(s_late, 16)
                sp.dma_start(iop[:, :], A["c_iop"]).then_inc(s_late, 16)
                sp.dma_start(ioc[:, :], A["c_ioc"]).then_inc(s_late, 16)
                sp.dma_start(iot[:, :], A["c_iot"]).then_inc(s_late, 16)
                sp.dma_start(plus1[:, :], A["c_plus1"]).then_inc(s_late, 16)
                sp.dma_start(spare[:, :], A["c_spare"]).then_inc(s_late, 16)
                sp.dma_start(fw1[:, :], A["L0_ffn_fw1"]).then_inc(s_fw, 16)
                sp.dma_start(fw2[:, :, :], A["L0_ffn_fw2"].rearrange("(k p) d -> p k d", p=P)).then_inc(s_fw, 16)
                with nc.allow_non_contiguous_dma("bias columns, once"):
                    sp.dma_start(fb1[:, :], A["L0_ffn_fb1"].rearrange("(k p) -> p k", p=P)).then_inc(s_fw, 16)
                    for e in range(NE):
                        sp.dma_start(eb1[:, e, :], A["L0_ffn_b1"][e, :].rearrange("(k p) -> p k", p=P)).then_inc(s_fw, 16)
                for g in range(1, 4):
                    sp.dma_start(xs[:, g, :].rearrange("p (j d) -> p j d", j=J), x_v[:, g, :, :]).then_inc(s_x1, 16)
                sp.dma_start(xs[:, 4:G, :].rearrange("p g (j d) -> p (g j) d", j=J),
                             x_v[:, 4:G].rearrange("t g j d -> t (g j) d")).then_inc(s_x2, 16)

                def load_ctx(g):
                    if later(g):
                        sp.wait_ge(S["c_ct"], g)
                    sp.dma_start(cx[:, :].rearrange("s (j d) -> s j d", j=J), ctx_v[:, g, :, :]).then_inc(s_ctx, 16)

                def store_z(g):
                    sp.wait_ge(S["e_norm"], g + 1)
                    sp.dma_start(z_rows_v[:, g, :, :], r(nrm["e"])).then_inc(s_zrow, 16)

                def store_zT(g):
                    sp.wait_ge(S["e_xt_sb"], g + 1)
                    sp.dma_start(zT[:, g, :], tr["e"][:, :]).then_inc(s_zT, 16)

                sp.wait_ge(s_prep_pool, 2)
                sp.dma_start(out_spare, zeros[:, 0:NQ * D].rearrange("p (n d) -> p n d", n=NQ)).then_inc(s_fill, 16)

                def load_expert(e, i):
                    if not isinstance(e, int):
                        sp.wait_ge(n_out, G + e - 1)
                    sp.dma_start(ew1[i][:, :], A["L0_ffn_W1"][e, :, :]).then_inc(x_w[i], 16)
                    sp.dma_start(ew2[i][:, :, :], A["L0_ffn_W2"][e, :, :].rearrange("(k p) d -> p k d", p=P))\
                      .then_inc(x_w[i], 16)

                load_expert(0, 0)
                load_expert(1, 1)
                runs(sp, SP_ORDER, dict(load_ctx=load_ctx, store_z=store_z, store_zT=store_zT))
                with sp.Fori(0, G) as g:
                    sp.wait_ge(o_base, g + 1)
                    sp.dma_start(out_v[:, g, :, :], xs[:, g, :].rearrange("p (j d) -> p j d", j=J)).then_inc(o_st, 16)
                with sp.Fori(1, NE // 2) as q:
                    for i in range(2):
                        load_expert(2 * q + i, i)

            @block.tensor
            def _(pe):
                pe.wait_ge(s_wload, NWAIT)
                pe.wait_ge(s_const, NCONST)
                keys = ["L0_attn_W_Q", "L0_attn_W_K", "L0_xattn_Wq", "L0_xattn_Wk", "L0_xattn_Wcq", "L0_xattn_Wck"]
                for i, n in enumerate(keys):
                    last = pe.transpose(bank[i // 4][:, (i % 4) * D:(i % 4 + 1) * D], Wn[n], ident[:, :])
                last.then_inc(s_prep_pe, 1)
                pe.wait_ge(s_prep_act, 2)
                for k in range(3):
                    last = pe.matmul(bank[2][:, k * D:(k + 1) * D], wtT[:, 2 * k, :], wtT[:, 2 * k + 1, :],
                                     start=True, stop=True)
                last.then_inc(s_prep_pe, 1)
                pe.wait_ge(s_prep_act, 3)
                pe.wait_ge(s_prep_dve, 6)

                def transposed(k, dst):
                    def step(g):
                        done = {"a": "a_norm", "b": "b_norm", "c": "c_norm", "d": "d_norm", "e": "e_norm"}[k]
                        free = {"a": "a_x1", "b": "b_pt_sb", "c": "c_c", "d": "d_u", "e": "e_l_sb"}[k]
                        pe.wait_ge(S[done], g + 1)
                        if later(g):
                            pe.wait_ge(S[free], g)
                        for j in range(J):
                            last = pe.transpose(dst[:, j * D:(j + 1) * D], nrm[k][:, j * D:(j + 1) * D], ident[:, :])
                        last.then_inc(S[f"{k}_xt"], 1)
                    return step

                def a_g(g):
                    pe.wait_ge(S["a_xt_sb"], g + 1)
                    if later(g):
                        pe.wait_ge(S["a_p"], g)
                    pe.matmul(a1[:, :], MA, tr["a"][:, :], start=True, stop=True).then_inc(S["a_g"], 1)

                def a_v(g):
                    pe.wait_ge(S["a_xt_sb"], g + 1)
                    for j in range(J):
                        c = slice(j * D, (j + 1) * D)
                        last = pe.matmul(a0[:, c], tr["a"][:, c], Wn["L0_attn_W_V"], start=True, stop=True)
                    last.then_inc(S["a_v"], 1)

                def a_s(g):
                    pe.wait_ge(S["a_g_sb"], g + 1)
                    for j in range(J):
                        c = slice(j * D, (j + 1) * D)
                        last = pe.matmul(a1[:, c], tr["a"][:, c], gq["a"][:, c], start=True, stop=True)
                    last.then_inc(S["a_s"], 1)

                def a_o(g):
                    pe.wait_ge(S["a_p"], g + 1)
                    pe.wait_ge(S["a_v_sb"], g + 1)
                    for j in range(J):
                        c = slice(j * D, (j + 1) * D)
                        last = pe.matmul(a0[:, c], va["a"][:, c], pa["a"][:, c], start=True, stop=True)
                    last.then_inc(S["a_o"], 1)

                def b_g(g):
                    pe.wait_ge(S["b_xt_sb"], g + 1)
                    if later(g):
                        pe.wait_ge(S["b_a"], g)
                    pe.matmul(b1[:, :], MB, tr["b"][:, :], start=True, stop=True).then_inc(S["b_g"], 1)

                def b_v(g):
                    pe.wait_ge(S["b_xt_sb"], g + 1)
                    for j in range(J):
                        c = slice(j * D, (j + 1) * D)
                        last = pe.matmul(b0[:, c], tr["b"][:, c], Wn["L0_xattn_Wv"], start=True, stop=True)
                    last.then_inc(S["b_v"], 1)

                def b_s(g):
                    pe.wait_ge(S["b_g_sb"], g + 1)
                    pe.matmul(b1[:, :], identb[:, :], maskb[:, :, :].rearrange("p j d -> p (j d)"),
                              start=True, stop=False, skip_group_check=True)
                    for j in range(J):
                        c = slice(j * D, (j + 1) * D)
                        last = pe.matmul(b1[:, c], gq["b"][:, c], tr["b"][:, c], start=False, stop=(j == J - 1),
                                         skip_group_check=True)
                    last.then_inc(S["b_s"], 1)

                def b_pt(g):
                    pe.wait_ge(S["b_exp"], g + 1)
                    pe.wait_ge(S["b_v_sb"], g + 1)
                    for j in range(J):
                        c = slice(j * D, (j + 1) * D)
                        last = pe.transpose(b0[:, c], pa["b"][:, c], ident[:, :])
                    last.then_inc(S["b_pt"], 1)

                def b_o(g):
                    pe.wait_ge(S["b_pt_sb"], g + 1)
                    for j in range(J):
                        c = slice(j * D, (j + 1) * D)
                        last = pe.matmul(b1[:, c], pT["b"][:, c], va["b"][:, c], start=True, stop=True)
                    last.then_inc(S["b_o"], 1)

                def c_ct(g):
                    if later(g):
                        pe.wait_ge(S["c_pt_sb"], g)
                    pe.wait_ge(s_ctx, 16 * (g + 1))
                    for j in range(J):
                        last = pe.transpose(c1[:, j * SC:(j + 1) * SC], cx[:, j * D:(j + 1) * D], ident[0:SC, 0:SC])
                    last.then_inc(S["c_ct"], 1)

                def c_v(g):
                    pe.wait_ge(S["c_ct_sb"], g + 1)
                    for j in range(J):
                        last = pe.matmul(c1[0:SC, j * D:(j + 1) * D], cT[:, j * SC:(j + 1) * SC],
                                         Wn["L0_xattn_Wcv"], start=True, stop=True)
                    last.then_inc(S["c_v"], 1)

                def c_g(g):
                    pe.wait_ge(S["c_ht_sb"], g + 1)
                    pe.matmul(c0[:, :], MC, tr["c"][:, :], start=True, stop=True).then_inc(S["c_g"], 1)

                def c_s(g):
                    pe.wait_ge(S["c_g_sb"], g + 1)
                    pe.wait_ge(S["c_ct_sb"], g + 1)
                    for j in range(J):
                        last = pe.matmul(c0[:, j * SC:(j + 1) * SC], gq["c"][:, j * D:(j + 1) * D],
                                         cT[:, j * SC:(j + 1) * SC], start=True, stop=True)
                    last.then_inc(S["c_s"], 1)

                def c_pt(g):
                    pe.wait_ge(S["c_exp"], g + 1)
                    pe.wait_ge(S["c_v_sb"], g + 1)
                    for j in range(J):
                        last = pe.transpose(c1[0:SC, j * D:(j + 1) * D], pa["c"][:, j * SC:(j + 1) * SC], ident[:, :])
                    last.then_inc(S["c_pt"], 1)

                def c_o(g):
                    pe.wait_ge(S["c_pt_sb"], g + 1)
                    for j in range(J):
                        c = slice(j * D, (j + 1) * D)
                        last = pe.matmul(c0[:, c], pT["c"][0:SC, c], va["c"][0:SC, c], start=True, stop=True)
                    last.then_inc(S["c_o"], 1)

                def d_f(g):
                    pe.wait_ge(S["d_ht_sb"], g + 1)
                    pe.matmul(d0[:, :], onesb[0:BR, :], ball[:, 0:D].unsqueeze(1).broadcast_to([BR, J, D]),
                              start=True, stop=False, skip_group_check=True)
                    for j in range(J):
                        c = slice(j * D, (j + 1) * D)
                        last = pe.matmul(d0[:, c], tr["d"][:, c], Wn["L0_xattn_W1"], start=False, stop=(j == J - 1),
                                         skip_group_check=True)
                    last.then_inc(S["d_f"], 1)

                def e_l(g):
                    pe.wait_ge(S["e_xt_sb"], g + 1)
                    for j in range(J):
                        last = pe.matmul(e0[:, j * NE:(j + 1) * NE], tr["e"][:, j * D:(j + 1) * D], wr[:, :],
                                         start=True, stop=True)
                    last.then_inc(S["e_l"], 1)

                runs(pe, PE_ORDER, dict(
                    a_xt=transposed("a", a0), b_xt=transposed("b", b0), c_xt=transposed("c", c0),
                    d_xt=transposed("d", d0), e_xt=transposed("e", e0),
                    a_g=a_g, a_v=a_v, a_s=a_s, a_o=a_o, b_g=b_g, b_v=b_v, b_s=b_s, b_pt=b_pt, b_o=b_o,
                    c_ct=c_ct, c_v=c_v, c_g=c_g, c_s=c_s, c_pt=c_pt, c_o=c_o, d_f=d_f, e_l=e_l))

                pe.wait_ge(S["e_l_sb"], G)
                pe.wait_ge(s_fw, (3 + NE) * 16)
                pe.wait_ge(s_zT, 16 * G)

                def f_hidden(g, blocks=range(FB)):
                    for k in blocks:
                        if not (isinstance(g, int) and g == 0):
                            pe.wait_ge(n_gelu, FB * (g - 1) + k + 1)
                        pe.matmul(bank[k][:, :], fw1[:, k * P:(k + 1) * P], zT[:, g, :], start=True, stop=True)\
                          .then_inc(n_hid, 1)

                def f_out(g, i, tiles=range(J)):
                    y = bank[4 + i]
                    if 0 in tiles:
                        pe.wait_ge(n_gelu, FB * (g + 1))
                        if not (isinstance(g, int) and g < 2):
                            pe.wait_ge(n_taken, g - 1)
                        pe.matmul(y[:, :], onesb[0:BR, :], ball[:, D:2 * D].unsqueeze(1).broadcast_to([BR, J, D]),
                                  start=True, stop=False, skip_group_check=True)
                    for j in tiles:
                        for k in range(FB):
                            last = pe.matmul(y[:, j * D:(j + 1) * D], hf[i][:, k, j * P:(j + 1) * P], fw2[:, k, :],
                                             start=False, stop=(j == J - 1 and k == FB - 1), skip_group_check=True)
                    if J - 1 in tiles:
                        last.then_inc(n_out, 1)

                def f_unit(g, i, between=()):
                    parts = (lambda: f_hidden(g + 1, (0, 1)), lambda: f_hidden(g + 1, (2, 3)),
                             lambda: f_out(g, i, (0, 1)), lambda: f_out(g, i, (2, 3)))
                    for n, part in enumerate(parts):
                        part()
                        if n < len(between):
                            between[n]()

                def route(e):
                    pe.wait_ge(r_elig, e + 1)
                    pe.matmul(bank[6][:, 0:NT], trib[:, :], eligb[:, 1:NT + 1], start=True, stop=True)
                    pe.matmul(bank[6][:, NT:2 * NT], onesb[:, :], eligb[:, 0:NT], start=True, stop=True)\
                      .then_inc(r_cnt, 1)

                def table(n, i):
                    pe.wait_ge(t_chunk, n + 1)
                    for t in range(CT):
                        last = pe.matmul(bank[7][:, 0:NV * NC], ohp[i][:, t, :],
                                         ohv[i][:, t, :, :].rearrange("p v c -> p (v c)"), start=False, stop=False,
                                         skip_group_check=True)
                    last.then_inc(t_used, 1)

                def table_edge(start):
                    return pe.matmul(bank[7][:, 0:NV * NC], zb[:, :], ohv_zero, start=start, stop=not start,
                                     skip_group_check=True)

                ohv_zero = zb[:, 0:NV * NC]

                def x_hidden(e, i, pair):
                    pe.wait_ge(x_tsb, e + 1)
                    pe.wait_ge(x_w[i], 32 * (pair + 1))
                    for k in range(FB):
                        pe.wait_ge(n_gelu, FB * (G + e - 1) + k + 1)
                        pe.matmul(bank[k][:, 0:CAP], ew1[i][:, k * P:(k + 1) * P],
                                  xgT[:, e, :],
                                  start=True, stop=True).then_inc(n_hid, 1)

                def x_out(e, i):
                    y = bank[4 + i]
                    pe.wait_ge(n_gelu, FB * (G + e + 1))
                    pe.wait_ge(n_taken, G + e - 1)
                    pe.matmul(y[:, 0:NQ * D], onesb[0:BR, :],
                              ball[:, bass.ds((2 + e) * D, D)].unsqueeze(1).broadcast_to([BR, NQ, D]),
                              start=True, stop=False, skip_group_check=True)
                    for n, w in enumerate(SQ):
                        for k in range(FB):
                            last = pe.matmul(y[0:w, n * D:(n + 1) * D], hf[i][:, k, n * P:n * P + w], ew2[i][:, k, :],
                                             start=False, stop=(n == NQ - 1 and k == FB - 1), skip_group_check=True)
                    last.then_inc(n_out, 1)

                def x_transpose(e, i, pair):
                    pe.wait_ge(x_g[i], 16 * NQ * (pair + 1))
                    if not (isinstance(e, int) and e < 2):
                        pe.wait_ge(x_tsb, e - 1)
                    for n, w in enumerate(SQ):
                        last = pe.transpose(bank[6 + i][:, n * P:n * P + w], xg[i][0:w, n, :], ident[0:w, 0:w])
                    last.then_inc(x_t, 1)

                f_hidden(0)
                f_unit(0, 0)
                f_unit(1, 1)
                f_unit(2, 0)
                for g in (3, 4):
                    f_unit(g, g % 2, [lambda n=n: route(4 * (g - 3) + n) for n in range(4)])
                f_unit(5, 1)
                table_edge(True)
                with pe.Fori(0, 2) as q:
                    for i in range(2):
                        f_unit(6 + 2 * q + i, i, [lambda n=n: table(6 * q + 3 * i + n, (3 * i + n) % 2) for n in range(3)])
                f_unit(10, 0, [lambda n=n: table(12 + n, n % 2) for n in range(3)])
                f_unit(11, 1, [lambda: table(15, 1), lambda: table_edge(False).then_inc(t_table, 1)])
                f_unit(12, 0)
                f_unit(13, 1)
                f_unit(14, 0, [lambda n=n: x_transpose(n, n % 2, n // 2) for n in range(4)])
                x_hidden(0, 0, 0)
                f_out(G - 1, 1)
                with pe.Fori(0, (NE - XR) // 2) as q:
                    x_transpose(2 * q + XR, 0, q + XR // 2)
                    x_hidden(2 * q + 1, 1, q)
                    x_out(2 * q, 0)
                    x_transpose(2 * q + XR + 1, 1, q + XR // 2)
                    x_hidden(2 * q + 2, 0, q + 1)
                    x_out(2 * q + 1, 1)
                for e in range(NE - XR, NE - 1):
                    x_hidden(e + 1, (e + 1) % 2, (e + 1) // 2)
                    x_out(e, e % 2)
                x_out(NE - 1, 1)

            @block.scalar
            def _(act):
                act.wait_ge(s_prep_pe, 1)
                for i in range(6):
                    last = act.activation(wtT[:, i, :], bank[i // 4][:, (i % 4) * D:(i % 4 + 1) * D], ACT.Copy)
                last.then_inc(s_prep_act, 2)
                act.wait_ge(s_prep_pe, 2)
                act.activation(mqk[:, :, :].rearrange("p k d -> p (k d)"), bank[2][:, 0:3 * D], ACT.Copy)\
                   .then_inc(s_prep_act, 1)

                def copied(dst, src, done, name, scale=1.0, free=None):
                    def step(g):
                        act.wait_ge(S[done], g + 1)
                        if free is not None and later(g):
                            act.wait_ge(S[free], g)
                        act.activation(dst, src, ACT.Copy, scale=scale).then_inc(S[name], 1)
                    return step

                def affine(k, src):
                    def step(g):
                        act.wait_ge(S[f"{k}_xt"], g + 1)
                        act.wait_ge(s_const, NCONST)
                        act.activation(tr[k][:, :], src[:, :], ACT.Identity, scale=gamT[:, :], bias=betT[:, :])\
                           .then_inc(S[f"{k}_ht_sb"], 1)
                    return step

                def exponent(k, src, width):
                    def step(g):
                        act.wait_ge(S[f"{k}_max"], g + 1)
                        if later(g):
                            act.wait_ge(S[f"{k}_pt"], g)
                            act.wait_ge(S[f"{k}_rinv"], g)
                        for j in range(J):
                            c = slice(j * width, (j + 1) * width)
                            last = act.activation(pa[k][:, c], src[:, c], ACT.Exp, bias=nmax[k][:, j:j + 1],
                                                  accum_out=rsum[k][:, j:j + 1])
                        last.then_inc(S[f"{k}_exp"], 1)
                    return step

                def norm(k, n):
                    u = "u" if n else k
                    def step(g):
                        act.wait_ge(S[f"{k}_shift{n}"], g + 1)
                        norm_free(act, k, n, g)
                        src = ln_source(k, n, g)
                        for j in range(J):
                            c = slice(j * D, (j + 1) * D)
                            last = act.activation(nrm[u][:, c], src[:, c], ACT.Identity, scale=rs[u][:, j:j + 1],
                                                  bias=shift[u][:, j:j + 1])
                        last.then_inc(S[f"{k}_norm{n}"], 1)
                    return step

                def e_xt_sb(g):
                    act.wait_ge(S["e_xt"], g + 1)
                    if later(g):
                        act.wait_ge(S["e_l"], g)
                        act.wait_ge(s_zT, 16 * g)
                    act.activation(tr["e"][:, :], e0[:, :], ACT.Copy).then_inc(S["e_xt_sb"], 1)

                runs(act, ACT_ORDER, dict(
                    **{f"{k}_norm{n}": norm(k, n) for k, n in (*((k, "") for k in "abcde"), ("d", "2"))},
                    a_xt_sb=copied(tr["a"][:, :], a0[:, :], "a_xt", "a_xt_sb"),
                    a_g_sb=copied(gq["a"][:, :], a1[:, :], "a_g", "a_g_sb"),
                    a_v_sb=copied(va["a"][:, :], a0[:, :], "a_v", "a_v_sb"),
                    b_xt_sb=copied(tr["b"][:, :], b0[:, :], "b_xt", "b_xt_sb"),
                    b_g_sb=copied(gq["b"][:, :], b1[:, :], "b_g", "b_g_sb", scale=SCALE),
                    b_v_sb=copied(va["b"][:, :], b0[:, :], "b_v", "b_v_sb", free="b_o"),
                    b_exp=exponent("b", b1, D),
                    b_pt_sb=copied(pT["b"][:, :], b0[:, :], "b_pt", "b_pt_sb"),
                    c_ht_sb=affine("c", c0),
                    c_g_sb=copied(gq["c"][:, :], c0[:, :], "c_g", "c_g_sb", scale=SCALE),
                    c_ct_sb=copied(cT[:, :], c1[:, 0:J * SC], "c_ct", "c_ct_sb", free="c_s"),
                    c_v_sb=copied(va["c"][0:SC, :], c1[0:SC, :], "c_v", "c_v_sb", free="c_o"),
                    c_exp=exponent("c", c0, SC),
                    c_pt_sb=copied(pT["c"][0:SC, :], c1[0:SC, :], "c_pt", "c_pt_sb"),
                    d_ht_sb=affine("d", d0),
                    e_xt_sb=e_xt_sb))

                act.wait_ge(r_sub, 1)
                act.activation(prob[:, :, :], ex[:, :, :], ACT.Exp).then_inc(r_exp, 1)
                act.wait_ge(s_fw, (3 + NE) * 16)

                def gelu(u, i, bias, width):
                    for k in range(FB):
                        act.wait_ge(n_hid, FB * u + k + 1)
                        if k == 0 and not (isinstance(u, int) and u < 2):
                            act.wait_ge(n_out, u - 1)
                        act.activation(hf[i][:, k, 0:width], bank[k][:, 0:width], ACT.Gelu, bias=bias(k))\
                           .then_inc(n_gelu, 1)

                def f_act(g, i):
                    gelu(g, i, lambda k: fb1[:, k:k + 1], W)

                def x_act(e, i):
                    gelu(G + e, i, lambda k: eb1[:, e, k:k + 1], CAP)

                def f_out_sb(g, i):
                    act.wait_ge(n_out, g + 1)
                    act.activation(mid[:, g, :], bank[4 + i][:, :], ACT.Copy).then_inc(n_taken, 1)

                f_act(0, 0)
                f_act(1, 1)
                f_out_sb(0, 0)
                with act.Fori(1, G // 2) as q:
                    f_act(2 * q, 0)
                    f_out_sb(2 * q - 1, 1)
                    f_act(2 * q + 1, 1)
                    f_out_sb(2 * q, 0)
                x_act(0, 0)
                f_out_sb(G - 1, 1)
                x_act(1, 1)
                with act.Fori(1, NE // 2) as q:
                    x_act(2 * q, 0)
                    x_act(2 * q + 1, 1)

            @block.gpsimd
            def _(pool):
                pool.memset(brow[:, :], 0.0).then_inc(s_prep_pool, 1)
                pool.memset(negh[:, :], -0.5)
                pool.memset(zeros[:, :], 0.0).then_inc(s_prep_pool, 1)
                pool.wait_ge(s_prep_pool, 2)
                pool.wait_ge(s_const, NCONST)

                def root(k, n, eps):
                    u = "u" if n else k
                    def step(g):
                        wait_apart(pool, S[f"{k}_aggr{n}"], g + 1)
                        pool.tensor_scalar(ve[u][:, :], mv[u][:, :, 1], eps, None, ALU.add).then_inc(S[f"{k}_veps{n}"], 1)
                        pool.wait_ge(S[f"{k}_veps{n}"], g + 1)
                        if later(g):
                            pool.wait_ge(S[f"{k}_norm{n}"], g)
                        pool.tensor_tensor(rs[u][:, :], ve[u][:, :], negh[:, :], ALU.pow).then_inc(S[f"{k}_rstd{n}"], 1)
                    return step

                def gamma_beta(src, mul, dst, done, mid_name, name, free):
                    def step(g):
                        pool.wait_ge(S[done], g + 1)
                        pool.tensor_tensor(r(mul), r(src), gam[:, :].unsqueeze(1).broadcast_to([P, J, D]), ALU.mult)\
                            .then_inc(S[mid_name], 1)
                        pool.wait_ge(S[mid_name], g + 1)
                        if later(g):
                            pool.wait_ge(S[free], g)
                        pool.tensor_tensor(r(dst), r(mul), bet[:, :].unsqueeze(1).broadcast_to([P, J, D]), ALU.add)\
                            .then_inc(S[name], 1)
                    return step

                runs(pool, POOL_ORDER, dict(
                    a_rstd=root("a", "", EPS1), b_rstd=root("b", "", EPS1), c_rstd=root("c", "", EPS2),
                    d_rstd=root("d", "", EPS2), d_rstd2=root("d", "2", EPS2), e_rstd=root("e", "", EPS1),
                    c_h=gamma_beta(nrm["c"], hmul["c"], hres["c"], "c_norm", "c_hmul", "c_h", "c_c"),
                    d_h=gamma_beta(nrm["d"], hmul["d"], hres["d"], "d_norm", "d_hmul", "d_h", "d_u"),
                    d_t=gamma_beta(nrm["u"], hmul["u"], td, "d_norm2", "d_tmul", "d_t", "d_x2")))

                pool.wait_ge(t_index, 1)
                pool.wait_ge(s_zrow, 16 * G)

                def gather(e, i):
                    if not (isinstance(e, int) and e < 2):
                        pool.wait_ge(x_t, e - 1)
                    pool.tensor_copy(gi[i][:, :], gidx[:, bass.ds(NQ * e, NQ)]).then_inc(x_gi, 1)
                    wait_apart(pool, x_gi, e + 1)
                    for n, w in enumerate(SQ):
                        pool.indirect_dma_start(xg[i][0:w, n, :], None, z_rows,
                                                bass.IndirectOffsetOnAxis(ap=gi[i][0:w, n:n + 1], axis=0))\
                            .then_inc(x_g[i], 16)

                def add(e, i):
                    if not (isinstance(e, int) and e == 0):
                        pool.wait_ge(x_add, 16 * NQ * e)
                    pool.tensor_copy(si[i][:, :], sidx[:, bass.ds(NQ * e, NQ)]).then_inc(x_si, 1)
                    wait_apart(pool, x_si, e + 1)
                    wait_apart(pool, n_taken, G + e + 1)
                    for n, w in enumerate(SQ):
                        pool.indirect_dma_start(out, bass.IndirectOffsetOnAxis(ap=si[i][0:w, n:n + 1], axis=0),
                                                ye[i][0:w, n, :], None, compute_op=ALU.add).then_inc(x_add, 16)

                gather(0, 0)
                gather(1, 1)
                with pool.Fori(1, NE // 2 - 1) as q:
                    gather(2 * q, 0)
                    gather(2 * q + 1, 1)
                pool.wait_ge(o_st, 16 * G)
                pool.wait_ge(s_fill, 16)
                add(0, 0)
                gather(NE - 2, 0)
                add(1, 1)
                gather(NE - 1, 1)
                with pool.Fori(1, NE // 2) as q:
                    add(2 * q, 0)
                    add(2 * q + 1, 1)
                pool.wait_ge(x_add, 16 * NQ * NE)

            @block.vector
            def _(dve):
                dve.wait_ge(s_const, NCONST)
                dve.tensor_copy(maskb[:, :, :], maskf[:, :].unsqueeze(1).broadcast_to([P, J, P]))
                dve.tensor_copy(trib[:, :], trif[:, :])
                dve.tensor_copy(identb[:, :], ident[:, :])
                dve.memset(onesb[:, :], 1.0).then_inc(s_prep_dve, 1)
                dve.memset(ball[:, :], 0.0)
                dve.wait_ge(s_brow, 9 * 16)
                dve.tensor_copy(bhi[:, :], brow[:, :]).then_inc(s_prep_dve, 1)
                dve.wait_ge(s_prep_dve, 2)
                dve.tensor_tensor(bres[:, :], brow[:, :], bhi[:, :], ALU.subtract).then_inc(s_prep_dve, 1)
                dve.wait_ge(s_prep_dve, 3)
                dve.tensor_copy(bmid[:, :], bres[:, :]).then_inc(s_prep_dve, 1)
                dve.wait_ge(s_prep_dve, 4)
                dve.tensor_tensor(blo[:, :], bres[:, :], bmid[:, :], ALU.subtract)
                dve.tensor_copy(ball[0:1, :], bhi[0:1, :])
                dve.tensor_copy(ball[32:33, :], bmid[32:33, :]).then_inc(s_prep_dve, 1)
                dve.wait_ge(s_prep_dve, 5)
                dve.tensor_copy(ball[64:65, :], blo[64:65, :]).then_inc(s_prep_dve, 1)

                def stats(k, n, wait):
                    u = "u" if n else k
                    def step(g):
                        if k == "a" and isinstance(g, int):
                            if g == 0:
                                dve.wait_ge(s_x0, 16)
                            if g == 1:
                                dve.wait_ge(s_x1, 3 * 16)
                            if g == 4:
                                dve.wait_ge(s_x2, 16)
                        if wait:
                            wait_apart(dve, S[wait], g + 1)
                        src = ln_source(k, n, g)
                        for j in range(J):
                            last = dve.bn_stats(st[u][:, j, :], src[:, j * D:(j + 1) * D])
                        last.then_inc(S[f"{k}_stats{n}"], 1)
                    return step

                def aggr(k, n):
                    u = "u" if n else k
                    def step(g):
                        wait_apart(dve, S[f"{k}_stats{n}"], g + 1)
                        if later(g):
                            dve.wait_ge(S[f"{k}_norm{n}"], g)
                        for j in range(J):
                            last = dve.bn_aggr(mv[u][:, j, :], st[u][:, j, :])
                        last.then_inc(S[f"{k}_aggr{n}"], 1)
                    return step

                def shifted(k, n):
                    u = "u" if n else k
                    def step(g):
                        dve.wait_ge(S[f"{k}_rstd{n}"], g + 1)
                        dve.scalar_tensor_tensor(shift[u][:, :], mv[u][:, :, 0], -1.0, rs[u][:, :], ALU.mult, ALU.mult)\
                           .then_inc(S[f"{k}_shift{n}"], 1)
                    return step

                def norm(k, n):
                    u = "u" if n else k
                    def step(g):
                        dve.wait_ge(S[f"{k}_rstd{n}"], g + 1)
                        norm_free(dve, k, n, g)
                        src = ln_source(k, n, g)
                        for j in range(J):
                            c = slice(j * D, (j + 1) * D)
                            last = dve.tensor_scalar(nrm[u][:, c], src[:, c], mv[u][:, j, 0:1], rs[u][:, j:j + 1],
                                                     ALU.subtract, ALU.mult)
                        last.then_inc(S[f"{k}_norm{n}"], 1)
                    return step

                def a_p(g):
                    dve.wait_ge(S["a_s"], g + 1)
                    if later(g):
                        dve.wait_ge(S["a_o"], g)
                    dve.tensor_tensor(r(pa["a"]), r(a1), decay[:, :].unsqueeze(1).broadcast_to([P, J, D]), ALU.mult)\
                       .then_inc(S["a_p"], 1)

                def a_x1(g):
                    dve.wait_ge(S["a_o"], g + 1)
                    dve.tensor_tensor(xs[:, g, :], a0[:, :], xs[:, g, :], ALU.add).then_inc(S["a_x1"], 1)

                def row_max(k, src, width):
                    def step(g):
                        dve.wait_ge(S[f"{k}_s"], g + 1)
                        if later(g):
                            dve.wait_ge(S[f"{k}_exp"], g)
                        dve.tensor_reduce(nmax[k][:, :], src[:, 0:J * width].rearrange("p (j s) -> p j s", j=J),
                                          AX.X, ALU.max, negate=True).then_inc(S[f"{k}_max"], 1)
                    return step

                def row_inv(k):
                    def step(g):
                        dve.wait_ge(S[f"{k}_exp"], g + 1)
                        if later(g):
                            dve.wait_ge(S[{"b": "b_a", "c": "c_c"}[k]], g)
                        dve.reciprocal(rinv[k][:, :], rsum[k][:, :]).then_inc(S[f"{k}_rinv"], 1)
                    return step

                def attended(k, src, res, name):
                    def step(g):
                        dve.wait_ge(S[f"{k}_o"], g + 1)
                        dve.wait_ge(S[f"{k}_rinv"], g + 1)
                        if k == "c":
                            dve.wait_ge(S["c_h"], g + 1)
                        for j in range(J):
                            c = slice(j * D, (j + 1) * D)
                            last = dve.scalar_tensor_tensor(mid[:, g, :][:, c], src[:, c], rinv[k][:, j:j + 1], res[:, c],
                                                            ALU.mult, ALU.add)
                        last.then_inc(S[name], 1)
                    return step

                def d_u(g):
                    dve.wait_ge(S["d_f"], g + 1)
                    dve.wait_ge(S["d_h"], g + 1)
                    if later(g):
                        dve.wait_ge(S["d_norm2"], g)
                    dve.scalar_tensor_tensor(ud[:, :], d0[:, :], 0.0, hres["d"][:, :], ALU.max, ALU.add)\
                       .then_inc(S["d_u"], 1)

                def d_x2(g):
                    dve.wait_ge(S["d_t"], g + 1)
                    dve.scalar_tensor_tensor(xs[:, g, :], td[:, :], 0.0, xs[:, g, :], ALU.max, ALU.add)\
                       .then_inc(S["d_x2"], 1)

                def e_l_sb(g):
                    dve.wait_ge(S["e_l"], g + 1)
                    dve.tensor_copy(logits[:, :, :].rearrange("p (g j) e -> p g (j e)", j=J)[:, g, :], e0[:, 0:J * NE])\
                       .then_inc(S["e_l_sb"], 1)

                runs(dve, DVE_ORDER, dict(
                    a_stats=stats("a", "", None), a_aggr=aggr("a", ""), a_norm=norm("a", ""),
                    b_stats=stats("b", "", "a_x1"), b_aggr=aggr("b", ""), b_norm=norm("b", ""),
                    c_stats=stats("c", "", "b_a"), c_aggr=aggr("c", ""), c_norm=norm("c", ""),
                    d_stats=stats("d", "", "c_c"), d_aggr=aggr("d", ""), d_norm=norm("d", ""),
                    d_stats2=stats("d", "2", "d_u"), d_aggr2=aggr("d", "2"), d_norm2=norm("d", "2"),
                    e_stats=stats("e", "", "d_x2"), e_aggr=aggr("e", ""), e_norm=norm("e", ""),
                    **{f"{k}_shift{n}": shifted(k, n) for k, n in (*((k, "") for k in "abcde"), ("d", "2"))},
                    a_p=a_p, a_x1=a_x1, b_max=row_max("b", b1, D), b_rinv=row_inv("b"),
                    b_a=attended("b", b1, nrm["b"], "b_a"), c_max=row_max("c", c0, SC), c_rinv=row_inv("c"),
                    c_c=attended("c", c0, hres["c"], "c_c"), d_u=d_u, d_x2=d_x2, e_l_sb=e_l_sb))

                linked = [0]

                def link(ins):
                    linked[0] += 1
                    ins.then_inc(r_chain, 1)
                    dve.wait_ge(r_chain, linked[0])

                def over_e(t):
                    return t[:, :].unsqueeze(2).broadcast_to([P, NT, NE])

                rev = revio[:, :].unsqueeze(1).broadcast_to([P, NT, NE])
                dve.wait_ge(S["e_l_sb"], G)
                dve.wait_ge(s_late, 7 * 16)
                link(dve.tensor_reduce(rt["max"][:, :], logits[:, :, :], AX.X, ALU.max))
                dve.tensor_tensor(ex[:, :, :], logits[:, :, :], over_e(rt["max"]), ALU.subtract).then_inc(r_sub, 1)
                dve.memset(eligb[:, :], 0.0)
                dve.memset(rt["free"][:, :], 1.0)
                dve.memset(ones[:, :], 1.0)
                dve.memset(zb[:, :], 0.0)
                dve.wait_ge(r_exp, 1)
                link(dve.tensor_reduce(rt["sum"][:, :], prob[:, :, :], AX.X, ALU.add))
                link(dve.reciprocal(rt["inv"][:, :], rt["sum"][:, :]))
                link(dve.tensor_tensor(prob[:, :, :], prob[:, :, :], over_e(rt["inv"]), ALU.mult))
                for c, (m, at) in enumerate((("m1", "i1"), ("m2", "i2"))):
                    link(dve.tensor_reduce(rt[m][:, :], prob[:, :, :], AX.X, ALU.max))
                    link(dve.tensor_tensor(cand[:, :, :], prob[:, :, :], over_e(rt[m]), ALU.is_equal))
                    link(dve.tensor_tensor(cand[:, :, :], cand[:, :, :], rev, ALU.mult))
                    link(dve.tensor_reduce(rt[at][:, :], cand[:, :, :], AX.X, ALU.max))
                    link(dve.tensor_tensor(oh[c][:, :, :], rev, over_e(rt[at]), ALU.is_equal))
                    if c == 0:
                        link(dve.scalar_tensor_tensor(prob[:, :, :], oh[0][:, :, :], -2.0, prob[:, :, :], ALU.mult, ALU.add))
                link(dve.tensor_tensor(asg[:, :, :].rearrange("p e t -> p t e"), oh[0][:, :, :], oh[1][:, :, :], ALU.add))

                def route(e):
                    def step_link(ins, n):
                        ins.then_inc(r_step, 1)
                        dve.wait_ge(r_step, 5 * e + n)
                    step_link(dve.tensor_tensor(elig[:, :], asg[:, e, :], rt["free"][:, :], ALU.mult), 1)
                    dve.tensor_copy(eligb[:, 1:NT + 1], elig[:, :]).then_inc(r_elig, 1)
                    dve.wait_ge(r_cnt, e + 1)
                    step_link(dve.tensor_tensor_scan(rt["cum"][:, :], ones[:, :], bank[6][:, NT:2 * NT], 0.0,
                                                     ALU.mult, ALU.add), 2)
                    step_link(dve.tensor_tensor(rank[:, e, :], bank[6][:, 0:NT], rt["cum"][:, :], ALU.add), 3)
                    dve.scalar_tensor_tensor(keep[:, e, :], rank[:, e, :], float(CAP), elig[:, :], ALU.is_le, ALU.mult)
                    step_link(dve.scalar_tensor_tensor(rt["drop"][:, :], rank[:, e, :], float(CAP), elig[:, :],
                                                       ALU.is_gt, ALU.mult), 4)
                    step_link(dve.tensor_tensor(rt["free"][:, :], rt["free"][:, :], rt["drop"][:, :], ALU.subtract), 5)

                with dve.Fori(0, NE) as e:
                    route(e)

                link(dve.tensor_scalar(piece[:, :, :], rank[:, :, :], float(P), None, ALU.is_gt))
                link(dve.scalar_tensor_tensor(piece[:, :, :], rank[:, :, :], 2.0 * P, piece[:, :, :], ALU.is_gt, ALU.add))
                dve.scalar_tensor_tensor(slot[:, :, :], piece[:, :, :], -float(P), rank[:, :, :], ALU.mult, ALU.add)
                link(dve.tensor_tensor(colm[:, :, :], piece[:, :, :], col0[:, :].unsqueeze(2).broadcast_to([P, NE, NT]), ALU.add))
                link(dve.tensor_tensor(slot[:, :, :], slot[:, :, :], keep[:, :, :], ALU.mult))
                for c in range(2):
                    for src, dst in ((slot, slotc), (colm, colc)):
                        link(dve.tensor_tensor(cand[:, :, :], oh[c][:, :, :], src[:, :, :].rearrange("p e t -> p t e"), ALU.mult))
                        link(dve.tensor_reduce(dst[:, c * NT:(c + 1) * NT], cand[:, :, :], AX.X, ALU.add))
                link(dve.tensor_tensor(rt["sum"][:, :], rt["m1"][:, :], rt["m2"][:, :], ALU.add))
                link(dve.tensor_scalar(rt["sum"][:, :], rt["sum"][:, :], 1e-9, None, ALU.max))
                link(dve.reciprocal(rt["inv"][:, :], rt["sum"][:, :]))
                dve.tensor_tensor(wch[:, 0, :], rt["m1"][:, :], rt["inv"][:, :], ALU.mult)
                link(dve.tensor_tensor(wch[:, 1, :], rt["m2"][:, :], rt["inv"][:, :], ALU.mult))
                link(dve.tensor_tensor(wch[:, :, :], wch[:, :, :], rt["free"][:, :].unsqueeze(1).broadcast_to([P, 2, NT]),
                                       ALU.mult))
                wv = wch[:, :, :].rearrange("p c t -> p (c t)")
                wr_ = wres[:, :, :].rearrange("p c t -> p (c t)")
                for c in range(2):
                    dve.tensor_copy(vals[:, c * NT:(c + 1) * NT, 0], iot[:, :])
                dve.tensor_copy(vals[:, :, 1], plus1[:, 0:1].broadcast_to([P, 2 * NT]))
                link(dve.tensor_copy(vals[:, :, 2], wv))
                link(dve.tensor_tensor(wr_, wv, vals[:, :, 2], ALU.subtract))
                link(dve.tensor_copy(vals[:, :, 3], wr_))
                link(dve.tensor_tensor(wv, wr_, vals[:, :, 3], ALU.subtract))
                link(dve.tensor_copy(vals[:, :, 4], wv))

                def chunk(n, i, q):
                    cs = bass.ds(n * CT, CT)
                    if q is not None:
                        dve.wait_ge(t_used, n - 1)
                    dve.tensor_tensor(ohp[i][:, :, :], slotc[:, cs].unsqueeze(2).broadcast_to([P, CT, P]),
                                      iop[:, :].unsqueeze(1).broadcast_to([P, CT, P]), ALU.is_equal)
                    dve.tensor_tensor(ohc[i][:, :, :], colc[:, cs].unsqueeze(2).broadcast_to([P, CT, NC]),
                                      ioc[:, :].unsqueeze(1).broadcast_to([P, CT, NC]), ALU.is_equal).then_inc(t_link, 1)
                    dve.wait_ge(t_link, n + 1)
                    dve.tensor_tensor(ohv[i][:, :, :, :], ohc[i][:, :, :].unsqueeze(2).broadcast_to([P, CT, NV, NC]),
                                      vals[:, cs, :].unsqueeze(3).broadcast_to([P, CT, NV, NC]), ALU.mult)\
                       .then_inc(t_chunk, 1)

                chunk(0, 0, None)
                chunk(1, 1, None)
                with dve.Fori(1, NCH // 2) as q:
                    chunk(2 * q, 0, q)
                    chunk(2 * q + 1, 1, q)

                dve.wait_ge(t_table, 1)
                link(dve.tensor_copy(tab[:, :, :].rearrange("p v c -> p (v c)"), bank[7][:, 0:NV * NC]))
                link(dve.scalar_tensor_tensor(tidx[:, :], tab[:, 0, :], float(P), tab[:, 1, :], ALU.mult, ALU.add))
                link(dve.tensor_scalar(tidx[:, :], tidx[:, :], -1.0, None, ALU.add))
                dve.tensor_scalar(gidx[:, :], tidx[:, :], 0.0, None, ALU.max)
                link(dve.tensor_scalar(temp[:, :], tab[:, 1, :], 0.0, None, ALU.is_equal))
                link(dve.tensor_tensor(temp[:, :], temp[:, :], spare[:, :], ALU.mult))
                link(dve.tensor_tensor(tw[:, :], tab[:, 3, :], tab[:, 4, :], ALU.add))
                link(dve.tensor_tensor(tw[:, :], tw[:, :], tab[:, 2, :], ALU.add))
                dve.tensor_tensor(sidx[:, :], tidx[:, :], temp[:, :], ALU.add).then_inc(t_index, 1)
                link(dve.tensor_scalar(rt["drop"][:, :], rt["free"][:, :], -1.0, 1.0, ALU.mult, ALU.add))

                dropv = rt["drop"][:, :].rearrange("p (g j) -> p g j", j=J)

                def base(g):
                    dve.wait_ge(n_taken, g + 1)
                    for j in range(J):
                        c = slice(j * D, (j + 1) * D)
                        last = dve.scalar_tensor_tensor(xs[:, g, :][:, c], mid[:, g, :][:, c], dropv[:, g, :][:, j:j + 1],
                                                        xs[:, g, :][:, c], ALU.mult, ALU.add)
                    last.then_inc(o_base, 1)

                def gathered_sb(e, i):
                    dve.wait_ge(x_t, e + 1)
                    dve.tensor_copy(xgT[:, e, :],
                                    bank[6 + i][:, 0:CAP]).then_inc(x_tsb, 1)

                def weighted(e, i):
                    dve.wait_ge(n_out, G + e + 1)
                    if not (isinstance(e, int) and e < 2):
                        dve.wait_ge(x_add, 16 * NQ * (e - 1))
                    dve.tensor_tensor(ye[i][:, :, :], bank[4 + i][:, 0:NQ * D].rearrange("p (n d) -> p n d", n=NQ),
                                      tw[:, bass.ds(NQ * e, NQ)].unsqueeze(2).broadcast_to([P, NQ, D]), ALU.mult)\
                       .then_inc(n_taken, 1)

                with dve.Fori(0, G - XR - 1) as g:
                    base(g)
                for e in range(XR):
                    base(G - XR - 1 + e)
                    gathered_sb(e, e % 2)
                base(G - 1)
                for e in range(NE - XR):
                    gathered_sb(e + XR, e % 2)
                    weighted(e, e % 2)
                with dve.Fori((NE - XR) // 2, NE // 2) as q:
                    weighted(2 * q, 0)
                    weighted(2 * q + 1, 1)
    return nc


_INS = ["x", "ctx_1024", "L0_attn_W_Q", "L0_attn_W_K", "L0_attn_W_V", "L0_xattn_Wq", "L0_xattn_Wk", "L0_xattn_Wv",
        "L0_xattn_Wcq", "L0_xattn_Wck", "L0_xattn_Wcv", "L0_xattn_gamma", "L0_xattn_beta", "L0_xattn_W1",
        "L0_xattn_b1", "L0_ffn_Wr", "L0_ffn_W1", "L0_ffn_b1", "L0_ffn_W2", "L0_ffn_b2", "L0_ffn_fw1", "L0_ffn_fb1",
        "L0_ffn_fw2", "L0_ffn_fb2"]


def constants():
    import numpy as np
    n = np.arange(128)
    d = n[None, :] - n[:, None]
    return {
        "c_ident": np.eye(128, dtype=np.float32),
        "c_decay": np.where(d >= 0, np.power(np.float32(0.99), np.maximum(d, 0).astype(np.float32)), 0).astype(np.float32),
        "c_mask": np.where(d > 0, np.float32(-1e30), np.float32(0)).astype(np.float32),
        "c_tri": (d >= 0).astype(np.float32),
        "c_revio": np.tile(8 - np.arange(8, dtype=np.float32), (128, 1)),
        "c_col0": np.tile(3 * np.arange(8, dtype=np.float32), (128, 1)),
        "c_iop": np.tile(np.arange(1, 129, dtype=np.float32), (128, 1)),
        "c_ioc": np.tile(np.arange(24, dtype=np.float32), (128, 1)),
        "c_iot": np.tile(np.arange(64, dtype=np.float32), (128, 1)),
        "c_plus1": np.arange(1, 129, dtype=np.float32)[:, None],
        "c_spare": (8192 + 1 + np.arange(128)[:, None] + 128 * (np.arange(24) % 3)[None, :]).astype(np.float32),
    }


def kernel(**inputs):
    import numpy as _np
    import concourse.bacc as _bacc
    from concourse import mybir as _mybir
    from concourse.bass_utils import run_bass_kernel_spmd as _run

    nc = _bacc.Bacc("TRN2", target_bir_lowering=False, num_devices=1)
    arrays, args = {}, {}
    for name, a in [(n, _np.ascontiguousarray(inputs[n])) for n in _INS] + list(constants().items()):
        arrays[f"in_{name}_dram"] = a
        args[name] = nc.dram_tensor(f"in_{name}_dram", a.shape, _mybir.dt.from_np(a.dtype), kind="ExternalInput").ap()
    out = nc.dram_tensor("out_0_dram", ((64 + 3) * 128, 128), _mybir.dt.float32, kind="ExternalOutput").ap()
    decoder_program(nc, args, out)
    r = _run(nc, [arrays], core_ids=[0])
    return r.results[0]["out_0_dram"][:64 * 128].reshape(64, 128, 128)
```

```python
import concourse.bass as bass
from concourse import mybir
from contextlib import ExitStack

DVE_ORDER = (
    (0, "a_stats"), (2, "b_max"), (0, "a_aggr"), (1, "a_p"), (4, "d_norm"), (2, "b_rinv"), (5, "d_x2"),
    (1, "a_x1"), (0, "a_shift"), (5, "e_stats"), (1, "b_stats"), (3, "c_max"), (1, "b_aggr"), (5, "e_aggr"),
    (2, "b_a"), (4, "d_u"), (1, "b_norm"), (3, "c_rinv"), (5, "e_shift"), (4, "d_stats2"), (2, "c_stats"),
    (4, "d_aggr2"), (2, "c_aggr"), (3, "c_c"), (4, "d_shift2"), (3, "d_stats"), (3, "d_aggr"), (2, "c_shift"),
    (2, "c_norm"), (5, "e_l_sb"),
)
POOL_ORDER = (
    (5, "d_t"), (0, "a_rstd"), (4, "d_h"), (1, "b_rstd"), (5, "e_rstd"), (3, "c_h"), (4, "d_rstd2"),
    (2, "c_rstd"), (3, "d_rstd"),
)
PE_ORDER = (
    (3, "c_xt"), (3, "c_k"), (1, "a_o"), (4, "d_xt"), (2, "b_pt"), (3, "c_s"), (3, "c_v"), (2, "b_o"),
    (4, "d_f"), (0, "a_xt"), (3, "c_pt"), (0, "a_g"), (1, "b_xt"), (3, "c_o"), (0, "a_v"), (5, "e_xt"),
    (1, "b_g"), (0, "a_s"), (5, "e_l"), (1, "b_s"), (2, "c_ct"), (1, "b_v"),
)
ACT_ORDER = (
    (3, "c_norm_act"), (3, "c_ct_sb"), (2, "b_exp"), (2, "b_v_sb"), (3, "c_ht_sb"), (3, "c_k_sb"),
    (4, "d_ht_sb"), (2, "b_pt_sb"), (0, "a_norm"), (3, "c_v_sb"), (3, "c_exp"), (0, "a_xt_sb"), (3, "c_pt_sb"),
    (5, "e_norm"), (1, "b_xt_sb"), (0, "a_g_sb"), (0, "a_v_sb"), (5, "e_xt_sb"), (1, "b_g_sb"), (4, "d_norm2"),
)
SP_ORDER = ((2, "load_ctx"), (5, "store_z"), (5, "store_zT"))



def decoder_program(nc, A, out):
    fp32, bf16 = mybir.dt.float32, mybir.dt.bfloat16
    u32 = mybir.dt.uint32
    ALU, ACT, AX = mybir.AluOpType, mybir.ActivationFunctionType, mybir.AxisListType

    NB, P, D = A["x"].shape
    SC = A["ctx_1024"].shape[1]
    J = 4
    G = NB // J
    W = J * D
    NT = NB
    NE, _, FF = A["L0_ffn_W1"].shape
    FB = FF // P
    CAP = int(1.25 * 4 * 256 * 2 / NE)
    SQ = (P, P, CAP - 2 * P)
    NQ = len(SQ)
    TOKENS = NB * P
    EPS1, EPS2 = 1e-5, 1e-3
    SCALE = float(D) ** -0.5
    LAGS = 1 + max(lag for o in (DVE_ORDER, POOL_ORDER, PE_ORDER, ACT_ORDER) for lag, _ in o)
    ACT_NORMS = ("a", "u", "e",)

    x_v = A["x"].rearrange("(g j) t d -> t g j d", j=J)
    ctx_v = A["ctx_1024"].rearrange("(g j) s d -> s g j d", j=J)
    SPARE = NQ * P
    out_v = out[0:TOKENS, :].rearrange("(g j t) d -> t g j d", j=J, t=P)
    out_spare = out[TOKENS:TOKENS + SPARE, :].rearrange("(n p) d -> p n d", p=P)
    z_rows = nc.dram_tensor("z_rows", (TOKENS, D), fp32, kind="Internal").ap()
    z_rows_v = z_rows.rearrange("(g j t) d -> t g j d", j=J, t=P)

    with ExitStack() as ctx:
        def sb(name, shape, dt=fp32):
            return ctx.enter_context(nc.sbuf_tensor(name, shape, dt))

        def sem(name):
            return ctx.enter_context(nc.semaphore(name))

        xs = sb("xs", [P, G, W])
        mid = sb("mid", [P, G, W])
        zT = sb("zT", [P, G, W])
        cx = sb("cx", [SC, W])
        ident = sb("ident", [P, P])
        identb = sb("identb", [P, P], bf16)
        decay = sb("decay", [P, P])
        maskf = sb("maskf", [P, P])
        maskb = sb("maskb", [P, J, P], bf16)
        trif = sb("trif", [P, P])
        trib = sb("trib", [P, P], bf16)
        onesb = sb("onesb", [P, P], bf16)
        NW = 12
        wts = sb("wts", [P, NW, D])
        Wn = {n: wts[:, i, :] for i, n in enumerate(
            ["L0_attn_W_Q", "L0_attn_W_K", "L0_attn_W_V", "L0_xattn_Wq", "L0_xattn_Wk", "L0_xattn_Wv",
             "L0_xattn_Wcq", "L0_xattn_Wck", "L0_xattn_Wcv", "L0_xattn_W1"])}
        wtT = sb("wtT", [P, 6, D])
        mqk = sb("mqk", [P, 3, D])
        MA, MB, MC = (mqk[:, i, :] for i in range(3))
        gam = sb("gam", [P, D])
        bet = sb("bet", [P, D])
        gamT = sb("gamT", [P, 1])
        betT = sb("betT", [P, 1])
        negh = sb("negh", [P, J])
        wr = sb("wr", [P, NE])
        BR = 65
        ball = sb("ball", [BR, (2 + NE) * D], bf16)
        fw1 = sb("fw1", [P, FF])
        fw2 = sb("fw2", [P, FB, D])
        fb1 = sb("fb1", [P, FB])
        eb1 = sb("eb1", [P, NE, FB])
        zeros = sb("zeros", [P, D])

        st = {k: sb(f"st_{k}", [P, J, 6]) for k in ("a", "b", "c", "d", "u", "e")}
        mv = {k: sb(f"mv_{k}", [P, J, 2]) for k in ("a", "b", "c", "d", "u", "e")}
        ve = {k: sb(f"ve_{k}", [P, J]) for k in ("a", "b", "c", "d", "u", "e")}
        rs = {k: sb(f"rs_{k}", [P, J]) for k in ("a", "b", "c", "d", "u", "e")}
        shift = {k: sb(f"shift_{k}", [P, J]) for k in (*ACT_NORMS, "c")}
        work = sb("work", [P, 29, W])
        places = iter(range(29))

        def buffers(*keys):
            return {k: work[:, next(places), :] for k in keys}

        gq, va, pa = {}, {}, {}
        gq.update(buffers("c"))
        va.update(buffers("c"))
        pa.update(buffers("c"))
        pT = buffers("c")
        hres = buffers("c", "d")
        hmul = buffers("c", "d", "u")
        ud = work[:, next(places), :]
        td = work[:, next(places), :]
        nrm = buffers("u", "c", "d", "e")
        tr = buffers("c", "d", "e")
        nrm.update(buffers("a", "b"))
        tr.update(buffers("a", "b"))
        gq.update(buffers("a", "b"))
        va.update(buffers("a", "b"))
        pa.update(buffers("a", "b"))
        pT.update(buffers("b"))
        cT = sb("cT", [P, J * SC])
        nmax = {k: sb(f"nmax_{k}", [P, J]) for k in ("b", "c")}
        rsum = {k: sb(f"rsum_{k}", [P, J]) for k in ("b", "c")}
        rinv = {k: sb(f"rinv_{k}", [P, J]) for k in ("b", "c")}
        BW = (2 + NE) * D
        brow, bres = (zT[0:BR, i:i + 3, :].rearrange("p a b -> p (a b)")[:, 0:BW] for i in (4, 7))
        bhi, bmid, blo = (zT[0:BR, i:i + 2, :].rearrange("p a b -> p (a b)").bitcast(bf16)[:, 0:BW] for i in (10, 12, 14))
        logits = sb("logits", [P, NT, NE])

        rt = {k: sb(f"rt_{k}", [P, NT]) for k in ("max", "sum", "inv", "m1", "m2", "i1", "i2", "free", "cum", "drop")}
        def te(t):
            return work[:, t, :].rearrange("p (t e) -> p t e", e=NE)

        def et(t):
            return work[:, t, :].rearrange("p (e t) -> p e t", e=NE)

        ex, prob, cand = te(26), te(27), te(28)
        oh = [sb(f"oh{c}", [P, NT, NE]) for c in range(2)]
        wch = sb("wch", [P, 2, NT])
        wres = sb("wres", [P, 2, NT])
        revio = sb("revio", [P, NE])
        asg = sb("asg", [P, NE, NT], bf16)
        elig = sb("elig", [P, NT])
        eligb = sb("eligb", [P, NT + 2], bf16)
        ones = sb("ones", [P, NT])
        rank = et(8)
        NC = NE * NQ
        NV = 5
        CT = 8
        NCH = 2 * NT // CT
        CR = 4
        piece = sb("piece", [P, 2 * NT])
        slotc = sb("slotc", [P, 2 * NT])
        colc = sb("colc", [P, 2 * NT])
        vals = sb("vals", [P, 2 * NT, NV], bf16)
        iop = sb("iop", [P, P])
        ioc = sb("ioc", [P, NC])
        iot = sb("iot", [P, NT])
        plus1 = sb("plus1", [P, 1])
        spare = sb("spare", [P, NC])
        ohp = [work[:, i, :].bitcast(bf16).rearrange("p (t q) -> p t q", q=P) for i in (26, 27, 12, 13)]
        ohc = [sb(f"ohc{i}", [P, CT, NC], bf16) for i in range(CR)]
        ohv = [work[:, i, :].bitcast(bf16)[:, 0:CT * NV * NC].rearrange("p (t v c) -> p t v c", v=NV, c=NC)
               for i in (28, 11, 14, 15)]
        zb = sb("zb", [P, P], bf16)
        tab = sb("tab", [P, NV, NC])
        tidx = sb("tidx", [P, NC])
        temp = sb("temp", [P, NC])
        tw = sb("tw", [P, NC])
        gidx = sb("gidx", [P, NC], u32)
        sidx = sb("sidx", [P, NC], u32)
        hf = [work[:, 18 + FB * i:18 + FB * (i + 1), :] for i in range(2)]
        ew1 = [sb(f"ew1_{i}", [P, FF]) for i in range(2)]
        ew2 = [sb(f"ew2_{i}", [P, FB, D]) for i in range(2)]
        gi = [sb(f"gi{i}", [P, NQ], u32) for i in range(2)]
        si = [sb(f"si{i}", [P, NQ], u32) for i in range(2)]
        xg = [work[:, 12 + i, 0:NQ * D].rearrange("p (n d) -> p n d", d=D) for i in range(2)]
        ye = [work[:, 14 + i, 0:NQ * D].rearrange("p (n d) -> p n d", d=D) for i in range(2)]
        xgT = work[:, 0:NE, 0:CAP]

        bank = [ctx.enter_context(nc.psum_tensor(f"bank{i}", [P, W], fp32)) for i in range(8)]
        a0, a1, b0, b1, c0, c1, d0, e0 = bank

        names = set(n for o in (DVE_ORDER, POOL_ORDER, PE_ORDER, ACT_ORDER) for _, n in o)
        S = {n: sem(n) for n in sorted(names)}
        for n in ("a_veps", "b_veps", "c_veps", "d_veps", "d_veps2", "e_veps", "c_hmul", "d_hmul", "d_tmul"):
            S[n] = sem(n)
        s_wload, s_const, s_x0, s_x1, s_x2, s_ctx = (
            sem(n) for n in ("weights_loaded", "constants_loaded", "x_first", "x_next", "x_rest", "ctx_loaded"))
        s_brow, s_brest = sem("bias_rows_loaded"), sem("later_bias_rows_loaded")
        s_wqk, s_pool0 = sem("query_key_weights_loaded"), sem("pool_memsets")
        s_decay = sem("decay_loaded")
        s_x23 = sem("x_third_fourth")
        s_bias1, s_bias2 = sem("bias_parts"), sem("later_bias_parts")
        s_prep_dve, s_prep_pe, s_prep_act = sem("prep_dve"), sem("prep_pe"), sem("prep_act")
        s_zrow, s_zT = sem("z_rows_stored"), sem("zT_stored")
        s_fill = sem("spare_rows_filled")
        s_late = sem("late_constants")
        s_fw = sem("fallback_weights")
        r_chain, r_sub, r_exp, r_elig, r_cnt, r_step = (
            sem(n) for n in ("route_chain", "route_shifted", "route_exp", "route_eligible", "route_counts", "route_rank"))
        t_whole = sem("table_chunk_whole")
        t_onehot, t_chunk, t_used, t_table, t_index = (
            sem(n) for n in ("table_one_hot", "table_chunk", "table_chunk_used", "table_sum", "table_ready"))
        n_hid, n_gelu, n_out, n_taken = (
            sem(n) for n in ("net_hidden", "net_gelu", "net_out", "net_out_taken"))
        x_w1, x_w2 = ([sem(f"x_weights{n}_{i}") for i in range(2)] for n in (1, 2))
        x_g = [sem(f"x_gathered{i}") for i in range(2)]
        x_t, x_tsb, x_add, x_gi, x_si = (
            sem(n) for n in ("x_transposed", "x_transposed_sb", "x_added", "x_gather_rows", "x_add_rows"))
        o_base, o_st = sem("base_ready"), sem("base_stored")

        QK = ["L0_attn_W_Q", "L0_attn_W_K", "L0_xattn_Wq", "L0_xattn_Wk", "L0_xattn_Wcq", "L0_xattn_Wck"]

        def r(t):
            return t[:, :].rearrange("p (j d) -> p j d", j=J)

        def later(g):
            return not (isinstance(g, int) and g == 0)

        def wait_apart(eng, *waits):
            waits = [(semaphore, value if isinstance(value, int) else eng.to_reg(value)) for semaphore, value in waits]
            eng.wait_ge(s_x0, 16)
            for semaphore, value in waits:
                eng.wait_ge(semaphore, value)

        def normalised(eng, k, n, g):
            eng.wait_ge(S[f"{k}_norm{n}"], g)
            if k == "c":
                eng.wait_ge(S["c_norm_act"], g)

        def ln_source(k, n, g):
            return ud[:, :] if n else {"a": xs, "b": xs, "c": mid, "d": mid, "e": xs}[k][:, g, :]

        def norm_free(eng, k, n, g):
            if later(g):
                for f in {"a": ("a_xt",), "b": ("b_xt", "b_a"), "c": ("c_xt", "c_hmul"), "d": ("d_xt", "d_hmul"),
                          "d2": ("d_tmul",), "e": ("e_xt",)}[k + n]:
                    eng.wait_ge(S[f], g)
                if k == "e":
                    eng.wait_ge(s_zrow, 16 * g)

        NCONST = 7 * 16
        BATCHES = ((0, 13), (13, G))
        NPARTS = 5

        with nc.Block() as block:
            def runs(eng, order, steps, after_turn={}, after_step={}):
                def turn(t, filled):
                    for lag, name in order:
                        if filled or 0 <= t - lag < G:
                            steps[name](t - lag)
                            if not filled:
                                for more in after_step.get((name, t - lag), ()):
                                    more()
                for t in range(LAGS):
                    turn(t, False)
                    for more in after_turn.get(t, ()):
                        more()
                with eng.Fori(0, (G - LAGS) // 2) as q:
                    turn(2 * q + LAGS, True)
                    turn(2 * q + LAGS + 1, True)
                for t in range(G - (G - LAGS) % 2, G + LAGS - 1):
                    turn(t, False)

            @block.sync
            def _(sp):
                sp.dma_start(xs[:, 0, :].rearrange("p (j d) -> p j d", j=J), x_v[:, 0, :, :]).then_inc(s_x0, 16)
                sp.dma_start(ident[:, :], A["c_ident"]).then_inc(s_wqk, 16)
                for n in QK:
                    sp.dma_start(Wn[n], A[n]).then_inc(s_wqk, 16)
                sp.dma_start(decay[:, :], A["c_decay"]).then_inc(s_decay, 16)
                for n in Wn:
                    if n not in QK:
                        sp.dma_start(Wn[n], A[n]).then_inc(s_wload, 16)
                sp.dma_start(xs[:, 1, :].rearrange("p (j d) -> p j d", j=J), x_v[:, 1, :, :]).then_inc(s_x1, 16)
                sp.dma_start(maskf[:, :], A["c_mask"]).then_inc(s_const, 16)
                sp.dma_start(trif[:, :], A["c_tri"]).then_inc(s_const, 16)
                sp.dma_start(gam[:, :], A["L0_xattn_gamma"].partition_broadcast(P)).then_inc(s_const, 16)
                sp.dma_start(bet[:, :], A["L0_xattn_beta"].partition_broadcast(P)).then_inc(s_const, 16)
                sp.dma_start(gamT[:, :], A["L0_xattn_gamma"].unsqueeze(1)).then_inc(s_const, 16)
                sp.dma_start(betT[:, :], A["L0_xattn_beta"].unsqueeze(1)).then_inc(s_const, 16)
                sp.dma_start(wr[:, :], A["L0_ffn_Wr"]).then_inc(s_const, 16)
                for g in range(2, 4):
                    sp.dma_start(xs[:, g, :].rearrange("p (j d) -> p j d", j=J), x_v[:, g, :, :]).then_inc(s_x23, 16)
                sp.wait_ge(s_pool0, 1)
                for k in (0, 32, 64):
                    sp.dma_start(brow[k:k + 1, 0:D], A["L0_xattn_b1"].unsqueeze(0)).then_inc(s_brow, 16)
                for k in (0, 32, 64):
                    sp.dma_start(brow[k:k + 1, D:2 * D], A["L0_ffn_fb2"].unsqueeze(0)).then_inc(s_brest, 16)
                    sp.dma_start(brow[k:k + 1, 2 * D:(2 + NE) * D],
                                 A["L0_ffn_b2"].rearrange("e d -> (e d)").unsqueeze(0)).then_inc(s_brest, 16)
                sp.dma_start(revio[:, :], A["c_revio"]).then_inc(s_late, 16)
                sp.dma_start(iop[:, :], A["c_iop"]).then_inc(s_late, 16)
                sp.dma_start(ioc[:, :], A["c_ioc"]).then_inc(s_late, 16)
                sp.dma_start(iot[:, :], A["c_iot"]).then_inc(s_late, 16)
                sp.dma_start(plus1[:, :], A["c_plus1"]).then_inc(s_late, 16)
                sp.dma_start(spare[:, :], A["c_spare"]).then_inc(s_late, 16)
                sp.dma_start(fw1[:, :], A["L0_ffn_fw1"]).then_inc(s_fw, 16)
                sp.dma_start(fw2[:, :, :], A["L0_ffn_fw2"].rearrange("(k p) d -> p k d", p=P)).then_inc(s_fw, 16)
                with nc.allow_non_contiguous_dma("bias columns, once"):
                    sp.dma_start(fb1[:, :], A["L0_ffn_fb1"].rearrange("(k p) -> p k", p=P)).then_inc(s_fw, 16)
                    for e in range(NE):
                        sp.dma_start(eb1[:, e, :], A["L0_ffn_b1"][e, :].rearrange("(k p) -> p k", p=P)).then_inc(s_fw, 16)
                sp.dma_start(xs[:, 4:G, :].rearrange("p g (j d) -> p (g j) d", j=J),
                             x_v[:, 4:G].rearrange("t g j d -> t (g j) d")).then_inc(s_x2, 16)

                def load_ctx(g):
                    if later(g):
                        sp.wait_ge(S["c_ct"], g)
                    sp.dma_start(cx[:, :].rearrange("s (j d) -> s j d", j=J), ctx_v[:, g, :, :]).then_inc(s_ctx, 16)

                def store_z(g):
                    sp.wait_ge(S["e_norm"], g + 1)
                    sp.dma_start(z_rows_v[:, g, :, :], r(nrm["e"])).then_inc(s_zrow, 16)

                def store_zT(g):
                    sp.wait_ge(S["e_xt_sb"], g + 1)
                    sp.dma_start(zT[:, g, :], tr["e"][:, :]).then_inc(s_zT, 16)

                sp.wait_ge(s_pool0, 2)
                sp.dma_start(out_spare, zeros[:, :].unsqueeze(1).broadcast_to([P, NQ, D])).then_inc(s_fill, 16)

                def load_first(e, i):
                    if not (isinstance(e, int) and e < 2):
                        sp.wait_ge(n_hid, FB * (G + e - 1))
                    sp.dma_start(ew1[i][:, :], A["L0_ffn_W1"][e, :, :]).then_inc(x_w1[i], 16)

                def load_second(e, i):
                    if not (isinstance(e, int) and e < 2):
                        sp.wait_ge(n_out, G + e - 1)
                    sp.dma_start(ew2[i][:, :, :], A["L0_ffn_W2"][e, :, :].rearrange("(k p) d -> p k d", p=P))\
                      .then_inc(x_w2[i], 16)

                for e in range(2):
                    load_first(e, e)
                    load_second(e, e)
                runs(sp, SP_ORDER, dict(load_ctx=load_ctx, store_z=store_z, store_zT=store_zT))
                with sp.Fori(0, G) as g:
                    sp.wait_ge(o_base, g + 1)
                    sp.dma_start(out_v[:, g, :, :], xs[:, g, :].rearrange("p (j d) -> p j d", j=J)).then_inc(o_st, 16)
                load_first(2, 0)
                with sp.Fori(1, NE // 2 - 1) as q:
                    load_first(2 * q + 1, 1)
                    load_second(2 * q, 0)
                    load_first(2 * q + 2, 0)
                    load_second(2 * q + 1, 1)
                load_first(NE - 1, 1)
                load_second(NE - 2, 0)
                load_second(NE - 1, 1)

            @block.tensor
            def _(pe):
                pe.wait_ge(s_wqk, 16 * (1 + len(QK)))
                for i, n in enumerate(QK):
                    last = pe.transpose(bank[4 + i // 4][:, (i % 4) * D:(i % 4 + 1) * D], Wn[n], ident[:, :])
                last.then_inc(s_prep_pe, 1)

                def weight_products():
                    pe.wait_ge(s_prep_act, 2)
                    for k, (left, right) in enumerate(((0, 1), (2, 3), (5, 4))):
                        last = pe.matmul(bank[6][:, k * D:(k + 1) * D], wtT[:, left, :], wtT[:, right, :],
                                         start=True, stop=True)
                    last.then_inc(s_prep_pe, 1)
                    pe.wait_ge(s_prep_act, 3)
                    pe.wait_ge(s_wload, 16 * (len(Wn) - len(QK)))

                def transposed(k, dst):
                    def step(g):
                        free = {"a": "a_x1", "b": "b_pt_sb", "c": "c_c", "d": "d_u", "e": "e_l_sb"}[k]
                        normalised(pe, k, "", g + 1)
                        if later(g):
                            pe.wait_ge(S[free], g)
                        for j in range(J):
                            last = pe.transpose(dst[:, j * D:(j + 1) * D], nrm[k][:, j * D:(j + 1) * D], ident[:, :])
                        last.then_inc(S[f"{k}_xt"], 1)
                    return step

                def a_g(g):
                    pe.wait_ge(S["a_xt_sb"], g + 1)
                    if later(g):
                        pe.wait_ge(S["a_p"], g)
                    pe.matmul(a1[:, :], MA, tr["a"][:, :], start=True, stop=True).then_inc(S["a_g"], 1)

                def a_v(g):
                    pe.wait_ge(S["a_xt_sb"], g + 1)
                    for j in range(J):
                        c = slice(j * D, (j + 1) * D)
                        last = pe.matmul(a0[:, c], tr["a"][:, c], Wn["L0_attn_W_V"], start=True, stop=True)
                    last.then_inc(S["a_v"], 1)

                def a_s(g):
                    pe.wait_ge(S["a_g_sb"], g + 1)
                    for j in range(J):
                        c = slice(j * D, (j + 1) * D)
                        last = pe.matmul(a1[:, c], tr["a"][:, c], gq["a"][:, c], start=True, stop=True)
                    last.then_inc(S["a_s"], 1)

                def a_o(g):
                    pe.wait_ge(S["a_p"], g + 1)
                    pe.wait_ge(S["a_v_sb"], g + 1)
                    for j in range(J):
                        c = slice(j * D, (j + 1) * D)
                        last = pe.matmul(a0[:, c], va["a"][:, c], pa["a"][:, c], start=True, stop=True)
                    last.then_inc(S["a_o"], 1)

                def b_g(g):
                    pe.wait_ge(S["b_xt_sb"], g + 1)
                    if later(g):
                        pe.wait_ge(S["b_a"], g)
                    pe.matmul(b1[:, :], MB, tr["b"][:, :], start=True, stop=True).then_inc(S["b_g"], 1)

                def b_v(g):
                    pe.wait_ge(S["b_xt_sb"], g + 1)
                    for j in range(J):
                        c = slice(j * D, (j + 1) * D)
                        last = pe.matmul(b0[:, c], tr["b"][:, c], Wn["L0_xattn_Wv"], start=True, stop=True)
                    last.then_inc(S["b_v"], 1)

                def b_s(g):
                    pe.wait_ge(s_prep_dve, 1)
                    pe.wait_ge(S["b_g_sb"], g + 1)
                    pe.matmul(b1[:, :], identb[:, :], maskb[:, :, :].rearrange("p j d -> p (j d)"),
                              start=True, stop=False, skip_group_check=True)
                    for j in range(J):
                        c = slice(j * D, (j + 1) * D)
                        last = pe.matmul(b1[:, c], gq["b"][:, c], tr["b"][:, c], start=False, stop=(j == J - 1),
                                         skip_group_check=True)
                    last.then_inc(S["b_s"], 1)

                def b_pt(g):
                    pe.wait_ge(S["b_exp"], g + 1)
                    pe.wait_ge(S["b_v_sb"], g + 1)
                    for j in range(J):
                        c = slice(j * D, (j + 1) * D)
                        last = pe.transpose(b0[:, c], pa["b"][:, c], ident[:, :])
                    last.then_inc(S["b_pt"], 1)

                def b_o(g):
                    pe.wait_ge(S["b_pt_sb"], g + 1)
                    for j in range(J):
                        c = slice(j * D, (j + 1) * D)
                        last = pe.matmul(b1[:, c], pT["b"][:, c], va["b"][:, c], start=True, stop=True)
                    last.then_inc(S["b_o"], 1)

                def c_ct(g):
                    if later(g):
                        pe.wait_ge(S["c_pt_sb"], g)
                    pe.wait_ge(s_ctx, 16 * (g + 1))
                    for j in range(J):
                        last = pe.transpose(c1[:, j * SC:(j + 1) * SC], cx[:, j * D:(j + 1) * D], ident[0:SC, 0:SC])
                    last.then_inc(S["c_ct"], 1)

                def c_v(g):
                    pe.wait_ge(S["c_k_sb"], g + 1)
                    for j in range(J):
                        last = pe.matmul(c1[0:SC, j * D:(j + 1) * D], cT[:, j * SC:(j + 1) * SC],
                                         Wn["L0_xattn_Wcv"], start=True, stop=True)
                    last.then_inc(S["c_v"], 1)

                def c_k(g):
                    pe.wait_ge(S["c_ct_sb"], g + 1)
                    pe.matmul(c1[:, 0:J * SC], MC, cT[:, :], start=True, stop=True).then_inc(S["c_k"], 1)

                def c_s(g):
                    pe.wait_ge(S["c_ht_sb"], g + 1)
                    pe.wait_ge(S["c_k_sb"], g + 1)
                    for j in range(J):
                        last = pe.matmul(c0[:, j * SC:(j + 1) * SC], tr["c"][:, j * D:(j + 1) * D],
                                         gq["c"][:, j * SC:(j + 1) * SC], start=True, stop=True)
                    last.then_inc(S["c_s"], 1)

                def c_pt(g):
                    pe.wait_ge(S["c_exp"], g + 1)
                    pe.wait_ge(S["c_v_sb"], g + 1)
                    for j in range(J):
                        last = pe.transpose(c1[0:SC, j * D:(j + 1) * D], pa["c"][:, j * SC:(j + 1) * SC], ident[:, :])
                    last.then_inc(S["c_pt"], 1)

                def c_o(g):
                    pe.wait_ge(S["c_pt_sb"], g + 1)
                    for j in range(J):
                        c = slice(j * D, (j + 1) * D)
                        last = pe.matmul(c0[:, c], pT["c"][0:SC, c], va["c"][0:SC, c], start=True, stop=True)
                    last.then_inc(S["c_o"], 1)

                def d_f(g):
                    pe.wait_ge(S["d_ht_sb"], g + 1)
                    pe.wait_ge(s_bias1, NPARTS)
                    pe.matmul(d0[:, :], onesb[0:BR, :], ball[:, 0:D].unsqueeze(1).broadcast_to([BR, J, D]),
                              start=True, stop=False, skip_group_check=True)
                    for j in range(J):
                        c = slice(j * D, (j + 1) * D)
                        last = pe.matmul(d0[:, c], tr["d"][:, c], Wn["L0_xattn_W1"], start=False, stop=(j == J - 1),
                                         skip_group_check=True)
                    last.then_inc(S["d_f"], 1)

                def e_l(g):
                    pe.wait_ge(s_const, NCONST)
                    pe.wait_ge(S["e_xt_sb"], g + 1)
                    for j in range(J):
                        last = pe.matmul(e0[:, j * NE:(j + 1) * NE], tr["e"][:, j * D:(j + 1) * D], wr[:, :],
                                         start=True, stop=True)
                    last.then_inc(S["e_l"], 1)

                def f_ready():
                    pe.wait_ge(s_fw, (3 + NE) * 16)
                    pe.wait_ge(s_bias2, NPARTS)
                    pe.wait_ge(s_zT, 4 * 16)

                def f_hidden(g, blocks=range(FB)):
                    for k in blocks:
                        if not (isinstance(g, int) and g == 0):
                            pe.wait_ge(n_gelu, FB * (g - 1) + k + 1)
                        pe.matmul(bank[k][:, :], fw1[:, k * P:(k + 1) * P], zT[:, g, :], start=True, stop=True)\
                          .then_inc(n_hid, 1)

                def f_out(g, i, tiles=range(J)):
                    y = bank[4 + i]
                    if 0 in tiles:
                        pe.wait_ge(n_gelu, FB * (g + 1))
                        if not (isinstance(g, int) and g < 2):
                            pe.wait_ge(n_taken, g - 1)
                        pe.matmul(y[:, :], onesb[0:BR, :], ball[:, D:2 * D].unsqueeze(1).broadcast_to([BR, J, D]),
                                  start=True, stop=False, skip_group_check=True)
                    for j in tiles:
                        for k in range(FB):
                            last = pe.matmul(y[:, j * D:(j + 1) * D], hf[i][:, k, j * P:(j + 1) * P], fw2[:, k, :],
                                             start=False, stop=(j == J - 1 and k == FB - 1), skip_group_check=True)
                    if J - 1 in tiles:
                        last.then_inc(n_out, 1)

                def f_unit(g, i, between=()):
                    parts = (lambda: f_hidden(g + 1, (0, 1)), lambda: f_hidden(g + 1, (2, 3)),
                             lambda: f_out(g, i, (0, 1)), lambda: f_out(g, i, (2, 3)))
                    for n, part in enumerate(parts):
                        part()
                        if n < len(between):
                            between[n]()

                runs(pe, PE_ORDER, dict(
                    a_xt=transposed("a", a0), b_xt=transposed("b", b0), c_xt=transposed("c", c0),
                    d_xt=transposed("d", d0), e_xt=transposed("e", e0),
                    a_g=a_g, a_v=a_v, a_s=a_s, a_o=a_o, b_g=b_g, b_v=b_v, b_s=b_s, b_pt=b_pt, b_o=b_o,
                    c_ct=c_ct, c_v=c_v, c_k=c_k, c_s=c_s, c_pt=c_pt, c_o=c_o, d_f=d_f, e_l=e_l),
                     after_step={("a_xt", 0): (weight_products,),
                                 ("e_l", G - 3): (f_ready, lambda: f_hidden(0)),
                                 ("d_f", G - 1): (lambda: f_hidden(1),),
                                 ("e_l", G - 2): (lambda: f_out(0, 0), lambda: f_unit(1, 1)),
                                 ("e_xt", G - 1): (lambda: f_hidden(3, (0,)),),
                                 ("e_l", G - 1): (lambda: f_hidden(3, (1, 2, 3)), lambda: f_out(2, 0))})

                pe.wait_ge(S["e_l_sb"], G)
                pe.wait_ge(s_zT, 16 * G)

                def route(e):
                    pe.wait_ge(r_elig, e + 1)
                    pe.matmul(bank[6][:, 0:NT], trib[:, :], eligb[:, 1:NT + 1], start=True, stop=True)
                    pe.matmul(bank[6][:, NT:2 * NT], onesb[:, :], eligb[:, 0:NT], start=True, stop=True)\
                      .then_inc(r_cnt, 1)

                def table(q, i):
                    if i < CR - 1:
                        pe.wait_ge(t_chunk, (CR - 1) * q + i + 1)
                    else:
                        pe.wait_ge(t_whole, q + 1)
                    for t in range(CT):
                        last = pe.matmul(bank[7][:, 0:NV * NC], ohp[i][:, t, :],
                                         ohv[i][:, t, :, :].rearrange("p v c -> p (v c)"), start=False, stop=False,
                                         skip_group_check=True)
                    last.then_inc(t_used, 1)

                def table_edge(start):
                    return pe.matmul(bank[7][:, 0:NV * NC], zb[:, :], ohv_zero, start=start, stop=not start,
                                     skip_group_check=True)

                ohv_zero = zb[:, 0:NV * NC]

                def x_hidden(e, i, pair):
                    pe.wait_ge(x_tsb, e + 1)
                    pe.wait_ge(x_w1[i], 16 * (pair + 1))
                    for k in range(FB):
                        pe.wait_ge(n_gelu, FB * (G + e - 1) + k + 1)
                        pe.matmul(bank[k][:, 0:CAP], ew1[i][:, k * P:(k + 1) * P],
                                  xgT[:, e, :],
                                  start=True, stop=True).then_inc(n_hid, 1)

                def x_out(e, i, pair):
                    y = bank[4 + i]
                    pe.wait_ge(n_gelu, FB * (G + e + 1))
                    pe.wait_ge(x_w2[i], 16 * (pair + 1))
                    pe.wait_ge(n_taken, G + e - 1)
                    pe.matmul(y[:, 0:NQ * D], onesb[0:BR, :],
                              ball[:, bass.ds((2 + e) * D, D)].unsqueeze(1).broadcast_to([BR, NQ, D]),
                              start=True, stop=False, skip_group_check=True)
                    for n, w in enumerate(SQ):
                        for k in range(FB):
                            last = pe.matmul(y[0:w, n * D:(n + 1) * D], hf[i][:, k, n * P:n * P + w], ew2[i][:, k, :],
                                             start=False, stop=(n == NQ - 1 and k == FB - 1), skip_group_check=True)
                    last.then_inc(n_out, 1)

                def x_transpose(e, i, pair):
                    pe.wait_ge(x_g[i], 16 * NQ * (pair + 1))
                    if not (isinstance(e, int) and e < 2):
                        pe.wait_ge(x_tsb, e - 1)
                    for n, w in enumerate(SQ):
                        last = pe.transpose(bank[6 + i][:, n * P:n * P + w], xg[i][0:w, n, :], ident[0:w, 0:w])
                    last.then_inc(x_t, 1)

                with pe.Fori(0, 2) as q:
                    for i in range(2):
                        e = 4 * q + 2 * i
                        f_unit(3 + 2 * q + i, 1 - i, (lambda: None, lambda: route(e), lambda: None, lambda: route(e + 1)))
                f_unit(7, 1)
                table_edge(True)
                with pe.Fori(0, 2) as q:
                    for i in range(2):
                        f_unit(8 + 2 * q + i, i, [lambda n=n: table(2 * q + i, n) for n in range(CR)])
                table_edge(False).then_inc(t_table, 1)
                f_unit(12, 0)
                f_unit(13, 1, (lambda: x_transpose(0, 0, 0), lambda: None, lambda: x_transpose(1, 1, 0)))
                f_unit(14, 0, (lambda: x_transpose(2, 0, 1), lambda: None, lambda: x_transpose(3, 1, 1)))
                x_transpose(4, 0, 2)
                x_hidden(0, 0, 0)
                x_transpose(5, 1, 2)
                f_out(G - 1, 1)
                for e in range(2):
                    x_hidden(e + 1, (e + 1) % 2, (e + 1) // 2)
                    x_transpose(e + 6, e % 2, 3)
                    x_out(e, e % 2, 0)
                with pe.Fori(1, NE // 2 - 1) as q:
                    x_hidden(2 * q + 1, 1, q)
                    x_out(2 * q, 0, q)
                    x_hidden(2 * q + 2, 0, q + 1)
                    x_out(2 * q + 1, 1, q)
                x_hidden(NE - 1, 1, NE // 2 - 1)
                x_out(NE - 2, 0, NE // 2 - 1)
                x_out(NE - 1, 1, NE // 2 - 1)

            @block.scalar
            def _(act):
                def weight_transposes_sb():
                    act.wait_ge(s_prep_pe, 1)
                    for i in range(6):
                        last = act.activation(wtT[:, i, :], bank[4 + i // 4][:, (i % 4) * D:(i % 4 + 1) * D], ACT.Copy)
                    last.then_inc(s_prep_act, 2)

                def weight_products_sb():
                    act.wait_ge(s_prep_pe, 2)
                    act.activation(mqk[:, :, :].rearrange("p k d -> p (k d)"), bank[6][:, 0:3 * D], ACT.Copy)\
                       .then_inc(s_prep_act, 1)

                def copied(dst, src, done, name, scale=1.0, free=None):
                    def step(g):
                        act.wait_ge(S[done], g + 1)
                        if free is not None and later(g):
                            act.wait_ge(S[free], g)
                        act.activation(dst, src, ACT.Copy, scale=scale).then_inc(S[name], 1)
                    return step

                def affine(k, src):
                    def step(g):
                        act.wait_ge(S[f"{k}_xt"], g + 1)
                        act.wait_ge(s_const, NCONST)
                        act.activation(tr[k][:, :], src[:, :], ACT.Identity, scale=gamT[:, :], bias=betT[:, :])\
                           .then_inc(S[f"{k}_ht_sb"], 1)
                    return step

                def exponent(k, src, width):
                    def step(g):
                        act.wait_ge(S[f"{k}_max"], g + 1)
                        if later(g):
                            act.wait_ge(S[f"{k}_pt"], g)
                            act.wait_ge(S[f"{k}_rinv"], g)
                        for j in range(J):
                            c = slice(j * width, (j + 1) * width)
                            last = act.activation(pa[k][:, c], src[:, c], ACT.Exp, bias=nmax[k][:, j:j + 1],
                                                  accum_out=rsum[k][:, j:j + 1])
                        last.then_inc(S[f"{k}_exp"], 1)
                    return step

                def norm(k, n, tiles=range(J), name=None):
                    u = "u" if n else k
                    def step(g):
                        act.wait_ge(S[f"{k}_shift{n}"], g + 1)
                        norm_free(act, k, n, g)
                        src = ln_source(k, n, g)
                        for j in tiles:
                            c = slice(j * D, (j + 1) * D)
                            last = act.activation(nrm[u][:, c], src[:, c], ACT.Identity, scale=rs[u][:, j:j + 1],
                                                  bias=shift[u][:, j:j + 1])
                        last.then_inc(S[name or f"{k}_norm{n}"], 1)
                    return step

                def e_xt_sb(g):
                    act.wait_ge(S["e_xt"], g + 1)
                    if later(g):
                        act.wait_ge(S["e_l"], g)
                        act.wait_ge(s_zT, 16 * g)
                    act.activation(tr["e"][:, :], e0[:, :], ACT.Copy).then_inc(S["e_xt_sb"], 1)

                def exponents(b):
                    t = slice(J * BATCHES[b][0], J * BATCHES[b][1])
                    act.wait_ge(r_sub, b + 1)
                    act.activation(prob[:, t, :], ex[:, t, :], ACT.Exp).then_inc(r_exp, 1)

                def gelu(u, i, bias, width):
                    for k in range(FB):
                        act.wait_ge(n_hid, FB * u + k + 1)
                        if k == 0 and not (isinstance(u, int) and u < 2):
                            act.wait_ge(n_out, u - 1)
                        act.activation(hf[i][:, k, 0:width], bank[k][:, 0:width], ACT.Gelu, bias=bias(k))\
                           .then_inc(n_gelu, 1)

                def f_act(g, i):
                    gelu(g, i, lambda k: fb1[:, k:k + 1], W)

                def x_act(e, i):
                    gelu(G + e, i, lambda k: eb1[:, e, k:k + 1], CAP)

                def f_out_sb(g, i):
                    act.wait_ge(n_out, g + 1)
                    act.activation(mid[:, g, :], bank[4 + i][:, :], ACT.Copy).then_inc(n_taken, 1)

                runs(act, ACT_ORDER, dict(
                    **{f"{k}_norm{n}": norm(k, n) for k, n in (*((k, "") for k in "abcde"), ("d", "2"))},
                    c_norm_act=norm("c", "", range(J // 2, J), "c_norm_act"),
                    a_xt_sb=copied(tr["a"][:, :], a0[:, :], "a_xt", "a_xt_sb"),
                    a_g_sb=copied(gq["a"][:, :], a1[:, :], "a_g", "a_g_sb"),
                    a_v_sb=copied(va["a"][:, :], a0[:, :], "a_v", "a_v_sb"),
                    b_xt_sb=copied(tr["b"][:, :], b0[:, :], "b_xt", "b_xt_sb"),
                    b_g_sb=copied(gq["b"][:, :], b1[:, :], "b_g", "b_g_sb", scale=SCALE),
                    b_v_sb=copied(va["b"][:, :], b0[:, :], "b_v", "b_v_sb", free="b_o"),
                    b_exp=exponent("b", b1, D),
                    b_pt_sb=copied(pT["b"][:, :], b0[:, :], "b_pt", "b_pt_sb"),
                    c_ht_sb=affine("c", c0),
                    c_k_sb=copied(gq["c"][:, 0:J * SC], c1[:, 0:J * SC], "c_k", "c_k_sb", scale=SCALE, free="c_s"),
                    c_ct_sb=copied(cT[:, :], c1[:, 0:J * SC], "c_ct", "c_ct_sb", free="c_v"),
                    c_v_sb=copied(va["c"][0:SC, :], c1[0:SC, :], "c_v", "c_v_sb", free="c_o"),
                    c_exp=exponent("c", c0, SC),
                    c_pt_sb=copied(pT["c"][0:SC, :], c1[0:SC, :], "c_pt", "c_pt_sb"),
                    d_ht_sb=affine("d", d0),
                    e_xt_sb=e_xt_sb),
                     after_step={("a_norm", 0): (weight_transposes_sb,),
                                 ("a_xt_sb", 0): (weight_products_sb,),
                                 ("c_exp", G - 1): (lambda: exponents(0),),
                                 ("d_norm2", G - 2): (lambda: act.wait_ge(s_fw, (3 + NE) * 16), lambda: f_act(0, 0)),
                                 ("d_norm2", G - 1): (lambda: f_act(1, 1), lambda: f_out_sb(0, 0), lambda: f_act(2, 0)),
                                 ("e_norm", G - 1): (lambda: f_out_sb(1, 1),),
                                 ("e_xt_sb", G - 1): (lambda: exponents(1), lambda: f_act(3, 1), lambda: f_out_sb(2, 0))})

                with act.Fori(2, G // 2) as q:
                    f_act(2 * q, 0)
                    f_out_sb(2 * q - 1, 1)
                    f_act(2 * q + 1, 1)
                    f_out_sb(2 * q, 0)
                x_act(0, 0)
                f_out_sb(G - 1, 1)
                x_act(1, 1)
                with act.Fori(1, NE // 2) as q:
                    x_act(2 * q, 0)
                    x_act(2 * q + 1, 1)

            @block.gpsimd
            def _(pool):
                pool.memset(brow[:, :], 0.0).then_inc(s_pool0, 1)
                pool.memset(negh[:, :], -0.5)
                pool.memset(zeros[:, :], 0.0).then_inc(s_pool0, 1)
                pool.wait_ge(s_pool0, 2)

                def root(k, n, eps):
                    u = "u" if n else k
                    def step(g):
                        wait_apart(pool, (S[f"{k}_aggr{n}"], g + 1))
                        pool.tensor_scalar(ve[u][:, :], mv[u][:, :, 1], eps, None, ALU.add).then_inc(S[f"{k}_veps{n}"], 1)
                        pool.wait_ge(S[f"{k}_veps{n}"], g + 1)
                        if later(g):
                            normalised(pool, k, n, g)
                        pool.tensor_tensor(rs[u][:, :], ve[u][:, :], negh[:, :], ALU.pow).then_inc(S[f"{k}_rstd{n}"], 1)
                    return step

                def gamma_beta(src, mul, dst, k, n, mid_name, name, free):
                    def step(g):
                        pool.wait_ge(s_const, NCONST)
                        normalised(pool, k, n, g + 1)
                        pool.tensor_tensor(r(mul), r(src), gam[:, :].unsqueeze(1).broadcast_to([P, J, D]), ALU.mult)\
                            .then_inc(S[mid_name], 1)
                        pool.wait_ge(S[mid_name], g + 1)
                        if later(g):
                            pool.wait_ge(S[free], g)
                        pool.tensor_tensor(r(dst), r(mul), bet[:, :].unsqueeze(1).broadcast_to([P, J, D]), ALU.add)\
                            .then_inc(S[name], 1)
                    return step

                runs(pool, POOL_ORDER, dict(
                    a_rstd=root("a", "", EPS1), b_rstd=root("b", "", EPS1), c_rstd=root("c", "", EPS2),
                    d_rstd=root("d", "", EPS2), d_rstd2=root("d", "2", EPS2), e_rstd=root("e", "", EPS1),
                    c_h=gamma_beta(nrm["c"], hmul["c"], hres["c"], "c", "", "c_hmul", "c_h", "c_c"),
                    d_h=gamma_beta(nrm["d"], hmul["d"], hres["d"], "d", "", "d_hmul", "d_h", "d_u"),
                    d_t=gamma_beta(nrm["u"], hmul["u"], td, "d", "2", "d_tmul", "d_t", "d_x2")))

                def chunk_values(n, i):
                    pool.wait_ge(t_onehot, n + 1)
                    pool.tensor_tensor(ohv[i][:, :, :, :], ohc[i][:, :, :].unsqueeze(2).broadcast_to([P, CT, NV, NC]),
                                       vals[:, bass.ds(n * CT, CT), :].unsqueeze(3).broadcast_to([P, CT, NV, NC]), ALU.mult)\
                        .then_inc(t_chunk, 1)

                with pool.Fori(0, NCH // CR) as q:
                    for i in range(CR - 1):
                        chunk_values(CR * q + i, i)

                pool.wait_ge(t_index, 1)
                pool.wait_ge(s_zrow, 16 * G)

                def gather(e, i):
                    if not (isinstance(e, int) and e < 2):
                        pool.wait_ge(x_t, e - 1)
                    pool.tensor_copy(gi[i][:, :], gidx[:, bass.ds(NQ * e, NQ)]).then_inc(x_gi, 1)
                    wait_apart(pool, (x_gi, e + 1))
                    for n, w in enumerate(SQ):
                        pool.indirect_dma_start(xg[i][0:w, n, :], None, z_rows,
                                                bass.IndirectOffsetOnAxis(ap=gi[i][0:w, n:n + 1], axis=0))\
                            .then_inc(x_g[i], 16)

                def add(e, i):
                    if not (isinstance(e, int) and e == 0):
                        pool.wait_ge(x_add, 16 * NQ * e)
                    pool.tensor_copy(si[i][:, :], sidx[:, bass.ds(NQ * e, NQ)]).then_inc(x_si, 1)
                    wait_apart(pool, (x_si, e + 1))
                    wait_apart(pool, (n_taken, G + e + 1))
                    for n, w in enumerate(SQ):
                        pool.indirect_dma_start(out, bass.IndirectOffsetOnAxis(ap=si[i][0:w, n:n + 1], axis=0),
                                                ye[i][0:w, n, :], None, compute_op=ALU.add).then_inc(x_add, 16)

                gather(0, 0)
                gather(1, 1)
                with pool.Fori(1, NE // 2) as q:
                    gather(2 * q, 0)
                    gather(2 * q + 1, 1)
                pool.wait_ge(o_st, 16 * G)
                pool.wait_ge(s_fill, 16)
                add(0, 0)
                add(1, 1)
                with pool.Fori(1, NE // 2) as q:
                    add(2 * q, 0)
                    add(2 * q + 1, 1)
                pool.wait_ge(x_add, 16 * NQ * NE)

            @block.vector
            def _(dve):
                def bf16_constants():
                    dve.wait_ge(s_const, NCONST)
                    dve.tensor_copy(maskb[:, :, :], maskf[:, :].unsqueeze(1).broadcast_to([P, J, P]))
                    dve.tensor_copy(trib[:, :], trif[:, :])
                    dve.wait_ge(s_wqk, 16 * (1 + len(QK)))
                    dve.tensor_copy(identb[:, :], ident[:, :])
                    dve.memset(onesb[:, :], 1.0).then_inc(s_prep_dve, 1)

                def bias_parts(c, loaded, count, made, n):
                    if n == 0:
                        dve.wait_ge(loaded, count)
                        dve.memset(ball[:, c], 0.0)
                        dve.tensor_copy(bhi[:, c], brow[:, c]).then_inc(made, 1)
                    elif n == 1:
                        dve.wait_ge(made, 1)
                        dve.tensor_tensor(bres[:, c], brow[:, c], bhi[:, c], ALU.subtract).then_inc(made, 1)
                    elif n == 2:
                        dve.wait_ge(made, 2)
                        dve.tensor_copy(bmid[:, c], bres[:, c]).then_inc(made, 1)
                    elif n == 3:
                        dve.wait_ge(made, 3)
                        dve.tensor_tensor(blo[:, c], bres[:, c], bmid[:, c], ALU.subtract).then_inc(made, 1)
                    else:
                        dve.wait_ge(made, 4)
                        dve.tensor_copy(ball[0:1, c], bhi[0:1, c])
                        dve.tensor_copy(ball[32:33, c], bmid[32:33, c])
                        dve.tensor_copy(ball[64:65, c], blo[64:65, c]).then_inc(made, 1)

                def first_bias(n):
                    bias_parts(slice(0, D), s_brow, 3 * 16, s_bias1, n)

                def later_bias(n):
                    bias_parts(slice(D, BW), s_brest, 6 * 16, s_bias2, n)

                def stats(k, n, wait):
                    u = "u" if n else k
                    def step(g):
                        if k == "a" and isinstance(g, int):
                            if g == 0:
                                dve.wait_ge(s_x0, 16)
                            if g == 1:
                                dve.wait_ge(s_x1, 16)
                            if g == 2:
                                dve.wait_ge(s_x23, 2 * 16)
                            if g == 4:
                                dve.wait_ge(s_x2, 16)
                        if wait:
                            wait_apart(dve, (S[wait], g + 1))
                        src = ln_source(k, n, g)
                        for j in range(J):
                            last = dve.bn_stats(st[u][:, j, :], src[:, j * D:(j + 1) * D])
                        last.then_inc(S[f"{k}_stats{n}"], 1)
                    return step

                def aggr(k, n):
                    u = "u" if n else k
                    def step(g):
                        wait_apart(dve, (S[f"{k}_stats{n}"], g + 1),
                                   *([(S[f"{k}_norm{n}"], g)] if later(g) else []),
                                   *([(S["c_norm_act"], g)] if later(g) and k == "c" else []))
                        for j in range(J):
                            last = dve.bn_aggr(mv[u][:, j, :], st[u][:, j, :])
                        last.then_inc(S[f"{k}_aggr{n}"], 1)
                    return step

                def shifted(k, n):
                    u = "u" if n else k
                    def step(g):
                        dve.wait_ge(S[f"{k}_rstd{n}"], g + 1)
                        dve.scalar_tensor_tensor(shift[u][:, :], mv[u][:, :, 0], -1.0, rs[u][:, :], ALU.mult, ALU.mult)\
                           .then_inc(S[f"{k}_shift{n}"], 1)
                    return step

                def norm(k, n, tiles=range(J)):
                    u = "u" if n else k
                    def step(g):
                        dve.wait_ge(S[f"{k}_rstd{n}"], g + 1)
                        norm_free(dve, k, n, g)
                        src = ln_source(k, n, g)
                        for j in tiles:
                            c = slice(j * D, (j + 1) * D)
                            last = dve.tensor_scalar(nrm[u][:, c], src[:, c], mv[u][:, j, 0:1], rs[u][:, j:j + 1],
                                                     ALU.subtract, ALU.mult)
                        last.then_inc(S[f"{k}_norm{n}"], 1)
                    return step

                def a_p(g):
                    dve.wait_ge(s_decay, 16)
                    dve.wait_ge(S["a_s"], g + 1)
                    if later(g):
                        dve.wait_ge(S["a_o"], g)
                    dve.tensor_tensor(r(pa["a"]), r(a1), decay[:, :].unsqueeze(1).broadcast_to([P, J, D]), ALU.mult)\
                       .then_inc(S["a_p"], 1)

                def a_x1(g):
                    dve.wait_ge(S["a_o"], g + 1)
                    dve.tensor_tensor(xs[:, g, :], a0[:, :], xs[:, g, :], ALU.add).then_inc(S["a_x1"], 1)

                def row_max(k, src, width):
                    def step(g):
                        dve.wait_ge(S[f"{k}_s"], g + 1)
                        if later(g):
                            dve.wait_ge(S[f"{k}_exp"], g)
                        dve.tensor_reduce(nmax[k][:, :], src[:, 0:J * width].rearrange("p (j s) -> p j s", j=J),
                                          AX.X, ALU.max, negate=True).then_inc(S[f"{k}_max"], 1)
                    return step

                def row_inv(k):
                    def step(g):
                        dve.wait_ge(S[f"{k}_exp"], g + 1)
                        if later(g):
                            dve.wait_ge(S[{"b": "b_a", "c": "c_c"}[k]], g)
                        dve.reciprocal(rinv[k][:, :], rsum[k][:, :]).then_inc(S[f"{k}_rinv"], 1)
                    return step

                def attended(k, src, res, name):
                    def step(g):
                        dve.wait_ge(S[f"{k}_o"], g + 1)
                        dve.wait_ge(S[f"{k}_rinv"], g + 1)
                        if k == "c":
                            dve.wait_ge(S["c_h"], g + 1)
                        for j in range(J):
                            c = slice(j * D, (j + 1) * D)
                            last = dve.scalar_tensor_tensor(mid[:, g, :][:, c], src[:, c], rinv[k][:, j:j + 1], res[:, c],
                                                            ALU.mult, ALU.add)
                        last.then_inc(S[name], 1)
                    return step

                def d_u(g):
                    dve.wait_ge(S["d_f"], g + 1)
                    dve.wait_ge(S["d_h"], g + 1)
                    if later(g):
                        dve.wait_ge(S["d_norm2"], g)
                    dve.scalar_tensor_tensor(ud[:, :], d0[:, :], 0.0, hres["d"][:, :], ALU.max, ALU.add)\
                       .then_inc(S["d_u"], 1)

                def d_x2(g):
                    dve.wait_ge(S["d_t"], g + 1)
                    dve.scalar_tensor_tensor(xs[:, g, :], td[:, :], 0.0, xs[:, g, :], ALU.max, ALU.add)\
                       .then_inc(S["d_x2"], 1)

                def e_l_sb(g):
                    dve.wait_ge(S["e_l"], g + 1)
                    dve.tensor_copy(logits[:, :, :].rearrange("p (g j) e -> p g (j e)", j=J)[:, g, :], e0[:, 0:J * NE])\
                       .then_inc(S["e_l_sb"], 1)

                linked = [0]

                def link(ins):
                    linked[0] += 1
                    ins.then_inc(r_chain, 1)
                    dve.wait_ge(r_chain, linked[0])

                def route_constants():
                    dve.wait_ge(s_late, 6 * 16)
                    dve.memset(eligb[:, :], 0.0)
                    dve.memset(rt["free"][:, :], 1.0)
                    dve.memset(ones[:, :], 1.0)
                    dve.memset(zb[:, :], 0.0)

                def batch(first, last):
                    t, n = slice(J * first, J * last), J * (last - first)
                    return (t, lambda a: a[:, t].unsqueeze(2).broadcast_to([P, n, NE]),
                            revio[:, :].unsqueeze(1).broadcast_to([P, n, NE]))

                def shifted_logits(b):
                    t, over_e, _ = batch(*BATCHES[b])
                    dve.wait_ge(S["e_l_sb"], BATCHES[b][1])
                    link(dve.tensor_reduce(rt["max"][:, t], logits[:, t, :], AX.X, ALU.max))
                    dve.tensor_tensor(ex[:, t, :], logits[:, t, :], over_e(rt["max"]), ALU.subtract).then_inc(r_sub, 1)

                def choose(b, first, last):
                    t, over_e, rev = batch(first, last)
                    dve.wait_ge(r_exp, b + 1)
                    link(dve.tensor_reduce(rt["sum"][:, t], prob[:, t, :], AX.X, ALU.add))
                    link(dve.reciprocal(rt["inv"][:, t], rt["sum"][:, t]))
                    link(dve.tensor_tensor(prob[:, t, :], prob[:, t, :], over_e(rt["inv"]), ALU.mult))
                    for c, (m, at) in enumerate((("m1", "i1"), ("m2", "i2"))):
                        link(dve.tensor_reduce(rt[m][:, t], prob[:, t, :], AX.X, ALU.max))
                        link(dve.tensor_tensor(cand[:, t, :], prob[:, t, :], over_e(rt[m]), ALU.is_equal))
                        link(dve.tensor_tensor(cand[:, t, :], cand[:, t, :], rev, ALU.mult))
                        link(dve.tensor_reduce(rt[at][:, t], cand[:, t, :], AX.X, ALU.max))
                        link(dve.tensor_tensor(oh[c][:, t, :], rev, over_e(rt[at]), ALU.is_equal))
                        if c == 0:
                            link(dve.scalar_tensor_tensor(prob[:, t, :], oh[0][:, t, :], -2.0, prob[:, t, :],
                                                          ALU.mult, ALU.add))
                    link(dve.tensor_tensor(asg[:, :, t].rearrange("p e t -> p t e"), oh[0][:, t, :], oh[1][:, t, :], ALU.add))

                runs(dve, DVE_ORDER, dict(
                    a_stats=stats("a", "", None), a_aggr=aggr("a", ""), a_norm=norm("a", ""),
                    b_stats=stats("b", "", "a_x1"), b_aggr=aggr("b", ""), b_norm=norm("b", ""),
                    c_stats=stats("c", "", "b_a"), c_aggr=aggr("c", ""), c_norm=norm("c", "", range(J // 2)),
                    d_stats=stats("d", "", "c_c"), d_aggr=aggr("d", ""), d_norm=norm("d", ""),
                    d_stats2=stats("d", "2", "d_u"), d_aggr2=aggr("d", "2"), d_norm2=norm("d", "2"),
                    e_stats=stats("e", "", "d_x2"), e_aggr=aggr("e", ""), e_norm=norm("e", ""),
                    **{f"{k}_shift{n}": shifted(k, n) for k, n in (*((k, "") for k in "abcde"), ("d", "2"))},
                    a_p=a_p, a_x1=a_x1, b_max=row_max("b", b1, D), b_rinv=row_inv("b"),
                    b_a=attended("b", b1, nrm["b"], "b_a"), c_max=row_max("c", c0, SC), c_rinv=row_inv("c"),
                    c_c=attended("c", c0, hres["c"], "c_c"), d_u=d_u, d_x2=d_x2, e_l_sb=e_l_sb),
                     after_turn={0: [lambda n=n: first_bias(n) for n in range(NPARTS)],
                                 1: [lambda n=n: later_bias(n) for n in (0, 1)],
                                 2: [lambda n=n: later_bias(n) for n in (2, 3)],
                                 3: [lambda: later_bias(4)]},
                     after_step={("a_p", 0): (bf16_constants,),
                                 ("c_max", G - 1): (lambda: shifted_logits(0),),
                                 ("d_norm", G - 1): (route_constants, lambda: choose(0, 0, 2)),
                                 ("d_shift2", G - 1): (lambda: choose(0, 2, 7),),
                                 ("e_shift", G - 1): (lambda: choose(0, 7, 13),)})
                shifted_logits(1)
                choose(1, 13, G)

                def slot_values():
                    link(dve.tensor_tensor(rt["sum"][:, :], rt["m1"][:, :], rt["m2"][:, :], ALU.add))
                    link(dve.tensor_scalar(rt["sum"][:, :], rt["sum"][:, :], 1e-9, None, ALU.max))
                    link(dve.reciprocal(rt["inv"][:, :], rt["sum"][:, :]))
                    dve.tensor_tensor(wch[:, 0, :], rt["m1"][:, :], rt["inv"][:, :], ALU.mult)
                    link(dve.tensor_tensor(wch[:, 1, :], rt["m2"][:, :], rt["inv"][:, :], ALU.mult))
                    for c in range(2):
                        dve.tensor_copy(vals[:, c * NT:(c + 1) * NT, 0], iot[:, :])
                        dve.tensor_scalar(colc[:, c * NT:(c + 1) * NT], rt[("i1", "i2")[c]][:, :], -float(NQ),
                                          float(NQ * NE), ALU.mult, ALU.add)
                    dve.tensor_copy(vals[:, :, 1], plus1[:, 0:1].broadcast_to([P, 2 * NT]))
                    wv = wch[:, :, :].rearrange("p c t -> p (c t)")
                    wr_ = wres[:, :, :].rearrange("p c t -> p (c t)")
                    link(dve.tensor_copy(vals[:, :, 2], wv))
                    link(dve.tensor_tensor(wr_, wv, vals[:, :, 2], ALU.subtract))
                    link(dve.tensor_copy(vals[:, :, 3], wr_))
                    link(dve.tensor_tensor(wv, wr_, vals[:, :, 3], ALU.subtract))
                    link(dve.tensor_copy(vals[:, :, 4], wv))

                def route(e):
                    def step_link(ins, n):
                        ins.then_inc(r_step, 1)
                        dve.wait_ge(r_step, 5 * e + n)
                    step_link(dve.tensor_tensor(elig[:, :], asg[:, e, :], rt["free"][:, :], ALU.mult), 1)
                    dve.tensor_copy(eligb[:, 1:NT + 1], elig[:, :]).then_inc(r_elig, 1)
                    if not later(e):
                        slot_values()
                    dve.wait_ge(r_cnt, e + 1)
                    step_link(dve.tensor_tensor_scan(rt["cum"][:, :], ones[:, :], bank[6][:, NT:2 * NT], 0.0,
                                                     ALU.mult, ALU.add), 2)
                    step_link(dve.tensor_tensor(rank[:, e, :], bank[6][:, 0:NT], rt["cum"][:, :], ALU.add), 3)
                    step_link(dve.scalar_tensor_tensor(rt["drop"][:, :], rank[:, e, :], float(CAP), elig[:, :],
                                                       ALU.is_gt, ALU.mult), 4)
                    step_link(dve.tensor_tensor(rt["free"][:, :], rt["free"][:, :], rt["drop"][:, :], ALU.subtract), 5)

                route(0)
                with dve.Fori(1, NE) as e:
                    route(e)

                for c in range(2):
                    link(dve.tensor_tensor(cand[:, :, :], oh[c][:, :, :], rank[:, :, :].rearrange("p e t -> p t e"), ALU.mult))
                    link(dve.tensor_reduce(slotc[:, c * NT:(c + 1) * NT], cand[:, :, :], AX.X, ALU.add))
                link(dve.tensor_tensor(slotc[:, :].rearrange("p (c t) -> p c t", c=2), slotc[:, :].rearrange("p (c t) -> p c t", c=2),
                                       rt["free"][:, :].unsqueeze(1).broadcast_to([P, 2, NT]), ALU.mult))
                link(dve.tensor_scalar(piece[:, :], slotc[:, :], float(P), None, ALU.is_gt))
                link(dve.scalar_tensor_tensor(piece[:, :], slotc[:, :], 2.0 * P, piece[:, :], ALU.is_gt, ALU.add))
                link(dve.scalar_tensor_tensor(slotc[:, :], piece[:, :], -float(P), slotc[:, :], ALU.mult, ALU.add))
                link(dve.tensor_tensor(colc[:, :], piece[:, :], colc[:, :], ALU.add))
                link(dve.tensor_scalar(rt["drop"][:, :], rt["free"][:, :], -1.0, 1.0, ALU.mult, ALU.add))

                dropv = rt["drop"][:, :].rearrange("p (g j) -> p g j", j=J)

                def base(g):
                    dve.wait_ge(n_taken, g + 1)
                    for j in range(J):
                        c = slice(j * D, (j + 1) * D)
                        last = dve.scalar_tensor_tensor(xs[:, g, :][:, c], mid[:, g, :][:, c], dropv[:, g, :][:, j:j + 1],
                                                        xs[:, g, :][:, c], ALU.mult, ALU.add)
                    last.then_inc(o_base, 1)

                def chunk(n, i, q):
                    cs = bass.ds(n * CT, CT)
                    if later(q):
                        dve.wait_ge(t_used, n - CR + 1)
                    dve.tensor_tensor(ohp[i][:, :, :], slotc[:, cs].unsqueeze(2).broadcast_to([P, CT, P]),
                                      iop[:, :].unsqueeze(1).broadcast_to([P, CT, P]), ALU.is_equal)
                    dve.tensor_tensor(ohc[i][:, :, :], colc[:, cs].unsqueeze(2).broadcast_to([P, CT, NC]),
                                      ioc[:, :].unsqueeze(1).broadcast_to([P, CT, NC]), ALU.is_equal)\
                       .then_inc(t_onehot, 1)

                def round_of_chunks(q):
                    for i in range(CR):
                        chunk(CR * q + i, i, q)
                    i, n = CR - 1, CR * q + CR - 1
                    dve.wait_ge(t_onehot, n + 1)
                    dve.tensor_tensor(ohv[i][:, :, :, :], ohc[i][:, :, :].unsqueeze(2).broadcast_to([P, CT, NV, NC]),
                                      vals[:, bass.ds(n * CT, CT), :].unsqueeze(3).broadcast_to([P, CT, NV, NC]), ALU.mult)\
                       .then_inc(t_whole, 1)
                    base(q)

                round_of_chunks(0)
                with dve.Fori(1, NCH // CR) as q:
                    round_of_chunks(q)
                for g in range(NCH // CR, 8):
                    base(g)

                dve.wait_ge(t_table, 1)
                link(dve.tensor_copy(tab[:, :, :].rearrange("p v c -> p (v c)"), bank[7][:, 0:NV * NC]))
                link(dve.scalar_tensor_tensor(tidx[:, :], tab[:, 0, :], float(P), tab[:, 1, :], ALU.mult, ALU.add))
                link(dve.tensor_scalar(tidx[:, :], tidx[:, :], -1.0, None, ALU.add))
                dve.tensor_scalar(gidx[:, :], tidx[:, :], 0.0, None, ALU.max)
                link(dve.tensor_scalar(temp[:, :], tab[:, 1, :], 0.0, None, ALU.is_equal))
                link(dve.tensor_tensor(temp[:, :], temp[:, :], spare[:, :], ALU.mult))
                link(dve.tensor_tensor(tw[:, :], tab[:, 3, :], tab[:, 4, :], ALU.add))
                link(dve.tensor_tensor(tw[:, :], tw[:, :], tab[:, 2, :], ALU.add))
                dve.tensor_tensor(sidx[:, :], tidx[:, :], temp[:, :], ALU.add).then_inc(t_index, 1)
                def gathered_sb(e, i):
                    dve.wait_ge(x_t, e + 1)
                    dve.tensor_copy(xgT[:, e, :],
                                    bank[6 + i][:, 0:CAP]).then_inc(x_tsb, 1)

                def weighted(e, i):
                    dve.wait_ge(n_out, G + e + 1)
                    if not (isinstance(e, int) and e < 2):
                        dve.wait_ge(x_add, 16 * NQ * (e - 1))
                    dve.tensor_tensor(ye[i][:, :, :], bank[4 + i][:, 0:NQ * D].rearrange("p (n d) -> p n d", n=NQ),
                                      tw[:, bass.ds(NQ * e, NQ)].unsqueeze(2).broadcast_to([P, NQ, D]), ALU.mult)\
                       .then_inc(n_taken, 1)

                for g in range(8, 12):
                    base(g)
                gathered_sb(0, 0)
                base(12)
                gathered_sb(1, 1)
                gathered_sb(2, 0)
                base(13)
                gathered_sb(3, 1)
                gathered_sb(4, 0)
                base(14)
                gathered_sb(5, 1)
                base(15)
                gathered_sb(6, 0)
                weighted(0, 0)
                gathered_sb(7, 1)
                weighted(1, 1)
                with dve.Fori(1, NE // 2) as q:
                    weighted(2 * q, 0)
                    weighted(2 * q + 1, 1)
    return nc
    return nc
    return nc


_INS = ["x", "ctx_1024", "L0_attn_W_Q", "L0_attn_W_K", "L0_attn_W_V", "L0_xattn_Wq", "L0_xattn_Wk", "L0_xattn_Wv",
        "L0_xattn_Wcq", "L0_xattn_Wck", "L0_xattn_Wcv", "L0_xattn_gamma", "L0_xattn_beta", "L0_xattn_W1",
        "L0_xattn_b1", "L0_ffn_Wr", "L0_ffn_W1", "L0_ffn_b1", "L0_ffn_W2", "L0_ffn_b2", "L0_ffn_fw1", "L0_ffn_fb1",
        "L0_ffn_fw2", "L0_ffn_fb2"]


def constants():
    import numpy as np
    n = np.arange(128)
    d = n[None, :] - n[:, None]
    return {
        "c_ident": np.eye(128, dtype=np.float32),
        "c_decay": np.where(d >= 0, np.power(np.float32(0.99), np.maximum(d, 0).astype(np.float32)), 0).astype(np.float32),
        "c_mask": np.where(d > 0, np.float32(-1e30), np.float32(0)).astype(np.float32),
        "c_tri": (d >= 0).astype(np.float32),
        "c_revio": np.tile(8 - np.arange(8, dtype=np.float32), (128, 1)),
        "c_iop": np.tile(np.arange(1, 129, dtype=np.float32), (128, 1)),
        "c_ioc": np.tile(np.arange(24, dtype=np.float32), (128, 1)),
        "c_iot": np.tile(np.arange(64, dtype=np.float32), (128, 1)),
        "c_plus1": np.arange(1, 129, dtype=np.float32)[:, None],
        "c_spare": (8192 + 1 + np.arange(128)[:, None] + 128 * (np.arange(24) % 3)[None, :]).astype(np.float32),
    }


def kernel(**inputs):
    import numpy as _np
    import concourse.bacc as _bacc
    from concourse import mybir as _mybir
    from concourse.bass_utils import run_bass_kernel_spmd as _run

    nc = _bacc.Bacc("TRN2", target_bir_lowering=False, num_devices=1)
    arrays, args = {}, {}
    for name, a in [(n, _np.ascontiguousarray(inputs[n])) for n in _INS] + list(constants().items()):
        arrays[f"in_{name}_dram"] = a
        args[name] = nc.dram_tensor(f"in_{name}_dram", a.shape, _mybir.dt.from_np(a.dtype), kind="ExternalInput").ap()
    out = nc.dram_tensor("out_0_dram", ((64 + 3) * 128, 128), _mybir.dt.float32, kind="ExternalOutput").ap()
    decoder_program(nc, args, out)
    r = _run(nc, [arrays], core_ids=[0])
    return r.results[0]["out_0_dram"][:64 * 128].reshape(64, 128, 128)
```
